# Optimizing a Trainium2 kernel written in Bass

```python
import numpy as np
import jax
import jax.numpy as jnp

def _softmax(x, axis=-1):
    return jax.nn.softmax(x, axis=axis)

def _gelu(x):
    return jax.nn.gelu(x, approximate=True)

def _silu(x):
    return jax.nn.silu(x)

def _sigmoid(x):
    return jax.nn.sigmoid(x)

def _layernorm(x, axis=-1, eps=1e-05):
    m = jnp.mean(x, axis=axis, keepdims=True)
    v = jnp.var(x, axis=axis, keepdims=True)
    return (x - m) / jnp.sqrt(v + eps)

def _scatter_add(tgt, idx, src, axis=0):
    return tgt.at[idx].add(src)

def _segment_sum(src, seg, n):
    return jax.ops.segment_sum(src, seg, n)
kernel_name = 'mk_early_fusion_d1_tok_img768_r4_a693d9'

def setup_inputs(seed: int=0):
    np.random.seed(seed)
    _w = jnp.asarray

    def _rec_inputs():
        import jax
        import jax.numpy as jnp
        _rk = jax.random.key(seed)
        x = -0.000147625 + 0.999875 * jax.random.normal(jax.random.fold_in(_rk, 1), (64, 12, 224, 224), jnp.float32)
        txt = -0.0221329 + 10 * jax.random.normal(jax.random.fold_in(_rk, 2), (64, 32, 192), jnp.float32)
        return (x, txt)
    x, txt = _rec_inputs()

    def _L0_tok_setup():
        import jax, jax.numpy as jnp
        import numpy as np
        IMG = 224
        PATCH = 16
        EMBED = 192
        C = 12
        B = 64
        key = jax.random.key(seed)
        k1, k2 = jax.random.split(key)
        x = jax.random.normal(k1, (B, C, IMG, IMG), dtype=jnp.float32)
        channel_weights = jax.random.normal(k2, (C, EMBED), dtype=jnp.float32)
        return {'x': x, 'channel_weights': channel_weights}
    _L0_tok_all = _L0_tok_setup()
    _L0_tok_in = {k: v for k, v in _L0_tok_all.items() if k in ('channel_weights',)}
    del _L0_tok_all

    def _L0_attn_setup():
        import jax, jax.numpy as jnp
        import numpy as np
        N_HEAD = 12
        N_EMBD = 192
        BLOCK = 512
        THETA = 10000.0

        def _rope_tables(head_dim, end, theta=THETA):
            half = head_dim // 2
            freqs = 1.0 / theta ** (jnp.arange(0, head_dim, 2, dtype=jnp.float32) / head_dim)
            t = jnp.arange(end, dtype=jnp.float32)
            ang = jnp.outer(t, freqs)
            return (jnp.cos(ang), jnp.sin(ang))

        def _apply_rope(x, cos, sin):
            B, H, T, hd = x.shape
            xr = x.reshape(B, H, T, hd // 2, 2)
            x0, x1 = (xr[..., 0], xr[..., 1])
            c = cos[None, None, :T, :]
            s = sin[None, None, :T, :]
            o0 = x0 * c - x1 * s
            o1 = x0 * s + x1 * c
            return jnp.stack([o0, o1], axis=-1).reshape(B, H, T, hd)
        key = jax.random.key(seed)
        ks = jax.random.split(key, 9)
        B, T, C = (2, 512, N_EMBD)
        std = 0.02
        return {'x': jax.random.normal(ks[0], (B, T, C), jnp.float32), 'norm_scale': jnp.ones((C,), jnp.float32), 'norm_bias': jnp.zeros((C,), jnp.float32), 'W_attn': jax.random.normal(ks[1], (C, 3 * C), jnp.float32) * std, 'b_attn': jax.random.normal(ks[2], (3 * C,), jnp.float32) * std, 'W_proj': jax.random.normal(ks[3], (C, C), jnp.float32) * std, 'b_proj': jax.random.normal(ks[4], (C,), jnp.float32) * std, 'sinks': jax.random.normal(ks[5], (N_HEAD,), jnp.float32) * 0.5, 'rezero': jax.random.normal(ks[6], (1,), jnp.float32) * 0.1}
    _L0_attn_all = _L0_attn_setup()
    _L0_attn_in = {k: v for k, v in _L0_attn_all.items() if k in ('norm_scale', 'norm_bias', 'W_attn', 'b_attn', 'W_proj', 'b_proj', 'sinks', 'rezero')}
    del _L0_attn_all

    def _L0_ffn_setup():
        import jax, jax.numpy as jnp
        import numpy as np
        import math
        B, S, D = (4, 1024, 192)
        E = 8
        TOP_K = 2
        H = 512
        CAP_F = 1.25
        EPS = 1e-06
        ALPHA = 1.0
        key = jax.random.key(seed)
        k0, k1, k2, k3 = jax.random.split(key, 4)
        x = jax.random.normal(k0, (B, S, D), jnp.float32)
        gate_w = jax.random.normal(k1, (E, D), jnp.float32) * 0.02
        w13 = jax.random.normal(k2, (E, 2 * H, D), jnp.float32) * 0.02
        w2 = jax.random.normal(k3, (E, D, H), jnp.float32) * 0.02
        norm_w = jnp.ones((E, D), jnp.float32)
        return {'x': x, 'gate_w': gate_w, 'w13': w13, 'w2': w2, 'norm_w': norm_w}
    _L0_ffn_all = _L0_ffn_setup()
    _L0_ffn_in = {k: v for k, v in _L0_ffn_all.items() if k in ('gate_w', 'w13', 'w2', 'norm_w')}
    del _L0_ffn_all
    return {'x': x, 'txt': txt, 'L0_tok_channel_weights': _L0_tok_in['channel_weights'], 'L0_attn_norm_scale': _L0_attn_in['norm_scale'], 'L0_attn_norm_bias': _L0_attn_in['norm_bias'], 'L0_attn_W_attn': _L0_attn_in['W_attn'], 'L0_attn_b_attn': _L0_attn_in['b_attn'], 'L0_attn_W_proj': _L0_attn_in['W_proj'], 'L0_attn_b_proj': _L0_attn_in['b_proj'], 'L0_attn_sinks': _L0_attn_in['sinks'], 'L0_attn_rezero': _L0_attn_in['rezero'], 'L0_ffn_gate_w': _L0_ffn_in['gate_w'], 'L0_ffn_w13': _L0_ffn_in['w13'], 'L0_ffn_w2': _L0_ffn_in['w2'], 'L0_ffn_norm_w': _L0_ffn_in['norm_w']}

def reference(x, txt, L0_tok_channel_weights, L0_attn_norm_scale, L0_attn_norm_bias, L0_attn_W_attn, L0_attn_b_attn, L0_attn_W_proj, L0_attn_b_proj, L0_attn_sinks, L0_attn_rezero, L0_ffn_gate_w, L0_ffn_w13, L0_ffn_w2, L0_ffn_norm_w):
    import jax
    import jax.numpy as jnp

    def _L0_tok_ref(x, channel_weights):
        import jax, jax.numpy as jnp
        import numpy as np
        IMG = 224
        PATCH = 16
        EMBED = 192
        C = 12
        B = 64
        Bb, Cc, H, W = x.shape
        K = PATCH
        n = H // K
        pooled = x.reshape(Bb, Cc, n, K, n, K).sum(axis=(3, 5))
        out = jnp.einsum('bcij,ce->bije', pooled, channel_weights)
        return out.reshape(Bb, n * n, EMBED)

    def _L0_attn_ref(x, norm_scale, norm_bias, W_attn, b_attn, W_proj, b_proj, sinks, rezero):
        import jax, jax.numpy as jnp
        import numpy as np
        N_HEAD = 12
        N_EMBD = 192
        BLOCK = 512
        THETA = 10000.0

        def _rope_tables(head_dim, end, theta=THETA):
            half = head_dim // 2
            freqs = 1.0 / theta ** (jnp.arange(0, head_dim, 2, dtype=jnp.float32) / head_dim)
            t = jnp.arange(end, dtype=jnp.float32)
            ang = jnp.outer(t, freqs)
            return (jnp.cos(ang), jnp.sin(ang))

        def _apply_rope(x, cos, sin):
            B, H, T, hd = x.shape
            xr = x.reshape(B, H, T, hd // 2, 2)
            x0, x1 = (xr[..., 0], xr[..., 1])
            c = cos[None, None, :T, :]
            s = sin[None, None, :T, :]
            o0 = x0 * c - x1 * s
            o1 = x0 * s + x1 * c
            return jnp.stack([o0, o1], axis=-1).reshape(B, H, T, hd)
        B, T, C = x.shape
        H = N_HEAD
        hd = C // H
        xn = norm_scale * x + norm_bias
        qkv = xn @ W_attn + b_attn
        q, k, v = jnp.split(qkv, 3, axis=-1)
        q = q.reshape(B, T, H, hd).transpose(0, 2, 1, 3)
        k = k.reshape(B, T, H, hd).transpose(0, 2, 1, 3)
        v = v.reshape(B, T, H, hd).transpose(0, 2, 1, 3)
        cos, sin = _rope_tables(hd, T)
        q = _apply_rope(q, cos, sin)
        k = _apply_rope(k, cos, sin)
        scale = 1.0 / jnp.sqrt(jnp.float32(hd))
        att = jnp.einsum('bhqd,bhkd->bhqk', q, k) * scale
        causal = jnp.tril(jnp.ones((T, T), dtype=bool))
        att = jnp.where(causal[None, None], att, -jnp.inf)
        sink_col = jnp.broadcast_to(sinks.reshape(1, H, 1, 1), (B, H, T, 1))
        att = jnp.concatenate([sink_col, att], axis=-1)
        att = jax.nn.softmax(att, axis=-1)[..., 1:]
        y = jnp.einsum('bhqk,bhkd->bhqd', att, v)
        y = y.transpose(0, 2, 1, 3).reshape(B, T, C)
        y = (y @ W_proj + b_proj) * rezero
        return y

    def _L0_ffn_ref(x, gate_w, w13, w2, norm_w):
        import jax, jax.numpy as jnp
        import numpy as np
        import math
        B, S, D = (4, 1024, 192)
        E = 8
        TOP_K = 2
        H = 512
        CAP_F = 1.25
        EPS = 1e-06
        ALPHA = 1.0
        Bx, Sx, Dx = x.shape
        N = Bx * Sx
        cap = int(math.ceil(CAP_F * TOP_K * N / E))
        xf = x.reshape(N, Dx)
        logits = xf.astype(jnp.float32) @ gate_w.T
        probs = jax.nn.softmax(logits, axis=-1)
        top_p, top_i = jax.lax.top_k(probs, TOP_K)
        w = top_p / jnp.sum(top_p, axis=-1, keepdims=True)
        flat_e = top_i.reshape(-1)
        onehot = jax.nn.one_hot(flat_e, E, dtype=jnp.int32)
        pos = jnp.take_along_axis(jnp.cumsum(onehot, axis=0) - 1, flat_e[:, None], axis=1)[:, 0]
        keep = pos < cap
        didx = flat_e * cap + jnp.minimum(pos, cap - 1)
        safe = jnp.where(keep, didx, E * cap)
        x_rep = jnp.repeat(xf, TOP_K, axis=0)
        buf = jnp.zeros((E * cap + 1, Dx), x.dtype).at[safe].set(x_rep)
        buf = buf[:-1].reshape(E, cap, Dx)
        z = 2.0 * buf
        z = z * jax.lax.rsqrt(jnp.mean(z * z, axis=-1, keepdims=True) + EPS)
        z = z * norm_w[:, None, :]
        gu = jnp.einsum('ecd,ehd->ech', z, w13)
        g, u = jnp.split(gu, 2, axis=-1)
        y = buf + ALPHA * jnp.einsum('ech,edh->ecd', jax.nn.silu(g) * u, w2)
        y_tok = y.reshape(E * cap, Dx)[didx]
        cw = (w.reshape(-1) * keep.astype(w.dtype)).astype(x.dtype)
        out = (cw[:, None] * y_tok).reshape(N, TOP_K, Dx).sum(axis=1)
        return out.reshape(Bx, Sx, Dx)
    h = _L0_tok_ref(x, L0_tok_channel_weights)
    h = jnp.concatenate([h, txt], axis=1)
    h = h + _L0_attn_ref(_layernorm(h, axis=-1), L0_attn_norm_scale, L0_attn_norm_bias, L0_attn_W_attn, L0_attn_b_attn, L0_attn_W_proj, L0_attn_b_proj, L0_attn_sinks, L0_attn_rezero)
    h = h + _L0_ffn_ref(_layernorm(h, axis=-1), L0_ffn_gate_w, L0_ffn_w13, L0_ffn_w2, L0_ffn_norm_w)
    return h

_drawn_inputs = setup_inputs


def setup_inputs(seed=0):
    import zlib

    import numpy as np

    out = dict(_drawn_inputs(seed))
    spreads = {'L0_attn_norm_scale': (1.0, 0.6),
     'L0_attn_norm_bias': (0.0, 0.8),
     'L0_ffn_norm_w': (1.0, 0.6)}
    factors = {'L0_attn_W_attn': 8.0,
     'L0_attn_b_attn': 8.0,
     'L0_attn_W_proj': 8.0,
     'L0_attn_b_proj': 8.0,
     'L0_attn_sinks': 8.0,
     'L0_ffn_gate_w': 8.0,
     'L0_ffn_w13': 8.0,
     'L0_ffn_w2': 8.0}
    for name, (base, spread) in spreads.items():
        noise = np.random.default_rng([zlib.crc32(name.encode()), seed]).standard_normal(out[name].shape)
        drawn = base * np.exp(spread * noise) if base else spread * noise
        out[name] = jnp.asarray(drawn.astype(out[name].dtype))
    for name, factor in factors.items():
        out[name] = (out[name] * factor).astype(out[name].dtype)
    return out
```

```python
import math
from contextlib import ExitStack

import numpy as np
import concourse.bass as bass
from concourse import mybir

IMG, PATCH, CH = 224, 16, 12
SIDE = IMG // PATCH
HALF = PATCH // 2
GRP = 4
NG = CH // GRP
XP = GRP * SIDE * 2
XF = HALF * IMG
D = 192
HEADS, HD = 12, 16
PAIRS = HEADS // 2
TXT = 32
T = SIDE * SIDE + TXT
TT = T // 2
IMG1 = SIDE * SIDE - TT
C = D // 2
C1 = C + 1
E, TOPK, HID = 8, 2, 512
NEG = -1e30
FAR = 1 << 20
RW = 204
COL_W, COL_ID = D, D + E
LN_EPS, RMS_EPS = 1e-5, 1e-6
SUB = 4
ROWS = TT * SUB


def capacity(tokens):
    return int(math.ceil(1.25 * TOPK * tokens / E))


def constants(tokens):
    cap = capacity(tokens)
    f = np.float32
    freqs = f(1.0) / f(10000.0) ** (np.arange(0, HD, 2, dtype=f) / f(HD))
    ang = np.outer(np.arange(T, dtype=f), freqs.astype(f)).astype(f)
    cos = np.cos(ang).astype(f).reshape(2, TT, HD // 2).transpose(1, 0, 2)
    sin = np.sin(ang).astype(f).reshape(2, TT, HD // 2).transpose(1, 0, 2)
    p = np.arange(128)
    q = np.arange(TT)
    later = np.where(q[None, :] > q[:, None], f(NEG), f(0))
    mask_q1 = np.zeros((TT, 2, 2, TT), f)
    mask_q1[:, :, 1, :] = later[:, None, :]
    sel = np.zeros((128, HEADS, TT + 1), f)
    for h in range(HEADS):
        sel[h, h] = 1
        sel[HEADS + h, h] = 1
    term = (p // HD) % 4
    split = np.zeros((128, 4), f)
    split[:, 0] = np.where(term % 2 == 1, -1, 0)
    split[:, 1] = np.where(term >= 2, -1, 0)
    split[HEADS:2 * HEADS, 2] = -1
    split[2 * HEADS + 1, 3] = -1
    small = np.zeros((128, 2 * E + 2), f)
    small[:, 0:E] = np.arange(E) * cap
    small[:, E:2 * E] = np.arange(E)
    small[:, 2 * E] = p
    small[:, 2 * E + 1] = p + TT
    filler = np.zeros((TT, 2, 2, RW), np.uint32)
    for par in range(2):
        for s in range(2):
            filler[:, par, s, COL_ID] = tokens + (par * T + 2 * q + s) % ROWS
    rows = np.arange(XP)
    return {
        "cos": np.ascontiguousarray(cos),
        "sin": np.ascontiguousarray(np.concatenate([sin, -sin], -1)),
        "ident": np.eye(128, dtype=f),
        "mask_q0": np.ascontiguousarray(np.repeat(later[:, None], 4, 1)),
        "mask_q1": mask_q1.reshape(TT, 2, T),
        "mask_k": np.ascontiguousarray(np.repeat(later.T[:, None], 4, 1)),
        "sel": sel,
        "split": split,
        "small": small,
        "before": (q[:, None] < q[None, :]).astype(f),
        "patch": ((rows[:, None] // 2) % SIDE == np.arange(SIDE)[None]).astype(f),
        "filler": filler,
    }


CONST_NAMES = ["cos", "sin", "ident", "mask_q0", "mask_q1", "mask_k", "sel", "split", "small",
               "before", "patch", "filler"]


class Batch:

    def __init__(self, half, par, lag=0):
        self.par = (par - lag) % 2
        self.half = half + (par - lag) // 2
        self.b = 2 * half + (par - lag)

    def ago(self, n):
        return Batch(self.half, self.par, n)


def wait(eng, sem, value):
    if not (isinstance(value, int) and value <= 0):
        eng.wait_ge(sem, value)


def hold(eng, sem, value, held):
    eng.wait_ge(sem, value)
    eng.sem_inc(held, 1)


def build(nc, x, txt, chan_w, norm_scale, norm_bias, w_attn, b_attn, w_proj, b_proj, sinks,
          rezero, gate_t, w13_t, w2_t, norm_w_t, const, out):
    fp32, fp32r, bf16 = mybir.dt.float32, mybir.dt.float32r, mybir.dt.bfloat16
    u32 = mybir.dt.uint32
    ALU, ACT, AX = mybir.AluOpType, mybir.ActivationFunctionType, mybir.AxisListType

    B = x.shape[0]
    TOKENS = B * T
    CAP = capacity(TOKENS)
    SLOTS = E * CAP
    FILLS = CAP // T
    TILES = CAP // ROWS
    assert FILLS * T == CAP and TILES * ROWS == CAP and TILES % 2 == 0 and B % 2 == 0
    assert CAP % (2 * T) == 0

    moe_rows = nc.dram_tensor("moe_rows", [SLOTS + ROWS, RW], fp32).ap()

    ctx = ExitStack()
    with ctx:
        def sb(name, shape, dt=fp32):
            return ctx.enter_context(nc.sbuf_tensor(name, shape, dt))

        def sem(name):
            return ctx.enter_context(nc.semaphore(name))

        bank = [ctx.enter_context(nc.psum_tensor(f"bank{i}", [128, 512], fp32)) for i in range(8)]

        cos = sb("cos", [TT, 2, 8])
        sin = sb("sin", [TT, 2, 16])
        ident = sb("ident", [128, 128])
        ident_r = sb("ident_r", [128, 128], fp32r)
        mask_q0 = sb("mask_q0", [TT, 4, TT], fp32r)
        mask_q1 = sb("mask_q1", [TT, 2, T], fp32r)
        mask_k = sb("mask_k", [TT, 4, TT], fp32r)
        sel = sb("sel", [128, HEADS, TT + 1], fp32r)
        split = sb("split", [128, 4])
        small = sb("small", [128, 2 * E + 2])
        minus_half = sb("minus_half", [TT, 4])
        before = sb("before", [TT, TT], bf16)
        ones = sb("ones", [TT, TT], bf16)
        patch = sb("patch", [XP, SIDE])
        filler = sb("filler", [TT, 2, 2, RW], u32)
        chan = sb("chan", [XP, NG, D])
        scale_col = sb("scale_col", [C, 2])
        bias_col = sb("bias_col", [C, 2])
        w_qkv = sb("w_qkv", [C1, 2, 3 * D])
        b_row = sb("b_row", [1, 3 * D])
        b_fold = sb("b_fold", [1, 3 * D])
        w_out = sb("w_out", [C1, 2, D])
        rez = sb("rez", [C1, 1])
        sink_tok = sb("sink_tok", [TT, HEADS])
        sink_key = sb("sink_key", [128, HEADS])
        sink_hi = sb("sink_hi", [128, HEADS], fp32r)
        sink_ones = sb("sink_ones", [128, HEADS])
        gate = sb("gate", [C, 2, E])
        staging = sb("staging", [128, HEADS * (TT + 1)])

        arena = sb("arena", [128, 2 * NG * XF])
        xin = [arena[0:XP, NG * XF * i:NG * XF * (i + 1)].rearrange("p (g f) -> p g f", g=NG) for i in range(2)]
        pooled = [sb(f"pooled{i}", [XP, NG, SIDE]) for i in range(2)]
        spread = sb("spread", [XP, NG, SIDE * SIDE])
        h = [sb(f"h{i}", [TT, 2, D]) for i in range(2)]
        st1 = sb("st1", [TT, 2, 6])
        mv1 = sb("mv1", [TT, 2, 2])
        rstd1 = sb("rstd1", [TT, 2])
        var1 = sb("var1", [TT, 2])
        xn = sb("xn", [TT, 2, 2, C1])
        xn_t = sb("xn_t", [C1, 2, T])
        rot_c = sb("rot_c", [TT, 2, 2 * D])
        rot_s = sb("rot_s", [TT, 2, 2 * D])
        qk = sb("qk", [TT, 2, 2 * HEADS, 4, HD])
        val = [sb(f"val{i}", [TT + 1, 2, HEADS, 32]) for i in range(2)]
        rounded = [sb(f"rounded{i}", [128, 4 * TT], fp32r) for i in range(2)]
        q_t = sb("q_t", [128, HEADS, T], fp32r)
        k_t = sb("k_t", [128, PAIRS, 2, TT + 1], fp32r)
        top = sb("top", [TT, 2, HEADS])
        shift = sb("shift", [TT, 2, 128])
        shift_hi = sb("shift_hi", [128, T], fp32r)
        shift_t = sb("shift_t", [128, T], fp32r)
        prob = sb("prob", [128, HEADS * T])
        prob0 = prob[0:TT + 1, :].rearrange("p (a n) -> p a n", a=HEADS)
        prob1 = sb("prob1", [TT, HEADS, TT])
        y_t = sb("y_t", [128, 3, T])
        rden = sb("rden", [TT, 2, HEADS])
        yn = sb("yn", [TT, 2, 2, C1])
        yn_t = sb("yn_t", [C1, 2, T])
        h2 = [sb(f"h2_{i}", [TT, 2, D]) for i in range(2)]
        st2 = sb("st2", [TT, 2, 6])
        mv2 = sb("mv2", [TT, 2, 2])
        rstd2 = sb("rstd2", [TT, 2])
        var2 = sb("var2", [TT, 2])
        row = [sb(f"row{i}", [TT, 2, RW]) for i in range(2)]
        xf_t = sb("xf_t", [C, 2, T])
        best = sb("best", [TT, 2, 8])
        best_i = sb("best_i", [TT, 2, 8], u32)
        best_f = sb("best_f", [TT, 2, 2])
        gap = sb("gap", [TT, 2])
        gexp = sb("gexp", [TT, 2])
        gden = sb("gden", [TT, 2])
        gw = sb("gw", [TT, 2, 2])
        hot = sb("hot", [TT, 2, 2, E])
        hot_sum = sb("hot_sum", [TT, 2, E], bf16)
        seen = sb("seen", [TT, E], bf16)
        over = sb("over", [TT, 2, E])
        place = sb("place", [TT, 2, E])
        pick = sb("pick", [TT, 2, 2, E])
        wpick = sb("wpick", [TT, 2, 2, E])
        slot_f = sb("slot_f", [TT, 4])
        slot = [sb(f"slot{i}", [TT, 4], u32) for i in range(2)]
        token = sb("token", [TT, 2])

        taken = 0

        def view(parts, a, b):
            nonlocal taken
            taken += a * b
            assert taken <= 2 * NG * XF
            return arena[0:parts, taken - a * b:taken].rearrange("p (a b) -> p a b", a=a)

        w_raw = view(128, 2, 2 * HID)
        xr = [view(TT, SUB, RW) for _ in range(2)]
        z = view(TT, SUB, 256)
        act_g = view(128, 2, ROWS)
        hid = view(128, 4, ROWS)
        y = view(TT, SUB, D)
        ys = [view(TT, SUB, D) for _ in range(2)]
        nw = sb("nw", [128, 2])
        w_hi = [sb(f"w_hi{i}", [128, 2, 2 * HID], fp32r) for i in range(2)]
        w_lo = [sb(f"w_lo{i}", [128, 2, 2 * HID], fp32r) for i in range(2)]
        w_dn = [prob[:, 4 * D * i:4 * D * (i + 1)].rearrange("p (j n) -> p j n", j=4) for i in range(2)]
        sq = prob[0:TT, 8 * D:(8 + SUB) * D].rearrange("p (s n) -> p s n", s=SUB)
        ssum = sb("ssum", [TT, SUB])
        rms = sb("rms", [TT, SUB])
        rms2 = sb("rms2", [TT, SUB])
        za_hi = sb("za_hi", [128, ROWS], fp32r)
        za_lo = sb("za_lo", [128, ROWS], fp32r)
        zb_hi = sb("zb_hi", [128, ROWS], fp32r)
        zb = sb("zb", [128, ROWS], fp32r)
        w_slot = sb("w_slot", [TT, SUB])
        who = [sb(f"who{i}", [TT, SUB], u32) for i in range(2)]

        loaded = sem("loaded")
        staged = sem("staged")
        unstaged = sem("unstaged")
        cleared = sem("cleared")
        prepared = sem("prepared")
        fold_done = sem("fold_done")
        folded = sem("folded")
        bias_placed = sem("bias_placed")
        held = sem("held")
        step0 = sem("step0")

        x_loaded = [sem(f"x_loaded{i}") for i in range(2)]
        txt_loaded = [sem(f"txt_loaded{i}") for i in range(2)]
        filled = [sem(f"filled{i}") for i in range(2)]
        h2_stored = [sem(f"h2_stored{i}") for i in range(2)]
        scattered = [sem(f"scattered{i}") for i in range(2)]
        spare_set = sem("spare_set")
        x_pooled = sem("x_pooled")
        x_spread = sem("x_spread")
        h_summed = sem("h_summed")
        h_copied = sem("h_copied")
        ln1_step, ln1_done = sem("ln1_step"), sem("ln1_done")
        xn_turned, xn_ready = sem("xn_turned"), sem("xn_ready")
        qk_made = [sem(f"qk_made{t}") for t in range(2)]
        v_made, v_ready = sem("v_made"), sem("v_ready")
        qk_read = [sem(f"qk_read{t}") for t in range(2)]
        qk_rotated = [sem(f"qk_rotated{t}") for t in range(2)]
        qk_turned = [sem(f"qk_turned{k}") for k in range(6)]
        qk_rounded = sem("qk_rounded")
        qk_split = [sem(f"qk_split{k}") for k in range(6)]
        scored = [sem(f"scored{k}") for k in range(9)]
        maxed = [sem(f"maxed{k}") for k in range(9)]
        top_sink, shift_made = sem("top_sink"), sem("shift_made")
        shift_turned, shift_rounded, shift_ready = (sem(n) for n in ("shift_turned", "shift_rounded", "shift_ready"))
        scored_t = [sem(f"scored_t{k}") for k in range(9)]
        probed = [sem(f"probed{k}") for k in range(9)]
        attended = [sem(f"attended{g}") for g in range(3)]
        y_copied = sem("y_copied")
        y_turned = [sem(f"y_turned{t}") for t in range(2)]
        den_ready = sem("den_ready")
        y_normed = sem("y_normed")
        yn_turned, yn_ready = sem("yn_turned"), sem("yn_ready")
        projected, h2_made = sem("projected"), sem("h2_made")
        ln2_step, ln2_done = sem("ln2_step"), sem("ln2_done")
        xf_turned, xf_ready = sem("xf_turned"), sem("xf_ready")
        gated, ranked, gaps_made, gate_exp = (sem(n) for n in ("gated", "ranked", "gaps_made", "gate_exp"))
        indexed = sem("indexed")
        hots_summed, ranks_made = sem("hots_summed"), sem("ranks_made")
        route_step = sem("route_step")
        weights_made, row_whole, ranks_read = sem("weights_made"), sem("row_whole"), sem("ranks_read")
        seen_counted = sem("seen_counted")
        routed = sem("routed")

        w_loaded = sem("w_loaded")
        w_rounded = sem("w_rounded")
        w_split = sem("w_split")
        rows_loaded = [sem(f"rows_loaded{i}") for i in range(2)]
        squared, rms_sum, rms_made, z_scaled, z_made = (sem(n) for n in ("squared", "rms_sum", "rms_made", "z_scaled", "z_made"))
        za_turned, zb_turned = sem("za_turned"), sem("zb_turned")
        za_rounded, zb_rounded = sem("za_rounded"), sem("zb_rounded")
        za_split, zb_split = sem("za_split"), sem("zb_split")
        gate_up = [sem(f"gate_up{j}") for j in range(4)]
        silued = sem("silued")
        hid_made = [sem(f"hid_made{j}") for j in range(4)]
        down = sem("down")
        y_added, y_weighted = sem("y_added"), sem("y_weighted")
        added = [sem(f"added{i}") for i in range(2)]

        N_SMALL = 21
        MASKS = 5

        def setup_sync(sp):
            for dst, src in (
                (cos[:, :, :], const["cos"]), (sin[:, :, :], const["sin"]), (ident[:, :], const["ident"]),
                (split[:, :], const["split"]), (small[:, :], const["small"]),
                (patch[:, :], const["patch"]), (filler[:, :, :, :], const["filler"]),
                (scale_col[:, :], norm_scale.rearrange("(c p) -> p c", p=C)),
                (bias_col[:, :], norm_bias.rearrange("(c p) -> p c", p=C)),
                (w_qkv[0:C, :, :], w_attn.rearrange("(c p) n -> p c n", p=C)),
                (b_row[:, :], b_attn.rearrange("(a n) -> a n", a=1)),
                (rez[:, :], rezero.rearrange("(a n) -> a n", a=1).to_broadcast([C1, 1])),
                (sink_tok[:, :], sinks.rearrange("(a n) -> a n", a=1).to_broadcast([TT, HEADS])),
                (gate[:, :, :], gate_t.rearrange("(c p) n -> p c n", p=C)),
            ):
                with nc.allow_non_contiguous_dma(reason="columns of a few vectors"):
                    sp.dma_start(dst, src).then_inc(loaded, 16)
            for g in range(NG):
                sp.dma_start(chan[:, g, :], chan_w[GRP * g:GRP * (g + 1), :].unsqueeze(1)
                             .to_broadcast([GRP, SIDE * 2, D])).then_inc(loaded, 16)
            sp.wait_ge(cleared, 1)
            sp.dma_start(w_out[0:C, :, :], w_proj.rearrange("(c p) n -> p c n", p=C)).then_inc(loaded, 16)
            sp.dma_start(w_out[C:C1, 1, :], b_proj.rearrange("(a n) -> a n", a=1)).then_inc(loaded, 16)
            for r in range(2):
                sp.dma_start(sink_key[2 * HEADS + r:2 * HEADS + r + 1, :],
                             sinks.rearrange("(a n) -> a n", a=1)).then_inc(loaded, 16)
            for n, (name, parts, width) in enumerate((("mask_q0", TT, 4 * TT), ("mask_q1", TT, 2 * T),
                                                      ("mask_k", TT, 4 * TT), ("sel", 128, HEADS * (TT + 1)),
                                                      ("before", TT, TT))):
                wait(sp, unstaged, n)
                src = const[name]
                if len(src.shape) == 3:
                    src = src.rearrange("p a b -> p (a b)")
                sp.dma_start(staging[0:parts, 0:width], src).then_inc(staged, 16)
            sp.wait_ge(loaded, 16 * N_SMALL)
            sp.dma_start(out[TOKENS:TOKENS + ROWS, :].rearrange("(p s) n -> p s n", s=SUB),
                         filler[:, 0, 0, 0:D].bitcast(fp32).unsqueeze(1).to_broadcast([TT, SUB, D])
                         ).then_inc(spare_set, 16)
            sp.dma_start(moe_rows[SLOTS:SLOTS + ROWS, :].rearrange("(a p s) n -> p a (s n)", p=TT, s=2),
                         filler[:, 0:ROWS // T, :, :].bitcast(fp32).rearrange("p a s n -> p a (s n)")
                         ).then_inc(spare_set, 16)
            sp.wait_ge(folded, 1)
            sp.dma_start(w_qkv[C:C1, 1, :], b_fold[:, :]).then_inc(bias_placed, 16)

        x_img = x.rearrange("b (g c) (q r) w -> b (c q) g (r w)", g=NG, r=HALF)
        out_b = out[0:TOKENS, :].rearrange("(b t p) n -> b p t n", t=2, p=TT)
        rows_e = moe_rows[0:SLOTS, :].rearrange("(e f p s) n -> f p e (s n)", e=E, p=TT, s=2)

        def load_image(sp, at):
            wait(sp, x_pooled, at.b - 1)
            sp.dma_start(xin[at.par][:, :, :], x_img[at.b, :, :, :]).then_inc(x_loaded[at.par], 16)

        def load_text(sp, at):
            wait(sp, h2_made, at.b - 1)
            sp.dma_start(h[at.par][IMG1:TT, 1, :], txt[at.b, :, :]).then_inc(txt_loaded[at.par], 16)

        def fill_slots(sp, at):
            wait(sp, filled[at.par], 16 * at.half)
            sp.dma_start(rows_e[at.b, :, :, :],
                         filler[:, at.par, :, :].bitcast(fp32).rearrange("p s n -> p (s n)")
                         .unsqueeze(1).to_broadcast([TT, E, 2 * RW])).then_inc(filled[at.par], 16)

        def store_h2(sp, at):
            sp.wait_ge(h2_made, at.b + 1)
            sp.dma_start(out_b[at.b, :, :, :], h2[at.par][:, :, :]).then_inc(h2_stored[at.par], 16)

        def setup_vector(dve):
            n = 0

            def done(ins):
                nonlocal n
                n += 1
                ins.then_inc(step0, 1)

            nc.vector.memset(sink_key[:, :], 0.0)
            nc.vector.memset(minus_half[:, :], -0.5)
            nc.vector.memset(w_out[:, :, :], 0.0).then_inc(cleared, 1)
            for tile in (w_qkv[C:C1, :, :], k_t[:, :, :, :].bitcast(fp32), q_t[:, :, :].bitcast(fp32),
                         shift[:, :, :], seen[:, :], val[0][:, :, :, :], val[1][:, :, :, :], row[0][:, :, :],
                         row[1][:, :, :]):
                nc.vector.memset(tile, 0.0)
            done(nc.vector.memset(ones[:, :], 1.0))
            dve.wait_ge(step0, n)
            for tile in (xn[:, :, :, C:C1], yn[:, :, :, C:C1], shift[:, :, 2 * HEADS:2 * HEADS + 2],
                         val[0][:, :, :, HD:HD + 1], val[1][:, :, :, HD:HD + 1]):
                nc.vector.memset(tile, 1.0)
            dve.wait_ge(loaded, 16 * N_SMALL)
            for k, (dst, parts, width) in enumerate((
                    (mask_q0[:, :, :], TT, 4 * TT), (mask_q1[:, :, :], TT, 2 * T), (mask_k[:, :, :], TT, 4 * TT),
                    (sel[:, :, :], 128, HEADS * (TT + 1)), (before[:, :], TT, TT))):
                dve.wait_ge(staged, 16 * (k + 1))
                src = staging[0:parts, 0:width]
                if len(dst.shape) == 3:
                    src = src.rearrange("p (a b) -> p a b", a=dst.shape[1])
                nc.vector.tensor_copy(dst, src).then_inc(unstaged, 1)
            nc.vector.tensor_copy(ident_r[:, :], ident[:, :])
            nc.vector.tensor_scalar(sink_tok[:, :], sink_tok[:, :], 4.0, None, ALU.mult)
            done(nc.vector.tensor_scalar(sink_ones[:, :], sink_key[:, :], 4.0, None, ALU.mult))
            nc.vector.tensor_copy(token[:, :], small[0:TT, 2 * E:2 * E + 2])
            dve.wait_ge(step0, n)
            done(nc.vector.tensor_copy(sink_hi[:, :], sink_ones[:, :]))
            dve.wait_ge(step0, n)
            done(nc.vector.scalar_tensor_tensor(out=sink_ones[:, :], in0=sink_hi[:, :].bitcast(fp32), scalar=split[:, 3:4],
                                                in1=sink_ones[:, :], op0=ALU.mult, op1=ALU.add))
            dve.wait_ge(step0, n)
            dve.wait_ge(unstaged, 4)
            sink_col = staging[:, 0:HEADS]
            dve.wait_ge(unstaged, 5)
            done(nc.vector.tensor_copy(sink_col, sel[:, :, TT:TT + 1].bitcast(fp32).rearrange("p a b -> p (a b)")))
            dve.wait_ge(step0, n)
            sink_at = sel[:, :, TT:TT + 1].rearrange("p a b -> p (a b)")
            done(nc.vector.tensor_tensor(sink_at, sink_ones[:, :], sink_col, ALU.add))
            dve.wait_ge(fold_done, 1)
            nc.vector.tensor_tensor(b_fold[:, 0:288], bank[0][0:1, 0:288], b_row[:, 0:288], ALU.add)
            nc.vector.tensor_tensor(b_fold[:, 288:576], bank[1][0:1, 0:288], b_row[:, 288:576],
                                    ALU.add).then_inc(folded, 1)
            for c in range(2):
                nc.vector.tensor_scalar(w_qkv[0:C, c, :], w_qkv[0:C, c, :], scale_col[:, c:c + 1], None, ALU.mult)
            nc.vector.tensor_scalar(w_out[:, :, :], w_out[:, :, :], rez[:, 0:1], None,
                                    ALU.mult).then_inc(prepared, 1)
            dve.wait_ge(prepared, 1)
            dve.wait_ge(step0, n)

        def setup_tensor(pe):
            pe.wait_ge(loaded, 16 * N_SMALL)
            for half in range(2):
                for c in range(2):
                    last = nc.tensor.matmul(bank[half][0:1, 0:288], bias_col[:, c:c + 1],
                                            w_qkv[0:C, c, 288 * half:288 * (half + 1)],
                                            start=(c == 0), stop=(c == 1))
            last.then_inc(fold_done, 1)
            pe.wait_ge(prepared, 1)
            pe.wait_ge(bias_placed, 16)

        def pool_image(dve, at, g):
            if g == 0:
                dve.wait_ge(x_loaded[at.par], 16 * (at.half + 1))
                wait(dve, x_spread, at.b - 1)
            ins = nc.vector.tensor_reduce(
                pooled[at.par][:, g, :], xin[at.par][:, g, :].rearrange("p (r j c) -> p j r c", r=HALF, c=PATCH),
                AX.XY, ALU.add)
            if g == NG - 1:
                ins.then_inc(x_pooled, 1)

        def norm1(dve, at):
            n = at.b + 1
            dve.wait_ge(h_copied, n)
            dve.wait_ge(txt_loaded[at.par], 16 * (at.half + 1))
            for t in range(2):
                ins = nc.vector.bn_stats(st1[:, t, :], h[at.par][:, t, :])
            ins.then_inc(ln1_step, 1)
            hold(dve, ln1_step, 4 * at.b + 1, held)
            for t in range(2):
                ins = nc.vector.bn_aggr(mv1[:, t, :], st1[:, t, :])
            ins.then_inc(ln1_step, 1)
            dve.wait_ge(ln1_step, 4 * at.b + 2)
            nc.vector.tensor_scalar(var1[:, :], mv1[:, :, 1:2].rearrange("p a b -> p (a b)"), LN_EPS, None,
                                    ALU.add).then_inc(ln1_step, 1)
            dve.wait_ge(ln1_step, 4 * at.b + 4)
            wait(dve, xn_turned, n - 1)
            for t in range(2):
                ins = nc.vector.tensor_scalar(xn[:, t, :, 0:C], h[at.par][:, t, :].rearrange("p (c k) -> p c k", c=2),
                                              mv1[:, t, 0:1], rstd1[:, t:t + 1], ALU.subtract, ALU.mult)
            ins.then_inc(ln1_done, 1)

        def rotate(dve, at, t):
            n = at.b + 1
            dve.wait_ge(qk_made[t], n)
            wait(dve, qk_rotated[t], 2 * at.b)
            src = bank[7][0:TT, 0:2 * D]
            nc.vector.tensor_tensor(rot_c[:, t, :].rearrange("p (a k) -> p a k", k=8), src.rearrange("p (a k) -> p a k", k=8),
                                    cos[:, t, :].unsqueeze(1).to_broadcast([TT, 48, 8]), ALU.mult)
            nc.vector.tensor_tensor(rot_s[:, t, :].rearrange("p (a k) -> p a k", k=16), src.rearrange("p (a k) -> p a k", k=16),
                                    sin[:, t, :].unsqueeze(1).to_broadcast([TT, 24, 16]), ALU.mult).then_inc(qk_read[t], 1)

        def split_qk(dve, at, k):
            n = at.b + 1
            dve.wait_ge(qk_rounded, 6 * at.b + k + 1)
            src, hi = bank[k % 4], rounded[k % 2]
            if k == 0:
                wait(dve, attended[2], at.b)
            if k < 3:
                for side in range(2):
                    lo = slice(64 * side, 64 * side + 64)
                    dst = q_t[lo, :, :].rearrange("p (a s) n -> p a s n", s=2)[:, 2 * k:2 * k + 2, side, :]
                    ins = nc.vector.scalar_tensor_tensor(
                        out=dst, in0=hi[lo, :].bitcast(fp32).rearrange("p (a n) -> p a n", a=2), scalar=split[lo, 0:1],
                        in1=src[lo, 0:4 * TT].rearrange("p (a n) -> p a n", a=2), op0=ALU.mult, op1=ALU.add)
            else:
                kk = k - 3
                dst = k_t[:, 2 * kk:2 * kk + 2, :, 0:TT].rearrange("p a t n -> p (a t) n")
                ins = nc.vector.scalar_tensor_tensor(
                    out=dst, in0=hi[:, :].bitcast(fp32).rearrange("p (a n) -> p a n", a=4), scalar=split[:, 1:2],
                    in1=src[:, 0:4 * TT].rearrange("p (a n) -> p a n", a=4), op0=ALU.mult, op1=ALU.add)
            ins.then_inc(qk_split[k], 1)

        def max_scores(dve, at, k):
            n = at.b + 1
            dve.wait_ge(scored[k], n)
            if k == 0:
                wait(dve, shift_made, at.b)
            if k < 3:
                dst, src = top[:, 0, 4 * k:4 * k + 4], bank[k % 4][0:TT, 0:4 * TT].rearrange("p (a n) -> p a n", a=4)
            else:
                kk = k - 3
                dst, src = top[:, 1, 2 * kk:2 * kk + 2], bank[k % 4][0:TT, 0:2 * T].rearrange("p (a n) -> p a n", a=2)
            nc.vector.tensor_reduce(dst, src, AX.X, ALU.max).then_inc(maxed[k], 1)

        def make_shift(dve, at):
            n = at.b + 1
            dve.wait_ge(maxed[8], n)
            nc.vector.tensor_tensor(top[:, :, :], top[:, :, :], sink_tok[:, :].unsqueeze(1).to_broadcast([TT, 2, HEADS]),
                                    ALU.max).then_inc(top_sink, 1)
            dve.wait_ge(top_sink, n)
            wait(dve, shift_turned, at.b)
            for part in range(2):
                ins = nc.vector.tensor_scalar(shift[:, :, HEADS * part:HEADS * (part + 1)], top[:, :, :], -1.0, None, ALU.mult)
            ins.then_inc(shift_made, 1)

        def split_shift(dve, at):
            dve.wait_ge(shift_rounded, at.b + 1)
            nc.vector.scalar_tensor_tensor(out=shift_t[:, :], in0=shift_hi[:, :].bitcast(fp32), scalar=split[:, 2:3],
                                           in1=bank[6][:, 0:T], op0=ALU.mult, op1=ALU.add).then_inc(shift_ready, 1)

        def normalize(dve, at, t):
            n = at.b + 1
            dve.wait_ge(y_turned[t], n)
            src = bank[6 + t][0:TT, 0:3 * 128].rearrange("p (a k) -> p a k", k=32)
            nc.vector.reciprocal(rden[:, t, :], src[:, :, HD:HD + 1].rearrange("p a b -> p (a b)")).then_inc(den_ready, 1)
            dve.wait_ge(den_ready, 2 * at.b + t + 1)
            if t == 0:
                wait(dve, yn_turned, at.b)
            for c in range(2):
                ins = nc.vector.tensor_tensor(yn[:, t, c, 0:C].rearrange("p (a k) -> p a k", k=HD), src[:, 6 * c:6 * c + 6, 0:HD],
                                              rden[:, t, 6 * c:6 * c + 6].unsqueeze(2).to_broadcast([TT, 6, HD]), ALU.mult)
            ins.then_inc(y_normed, 1)

        def residual(dve, at):
            n = at.b + 1
            dve.wait_ge(projected, n)
            wait(dve, h2_stored[at.par], 16 * at.half)
            nc.vector.tensor_tensor(h2[at.par][:, :, :], bank[7][0:TT, 0:2 * D].rearrange("p (t n) -> p t n", t=2),
                                    h[at.par][:, :, :], ALU.add).then_inc(h2_made, 1)

        def norm2(dve, at):
            n = at.b + 1
            dve.wait_ge(h2_made, n)
            for t in range(2):
                ins = nc.vector.bn_stats(st2[:, t, :], h2[at.par][:, t, :])
            ins.then_inc(ln2_step, 1)
            hold(dve, ln2_step, 4 * at.b + 1, held)
            for t in range(2):
                ins = nc.vector.bn_aggr(mv2[:, t, :], st2[:, t, :])
            ins.then_inc(ln2_step, 1)
            dve.wait_ge(ln2_step, 4 * at.b + 2)
            nc.vector.tensor_scalar(var2[:, :], mv2[:, :, 1:2].rearrange("p a b -> p (a b)"), LN_EPS, None,
                                    ALU.add).then_inc(ln2_step, 1)
            dve.wait_ge(ln2_step, 4 * at.b + 4)
            wait(dve, scattered[at.par], 64 * at.half)
            for t in range(2):
                ins = nc.vector.tensor_scalar(row[at.par][:, t, 0:D], h2[at.par][:, t, :], mv2[:, t, 0:1], rstd2[:, t:t + 1],
                                              ALU.subtract, ALU.mult)
            ins.then_inc(ln2_done, 1)

        def choose(dve, at):
            n = at.b + 1
            hold(dve, gated, n, held)
            for t in range(2):
                ins = nc.vector.max(best[:, t, :], bank[6][0:TT, E * t:E * (t + 1)])
            ins.then_inc(ranked, 1)
            hold(dve, ranked, n, held)
            for t in range(2):
                ins = nc.vector.max_index(best_i[:, t, :], best[:, t, :], bank[6][0:TT, E * t:E * (t + 1)])
            ins.then_inc(indexed, 1)
            nc.vector.tensor_tensor(gap[:, :], best[:, :, 1:2].rearrange("p a b -> p (a b)"),
                                    best[:, :, 0:1].rearrange("p a b -> p (a b)"), ALU.subtract).then_inc(gaps_made, 1)
            dve.wait_ge(indexed, n)
            nc.vector.tensor_copy(best_f[:, :, :], best_i[:, :, 0:2]).then_inc(route_step, 1)
            dve.wait_ge(route_step, 8 * at.b + 1)
            nc.vector.tensor_tensor(hot[:, :, :, :].rearrange("p t k e -> p (t k) e"),
                                    small[0:TT, E:2 * E].unsqueeze(1).to_broadcast([TT, 4, E]),
                                    best_f[:, :, :].rearrange("p t k -> p (t k)").unsqueeze(2).to_broadcast([TT, 4, E]),
                                    ALU.is_equal).then_inc(route_step, 1)
            dve.wait_ge(route_step, 8 * at.b + 2)
            wait(dve, seen_counted, at.b)
            nc.vector.tensor_tensor(hot_sum[:, :, :], hot[:, :, 0, :], hot[:, :, 1, :], ALU.add).then_inc(hots_summed, 1)

        def weigh(dve, at):
            n = at.b + 1
            dve.wait_ge(gate_exp, n)
            nc.vector.tensor_scalar(gden[:, :], gexp[:, :], 1.0, None, ALU.add).then_inc(route_step, 1)
            dve.wait_ge(route_step, 8 * at.b + 3)
            nc.vector.reciprocal(gw[:, :, 0:1].rearrange("p a b -> p (a b)"), gden[:, :]).then_inc(route_step, 1)
            dve.wait_ge(route_step, 8 * at.b + 4)
            nc.vector.tensor_tensor(gw[:, :, 1:2].rearrange("p a b -> p (a b)"), gexp[:, :],
                                    gw[:, :, 0:1].rearrange("p a b -> p (a b)"), ALU.mult).then_inc(weights_made, 1)
            dve.wait_ge(weights_made, n)
            nc.vector.tensor_tensor(wpick[:, :, :, :].rearrange("p t k e -> p (t k) e"), hot[:, :, :, :].rearrange("p t k e -> p (t k) e"),
                                    gw[:, :, :].rearrange("p t k -> p (t k)").unsqueeze(2).to_broadcast([TT, 4, E]),
                                    ALU.mult).then_inc(route_step, 1)
            dve.wait_ge(route_step, 8 * at.b + 5)
            nc.vector.tensor_tensor(row[at.par][:, :, COL_W:COL_W + E], wpick[:, :, 0, :], wpick[:, :, 1, :], ALU.add)
            nc.vector.tensor_copy(row[at.par][:, :, COL_ID:COL_ID + 1].bitcast(u32).rearrange("p a b -> p (a b)"),
                                  token[:, :]).then_inc(row_whole, 1)
            dve.wait_ge(row_whole, n)
            nc.vector.tensor_scalar(token[:, :], token[:, :], float(T), None, ALU.add)

        def assign(dve, at):
            n = at.b + 1
            dve.wait_ge(ranks_made, n)
            ranks = bank[6][0:TT, 0:2 * E].rearrange("p (t e) -> p t e", t=2)
            nc.vector.tensor_scalar(over[:, :, :], ranks, float(CAP), float(FAR), ALU.is_ge, ALU.mult)
            nc.vector.tensor_tensor(place[:, :, :], ranks, small[0:TT, 0:E].unsqueeze(1).to_broadcast([TT, 2, E]),
                                    ALU.add).then_inc(route_step, 1)
            dve.wait_ge(route_step, 8 * at.b + 6)
            nc.vector.tensor_tensor(place[:, :, :], place[:, :, :], over[:, :, :], ALU.add).then_inc(ranks_read, 1)
            dve.wait_ge(ranks_read, n)
            for k in range(2):
                ins = nc.vector.tensor_tensor(pick[:, :, k, :], hot[:, :, k, :], place[:, :, :], ALU.mult)
            ins.then_inc(route_step, 1)
            dve.wait_ge(route_step, 8 * at.b + 7)
            nc.vector.tensor_reduce(slot_f[:, :], pick[:, :, :, :].rearrange("p t k e -> p (t k) e"), AX.X,
                                    ALU.add).then_inc(route_step, 1)
            dve.wait_ge(route_step, 8 * at.b + 8)
            nc.vector.tensor_copy(slot[at.par][:, :], slot_f[:, :]).then_inc(routed, 1)
            nc.vector.tensor_tensor(seen[:, :], seen[:, :], hot_sum[:, 0, :], ALU.add).then_inc(seen_counted, 1)
            dve.wait_ge(seen_counted, 2 * at.b + 1)
            nc.vector.tensor_tensor(seen[:, :], seen[:, :], hot_sum[:, 1, :], ALU.add).then_inc(seen_counted, 1)

        def spread_patches(pool, at):
            pool.wait_ge(x_pooled, at.b + 1)
            wait(pool, h_summed, at.b)
            for g in range(NG):
                ins = nc.gpsimd.tensor_tensor(spread[:, g, :].rearrange("p (i j) -> p i j", j=SIDE),
                                              pooled[at.par][:, g, :].unsqueeze(1).to_broadcast([XP, SIDE, SIDE]),
                                              patch[:, :].unsqueeze(2).to_broadcast([XP, SIDE, SIDE]), ALU.mult)
            ins.then_inc(x_spread, 1)

        def inverse_std(pool, at, var, rstd, ln_step):
            pool.wait_ge(ln_step, 4 * at.b + 3)
            nc.gpsimd.tensor_tensor(rstd[:, :], var[:, :], minus_half[:, 0:2], ALU.pow).then_inc(ln_step, 1)

        def add_rotation(pool, at, t):
            n = at.b + 1
            pool.wait_ge(qk_read[t], n)
            if t == 0:
                wait(pool, qk_turned[5], at.b)
            for half in range(2):
                dst = qk[:, t, :, :, 8 * half:8 * half + 8]
                a = rot_c[:, t, :].rearrange("p (a s k) -> p a s k", s=2, k=8)[:, :, half, :].unsqueeze(2)
                b = rot_s[:, t, :].rearrange("p (a s k) -> p a s k", s=2, k=8)[:, :, 1 - half, :].unsqueeze(2)
                a, b = (v.to_broadcast([TT, 2 * HEADS, 4, 8]) for v in (a, b))
                nc.gpsimd.tensor_tensor(dst, a, b, ALU.add).then_inc(qk_rotated[t], 1)

        def copy_h(act, at):
            n = at.b + 1
            act.wait_ge(h_summed, n)
            wait(act, h2_made, n - 2)
            nc.scalar.activation(h[at.par][:, 0, :], bank[6][0:TT, 0:D], ACT.Copy)
            nc.scalar.activation(h[at.par][0:IMG1, 1, :], bank[6][0:IMG1, D:2 * D], ACT.Copy).then_inc(h_copied, 1)

        def copy_xn(act, at):
            act.wait_ge(xn_turned, at.b + 1)
            wait(act, v_made, at.b)
            nc.scalar.activation(xn_t[:, :, :], bank[7][0:C1, 0:2 * T].rearrange("p (c n) -> p c n", c=2),
                                 ACT.Copy).then_inc(xn_ready, 1)

        def copy_v(act, at):
            act.wait_ge(v_made, at.b + 1)
            wait(act, attended[2], at.b - 1)
            nc.scalar.activation(val[at.par][0:TT, :, :, 0:HD].rearrange("p t a k -> p (t a) k"),
                                 bank[6][0:TT, 0:2 * D].rearrange("p (a k) -> p a k", k=HD), ACT.Copy).then_inc(v_ready, 1)

        def round_qk(act, at, k):
            n = at.b + 1
            act.wait_ge(qk_turned[k], n)
            if k >= 2:
                act.wait_ge(qk_split[k - 2], n)
            else:
                wait(act, qk_split[k + 4], at.b)
            nc.scalar.activation(rounded[k % 2][:, :], bank[k % 4][:, 0:4 * TT], ACT.Copy).then_inc(qk_rounded, 1)

        def round_shift(act, at):
            act.wait_ge(shift_turned, at.b + 1)
            wait(act, shift_ready, at.b)
            nc.scalar.activation(shift_hi[:, :], bank[6][:, 0:T], ACT.Copy).then_inc(shift_rounded, 1)

        def exp_scores(act, at, k):
            g, m = divmod(k, 3)
            act.wait_ge(scored_t[k], at.b + 1)
            if m == 0:
                wait(act, attended[g], at.b)
            src = bank[k % 4]
            if m < 2:
                p = 2 * g + m
                nc.scalar.activation(prob0[:, 2 * p:2 * p + 2, :], src[0:TT + 1, 0:2 * T].rearrange("p (a n) -> p a n", a=2),
                                     ACT.Exp, scale=0.25).then_inc(probed[k], 1)
            else:
                nc.scalar.activation(prob1[:, 4 * g:4 * g + 4, :], src[0:TT, 0:4 * TT].rearrange("p (a n) -> p a n", a=4),
                                     ACT.Exp, scale=0.25).then_inc(probed[k], 1)

        def copy_y(act, at):
            act.wait_ge(attended[2], at.b + 1)
            wait(act, y_turned[1], at.b)
            nc.scalar.activation(y_t[:, 0:2, :], bank[4][:, 0:2 * T].rearrange("p (a n) -> p a n", a=2), ACT.Copy)
            nc.scalar.activation(y_t[:, 2, :], bank[5][:, 0:T], ACT.Copy).then_inc(y_copied, 1)

        def copy_yn(act, at):
            act.wait_ge(yn_turned, at.b + 1)
            wait(act, projected, at.b)
            nc.scalar.activation(yn_t[:, :, :], bank[6][0:C1, 0:2 * T].rearrange("p (c n) -> p c n", c=2),
                                 ACT.Copy).then_inc(yn_ready, 1)

        def copy_xf(act, at):
            act.wait_ge(xf_turned, at.b + 1)
            wait(act, gated, at.b)
            nc.scalar.activation(xf_t[:, :, :], bank[7][0:C, 0:2 * T].rearrange("p (c n) -> p c n", c=2),
                                 ACT.Copy).then_inc(xf_ready, 1)

        def exp_gap(act, at):
            act.wait_ge(gaps_made, at.b + 1)
            wait(act, weights_made, at.b)
            nc.scalar.activation(gexp[:, :], gap[:, :], ACT.Exp).then_inc(gate_exp, 1)

        def sum_channels(pe, at):
            n = at.b + 1
            pe.wait_ge(x_spread, n)
            wait(pe, yn_ready, n - 2)
            for t, (lo, hi) in enumerate(((0, TT), (TT, SIDE * SIDE))):
                for g in range(NG):
                    ins = nc.tensor.matmul(bank[6][0:hi - lo, D * t:D * (t + 1)], spread[:, g, lo:hi], chan[:, g, :],
                                           start=(g == 0), stop=(g == NG - 1))
            ins.then_inc(h_summed, 1)

        def turn_xn(pe, at):
            n = at.b + 1
            pe.wait_ge(ln1_done, n)
            wait(pe, xf_ready, n - 2)
            for c in range(2):
                for t in range(2):
                    ins = nc.tensor.transpose(bank[7][0:C1, T * c + TT * t:T * c + TT * (t + 1)], xn[:, t, c, :], ident[0:TT, 0:TT])
            ins.then_inc(xn_turned, 1)

        def make_qk(pe, at, t):
            n = at.b + 1
            if t == 0:
                pe.wait_ge(xn_ready, n)
            else:
                pe.wait_ge(qk_read[0], n)
            for c in range(2):
                ins = nc.tensor.matmul(bank[7][0:TT, 0:2 * D], xn_t[:, c, TT * t:TT * (t + 1)], w_qkv[:, c, 0:2 * D],
                                       start=(c == 0), stop=(c == 1))
            ins.then_inc(qk_made[t], 1)

        def make_v(pe, at):
            n = at.b + 1
            wait(pe, ranks_read, n - 2)
            for t in range(2):
                for c in range(2):
                    ins = nc.tensor.matmul(bank[6][0:TT, D * t:D * (t + 1)], xn_t[:, c, TT * t:TT * (t + 1)],
                                           w_qkv[:, c, 2 * D:3 * D], start=(c == 0), stop=(c == 1))
            ins.then_inc(v_made, 1)

        def turn_qk(pe, at, k):
            n = at.b + 1
            if k == 0:
                pe.wait_ge(qk_rotated[1], 2 * n)
                pe.wait_ge(qk_rotated[0], 2 * n)
            if k < 4:
                wait(pe, probed[5 + k], at.b)
            else:
                pe.wait_ge(qk_split[k - 4], n)
            for a in range(2):
                for t in range(2):
                    src = qk[:, t, 4 * k + 2 * a:4 * k + 2 * a + 2, :, :].rearrange("p a s k -> p (a s k)")
                    ins = nc.tensor.transpose(bank[k % 4][:, TT * (2 * a + t):TT * (2 * a + t + 1)], src, ident[0:TT, 0:TT])
            ins.then_inc(qk_turned[k], 1)

        RING_S = [2, 3, 4, 5]

        def score(pe, at, k):
            n = at.b + 1
            if k == 0:
                for m in range(6):
                    pe.wait_ge(qk_split[m], n)
            elif k >= 4:
                pe.wait_ge(maxed[k - 4], n)
            dst = bank[k % 4]
            if k < 3:
                nc.tensor.matmul(dst[0:TT, 0:4 * TT], ident_r[0:TT, 0:TT], mask_q0[:, :, :], start=True, stop=False)
                for a in range(4):
                    hh = 4 * k + a
                    ins = nc.tensor.matmul(dst[0:TT, TT * a:TT * (a + 1)], q_t[:, hh, 0:TT], k_t[:, hh // 2, 0, 0:TT],
                                           start=False, stop=(a == 3))
            else:
                kk = k - 3
                nc.tensor.matmul(dst[0:TT, 0:2 * T], ident_r[0:TT, 0:TT], mask_q1[:, :, :], start=True, stop=False)
                for a in range(2):
                    hh = 2 * kk + a
                    ins = nc.tensor.matmul(dst[0:TT, T * a:T * (a + 1)], q_t[:, hh, TT:T], k_t[:, kk, :, 0:TT],
                                           start=False, stop=(a == 1))
            ins.then_inc(scored[k], 1)

        def turn_shift(pe, at):
            n = at.b + 1
            pe.wait_ge(shift_made, n)
            for t in range(2):
                ins = nc.tensor.transpose(bank[6][:, TT * t:TT * (t + 1)], shift[:, t, :], ident[0:TT, 0:TT])
            ins.then_inc(shift_turned, 1)

        def score_t(pe, at, k):
            n = at.b + 1
            g, m = divmod(k, 3)
            if k == 0:
                pe.wait_ge(shift_ready, n)
                pe.wait_ge(maxed[8], n)
            elif k < 4:
                pe.wait_ge(maxed[4 + k], n)
            else:
                pe.wait_ge(probed[k - 4], n)
            dst = bank[k % 4]
            if m < 2:
                p = 2 * g + m
                nc.tensor.matmul(dst[0:TT + 1, 0:2 * T], k_t[:, p, 0, :], q_t[:, 2 * p:2 * p + 2, :], start=True, stop=False)
                for a in range(2):
                    nc.tensor.matmul(dst[0:TT + 1, T * a:T * (a + 1)], sel[:, 2 * p + a, :], shift_t[:, :], start=False, stop=False)
                ins = nc.tensor.matmul(dst[0:TT, 0:2 * T].rearrange("p (a n) -> p a n", a=2)[:, :, 0:TT], ident_r[0:TT, 0:TT],
                                       mask_k[:, 0:2, :], start=False, stop=True)
            else:
                nc.tensor.matmul(dst[0:TT, 0:4 * TT], ident_r[0:TT, 0:TT], mask_k[:, :, :], start=True, stop=False)
                for p in range(2):
                    nc.tensor.matmul(dst[0:TT, 2 * TT * p:2 * TT * (p + 1)], k_t[:, 2 * g + p, 1, 0:TT],
                                     q_t[:, 4 * g + 2 * p:4 * g + 2 * p + 2, TT:T], start=False, stop=False)
                for a in range(4):
                    ins = nc.tensor.matmul(dst[0:TT, TT * a:TT * (a + 1)], sel[:, 4 * g + a, 0:TT], shift_t[:, TT:T],
                                           start=False, stop=(a == 3))
            ins.then_inc(scored_t[k], 1)

        def attend(pe, at, g):
            n = at.b + 1
            if g == 0:
                wait(pe, y_copied, at.b)
                pe.wait_ge(v_ready, n)
            for m in range(3):
                pe.wait_ge(probed[3 * g + m], n)
            dst = bank[4][:, T * g:T * (g + 1)] if g < 2 else bank[5][:, 0:T]
            for a in range(4):
                hh = 4 * g + a
                nc.tensor.matmul(dst[32 * a:32 * a + 32, :], val[at.par][:, 0, hh, :], prob0[:, hh, :], start=True, stop=False,
                                 skip_group_check=True)
                ins = nc.tensor.matmul(dst[32 * a:32 * a + 32, TT:T], val[at.par][0:TT, 1, hh, :], prob1[:, hh, :], start=False,
                                       stop=True, skip_group_check=True)
            ins.then_inc(attended[g], 1)

        def after(at):
            return min(at.b + 2, B) if isinstance(at.b, int) else at.b + 2

        def turn_y(pe, at, t):
            n = at.b + 1
            if t == 0:
                pe.wait_ge(y_copied, n)
                if isinstance(at.b, int):
                    wait(pe, ranks_read, at.b)
            if t == 0:
                pe.wait_ge(v_ready, after(at))
            else:
                pe.wait_ge(qk_read[1], after(at))
            for g in range(3):
                ins = nc.tensor.transpose(bank[6 + t][0:TT, 128 * g:128 * (g + 1)], y_t[:, g, TT * t:TT * (t + 1)], ident[:, :])
            ins.then_inc(y_turned[t], 1)

        def turn_yn(pe, at):
            n = at.b + 1
            pe.wait_ge(y_normed, 2 * n)
            for c in range(2):
                for t in range(2):
                    ins = nc.tensor.transpose(bank[6][0:C1, T * c + TT * t:T * c + TT * (t + 1)], yn[:, t, c, :], ident[0:TT, 0:TT])
            ins.then_inc(yn_turned, 1)

        def project(pe, at):
            n = at.b + 1
            pe.wait_ge(yn_ready, n)
            for t in range(2):
                for c in range(2):
                    ins = nc.tensor.matmul(bank[7][0:TT, D * t:D * (t + 1)], yn_t[:, c, TT * t:TT * (t + 1)], w_out[:, c, :],
                                           start=(c == 0), stop=(c == 1))
            ins.then_inc(projected, 1)

        def turn_xf(pe, at):
            n = at.b + 1
            pe.wait_ge(ln2_done, n)
            for c in range(2):
                for t in range(2):
                    ins = nc.tensor.transpose(bank[7][0:C, T * c + TT * t:T * c + TT * (t + 1)], row[at.par][:, t, C * c:C * (c + 1)],
                                              ident[0:TT, 0:TT])
            ins.then_inc(xf_turned, 1)

        def gate_logits(pe, at):
            n = at.b + 1
            pe.wait_ge(xf_ready, n)
            pe.wait_ge(shift_ready, after(at))
            for t in range(2):
                for c in range(2):
                    ins = nc.tensor.matmul(bank[6][0:TT, E * t:E * (t + 1)], xf_t[:, c, TT * t:TT * (t + 1)], gate[:, c, :],
                                           start=(c == 0), stop=(c == 1))
            ins.then_inc(gated, 1)

        def rank(pe, at):
            n = at.b + 1
            pe.wait_ge(hots_summed, n)
            wait(pe, seen_counted, 2 * at.b)
            first, second = bank[6][0:TT, 0:E], bank[6][0:TT, E:2 * E]
            nc.tensor.matmul(first, before[:, :], hot_sum[:, 0, :], start=True, stop=False)
            nc.tensor.matmul(first, ones[:, :], seen[:, :], start=False, stop=True)
            nc.tensor.matmul(second, before[:, :], hot_sum[:, 1, :], start=True, stop=False)
            nc.tensor.matmul(second, ones[:, :], hot_sum[:, 0, :], start=False, stop=False)
            nc.tensor.matmul(second, ones[:, :], seen[:, :], start=False, stop=True).then_inc(ranks_made, 1)

        def step_tensor(pe, a, m, z):
            if m:
                for k in range(6):
                    turn_qk(pe, m, k)
            if z:
                turn_y(pe, z, 0)
                turn_y(pe, z, 1)
            if m:
                for k in range(3):
                    score(pe, m, k)
            if z:
                turn_yn(pe, z)
            if m:
                for k in range(3, 6):
                    score(pe, m, k)
            if z:
                project(pe, z)
            if m:
                for k in range(6, 9):
                    score(pe, m, k)
            if a:
                sum_channels(pe, a)
            if z:
                turn_xf(pe, z)
            if m:
                if a:
                    pe.wait_ge(h_copied, a.b + 1)
                turn_shift(pe, m)
            if a:
                turn_xn(pe, a)
            if z:
                gate_logits(pe, z)
            if m:
                for k in range(3):
                    score_t(pe, m, k)
            if a:
                make_qk(pe, a, 0)
            if m:
                for k in range(3, 5):
                    score_t(pe, m, k)
            if z:
                rank(pe, z)
            if m:
                attend(pe, m, 0)
            if a:
                make_qk(pe, a, 1)
            if m:
                for k in range(5, 7):
                    score_t(pe, m, k)
            if a:
                make_v(pe, a)
            if m:
                attend(pe, m, 1)
                for k in range(7, 9):
                    score_t(pe, m, k)
                attend(pe, m, 2)

        def step_scalar(act, a, m, z):
            if m:
                for k in range(6):
                    round_qk(act, m, k)
            if z:
                copy_yn(act, z)
            if a:
                copy_h(act, a)
            if z:
                copy_xf(act, z)
            if m:
                round_shift(act, m)
            if a:
                copy_xn(act, a)
            if z:
                exp_gap(act, z)
            if m:
                for k in range(7):
                    exp_scores(act, m, k)
            if a:
                copy_v(act, a)
            if m:
                for k in range(7, 9):
                    exp_scores(act, m, k)
                copy_y(act, m)

        def step_vector(dve, a, m, z):
            if m:
                for k in range(6):
                    split_qk(dve, m, k)
            if z:
                normalize(dve, z, 0)
                normalize(dve, z, 1)
            if a:
                pool_image(dve, a, 0)
            if m:
                for k in range(3):
                    max_scores(dve, m, k)
            if a:
                pool_image(dve, a, 1)
            if m:
                for k in range(3, 6):
                    max_scores(dve, m, k)
            if a:
                pool_image(dve, a, 2)
            if z:
                residual(dve, z)
                norm2(dve, z)
            if m:
                for k in range(6, 9):
                    max_scores(dve, m, k)
                make_shift(dve, m)
                split_shift(dve, m)
            if a:
                norm1(dve, a)
            if z:
                choose(dve, z)
            if a:
                rotate(dve, a, 0)
            if z:
                weigh(dve, z)
                assign(dve, z)
            if a:
                rotate(dve, a, 1)

        PEEL = 4

        def steps(eng, step):
            def one(half, par, known):
                i = 2 * half + par if known else None
                a = Batch(half, par) if not known or i < B else None
                m = Batch(half, par, 1) if not known or 0 <= i - 1 < B else None
                z = Batch(half, par, 2) if not known or 0 <= i - 2 < B else None
                step(eng, a, m, z)

            for i in range(PEEL):
                one(i // 2, i % 2, True)
            with eng.Fori(PEEL // 2, B // 2) as half:
                one(half, 0, False)
                one(half, 1, False)
            for i in range(B, B + 2):
                one(i // 2, i % 2, True)

        def pass1_sync(sp):
            def one(half, par, fill, first=False, last=False, n=None):
                z = None if first else Batch(half, par, 2)
                if not last:
                    a = Batch(half, par)
                    load_image(sp, a)
                    load_text(sp, a)
                    if fill:
                        fill_slots(sp, a)
                if z:
                    store_h2(sp, z)

            for i in range(PEEL):
                one(i // 2, i % 2, i < FILLS, first=i < 2)
            with sp.Fori(PEEL // 2, FILLS // 2) as half:
                one(half, 0, True)
                one(half, 1, True)
            with sp.Fori(FILLS // 2, B // 2) as half:
                one(half, 0, False)
                one(half, 1, False)
            for i in range(B, B + 2):
                one(i // 2, i % 2, False, last=True)
            for par in range(2):
                sp.wait_ge(h2_stored[par], 16 * (B // 2))
            sp.wait_ge(spare_set, 32)

        def pass1_gpsimd(pool):
            def one(half, par, known, fill=None):
                i = 2 * half + par if known else None
                a = Batch(half, par) if not known or i < B else None
                z = Batch(half, par, 2) if not known or 0 <= i - 2 < B else None
                if a:
                    spread_patches(pool, a)
                if z:
                    inverse_std(pool, z, var2, rstd2, ln2_step)
                if a:
                    inverse_std(pool, a, var1, rstd1, ln1_step)
                    add_rotation(pool, a, 0)
                if z:
                    scatter_waits(pool, z, fill)
                if a:
                    add_rotation(pool, a, 1)

            for i in range(PEEL):
                one(i // 2, i % 2, True)
            with pool.Fori(PEEL // 2, FILLS // 2) as half:
                one(half, 0, False, True)
                one(half, 1, False, True)
            with pool.Fori(FILLS // 2, B // 2) as half:
                one(half, 0, False, False)
                one(half, 1, False, False)
            for i in range(B, B + 2):
                one(i // 2, i % 2, True)

        def scatter_waits(pool, z, fill):
            if fill or (fill is None and z.b < FILLS):
                pool.wait_ge(filled[z.par], 16 * (z.half + 1))
            else:
                pool.wait_ge(filled[z.par], 16 * (FILLS // 2))
            scatter_rows(pool, z)

        def scatter_rows(pool, at):
            pool.wait_ge(row_whole, at.b + 1)
            hold(pool, routed, at.b + 1, held)
            for t in range(2):
                for k in range(TOPK):
                    nc.gpsimd.indirect_dma_start(
                        out=moe_rows[0:SLOTS, :],
                        out_offset=bass.IndirectOffsetOnAxis(ap=slot[at.par][:, 2 * t + k:2 * t + k + 1], axis=0),
                        in_=row[at.par][:, t, :], in_offset=None, bounds_check=SLOTS - 1, oob_is_err=False,
                    ).then_inc(scattered[at.par], 16)

        rows_n = moe_rows.rearrange("(n p s) w -> n p s w", p=TT, s=SUB)

        def load_expert(sp, e):
            sp.wait_ge(w_split, e) if not isinstance(e, int) or e else None
            if not isinstance(e, int) or e:
                sp.wait_ge(down, TILES * (e - 1)) if not isinstance(e, int) or e > 1 else None
            for dst, src in ((w_raw[:, 0, :], w13_t[e, 0:128, :]), (w_raw[0:64, 1, :], w13_t[e, 128:D, :]),
                             (w_raw[64:128, 1, :], w13_t[e, 128:D, :]),
                             (nw[:, 0:1], norm_w_t[e, 0:128, :]), (nw[0:64, 1:2], norm_w_t[e, 128:D, :]),
                             (nw[64:128, 1:2], norm_w_t[e, 128:D, :])):
                sp.dma_start(dst, src).then_inc(w_loaded, 16)

        def load_down(sp, e, par):
            sp.dma_start(w_dn[par][:, :, :], w2_t[e, :, :].rearrange("(j p) n -> p j n", p=128)).then_inc(w_loaded, 16)

        def load_rows(sp, n, par, pair):
            wait(sp, y_weighted, n - 1)
            wait(sp, z_made, n - 1)
            sp.dma_start(xr[par][:, :, :], rows_n[n, :, :, :]).then_inc(rows_loaded[par], 16)

        def round_expert(act, e, par):
            act.wait_ge(w_loaded, 112 * (e + 1))
            wait(act, down, TILES * (e - 1))
            for c in range(2):
                ins = nc.scalar.activation(w_hi[par][:, c, :], w_raw[:, c, :], ACT.Copy, scale=nw[:, c:c + 1])
            ins.then_inc(w_rounded, 1)

        def split_expert(dve, e, par):
            dve.wait_ge(w_rounded, e + 1)
            for c in range(2):
                ins = nc.vector.scalar_tensor_tensor(out=w_lo[par][:, c, :], in0=w_raw[:, c, :], scalar=nw[:, c:c + 1],
                                                     in1=w_hi[par][:, c, :].bitcast(fp32), op0=ALU.mult, op1=ALU.subtract)
            ins.then_inc(w_split, 1)

        def square_rows(act, n, par, pair):
            act.wait_ge(rows_loaded[par], 16 * (pair + 1))
            wait(act, rms_sum, n)
            for s in range(SUB):
                ins = nc.scalar.activation(sq[:, s, :], xr[par][:, s, 0:D], ACT.Square, accum_out=ssum[:, s:s + 1])
            ins.then_inc(squared, 1)

        def make_z(dve, n, par):
            dve.wait_ge(squared, n + 1)
            nc.vector.tensor_scalar(rms[:, :], ssum[:, :], 1.0 / D, RMS_EPS / 4.0, ALU.mult, ALU.add).then_inc(rms_sum, 1)
            dve.wait_ge(rms_made, n + 1)
            wait(dve, zb_turned, n)
            for s in range(SUB):
                ins = nc.vector.tensor_scalar(z[:, s, 0:D], xr[par][:, s, 0:D], rms2[:, s:s + 1], None, ALU.mult)
            ins.then_inc(z_scaled, 1)
            dve.wait_ge(z_scaled, n + 1)
            nc.vector.tensor_copy(z[:, :, D:256], z[:, :, 128:D]).then_inc(z_made, 1)

        def turn_z(pe, n):
            pe.wait_ge(z_made, n + 1)
            wait(pe, za_split, n)
            wait(pe, zb_split, n)
            for s in range(SUB):
                ins = nc.tensor.transpose(bank[4][:, TT * s:TT * (s + 1)], z[:, s, 0:128], ident[0:TT, 0:TT])
            ins.then_inc(za_turned, 1)
            for s in range(SUB):
                ins = nc.tensor.transpose(bank[5][:, TT * s:TT * (s + 1)], z[:, s, 128:256], ident[0:TT, 0:TT])
            ins.then_inc(zb_turned, 1)

        def round_z(act, n):
            act.wait_ge(za_turned, n + 1)
            nc.scalar.activation(za_hi[:, :], bank[4][:, 0:ROWS], ACT.Copy).then_inc(za_rounded, 1)
            act.wait_ge(zb_turned, n + 1)
            nc.scalar.activation(zb_hi[:, :], bank[5][:, 0:ROWS], ACT.Copy).then_inc(zb_rounded, 1)

        def split_z(dve, n):
            dve.wait_ge(za_rounded, n + 1)
            nc.vector.tensor_tensor(za_lo[:, :], bank[4][:, 0:ROWS], za_hi[:, :].bitcast(fp32), ALU.subtract).then_inc(za_split, 1)
            dve.wait_ge(zb_rounded, n + 1)
            nc.vector.tensor_copy(zb[0:64, :], zb_hi[0:64, :].bitcast(fp32))
            nc.vector.tensor_tensor(zb[64:128, :], bank[5][64:128, 0:ROWS], zb_hi[64:128, :].bitcast(fp32),
                                    ALU.subtract).then_inc(zb_split, 1)

        def expert_up(pe, n, e_par, j):
            if j == 0:
                pe.wait_ge(za_split, n + 1)
                pe.wait_ge(zb_split, n + 1)
            if j >= 2:
                pe.wait_ge(hid_made[j - 2], n + 1)
            else:
                wait(pe, hid_made[j + 2], n)
            hi, lo = w_hi[e_par], w_lo[e_par]
            for side in range(2):
                dst = bank[2 * (j % 2) + side][:, 0:ROWS]
                col = slice(HID * side + 128 * j, HID * side + 128 * (j + 1))
                nc.tensor.matmul(dst, hi[:, 0, col], za_hi[:, :], start=True, stop=False)
                nc.tensor.matmul(dst, hi[:, 0, col], za_lo[:, :], start=False, stop=False)
                nc.tensor.matmul(dst, lo[:, 0, col], za_hi[:, :], start=False, stop=False)
                nc.tensor.matmul(dst, hi[:, 1, col], zb[:, :], start=False, stop=False)
                ins = nc.tensor.matmul(dst, lo[:, 1, col], zb[:, :], start=False, stop=True)
            ins.then_inc(gate_up[j], 1)

        def silu(act, n, j):
            act.wait_ge(gate_up[j], n + 1)
            if j >= 2:
                act.wait_ge(hid_made[j - 2], n + 1)
            else:
                wait(act, hid_made[j + 2], n)
            nc.scalar.activation(act_g[:, j % 2, :], bank[2 * (j % 2)][:, 0:ROWS], ACT.Silu).then_inc(silued, 1)

        def make_hid(dve, n, j):
            dve.wait_ge(silued, 4 * n + j + 1)
            if j == 0:
                wait(dve, down, n)
            nc.vector.tensor_tensor(hid[:, j, :], bank[2 * (j % 2) + 1][:, 0:ROWS], act_g[:, j % 2, :], ALU.mult).then_inc(hid_made[j], 1)

        def expert_down(pe, n, e_par):
            wait(pe, y_added, n)
            for j in range(4):
                pe.wait_ge(hid_made[j], n + 1)
                for s in range(SUB):
                    ins = nc.tensor.matmul(bank[6 + s // 2][0:TT, D * (s % 2):D * (s % 2 + 1)], hid[:, j, TT * s:TT * (s + 1)],
                                           w_dn[e_par][:, j, :], start=(j == 0 and s % 2 == 0), stop=(j == 3),
                                           skip_group_check=True)
            ins.then_inc(down, 1)

        def weigh_rows(dve, n, par, pair, e):
            dve.wait_ge(down, n + 1)
            wait(dve, added[par], 16 * SUB * pair)
            for s in range(0, SUB, 2):
                ins = nc.vector.tensor_tensor(y[:, s:s + 2, :], bank[6 + s // 2][0:TT, 0:2 * D].rearrange("p (s n) -> p s n", s=2),
                                              xr[par][:, s:s + 2, 0:D], ALU.add)
            nc.vector.tensor_copy(w_slot[:, :].unsqueeze(2), xr[par][:, :, bass.ds(COL_W + e, 1)])
            nc.vector.tensor_copy(who[par][:, :].unsqueeze(2), xr[par][:, :, COL_ID:COL_ID + 1].bitcast(u32)).then_inc(y_added, 1)
            dve.wait_ge(y_added, n + 1)
            for s in range(SUB):
                ins = nc.vector.tensor_scalar(ys[par][:, s, :], y[:, s, :], w_slot[:, s:s + 1], None, ALU.mult)
            ins.then_inc(y_weighted, 1)

        def inverse_rms(pool, n):
            pool.wait_ge(rms_sum, n + 1)
            nc.gpsimd.tensor_tensor(rms2[:, :], rms[:, :], minus_half[:, 0:SUB], ALU.pow).then_inc(rms_made, 1)

        def add_rows(pool, n, par, pair):
            pool.wait_ge(y_weighted, n + 1)
            if par:
                hold(pool, added[0], 16 * SUB * (pair + 1), held)
            else:
                hold(pool, added[1], 16 * SUB * pair, held)
            for s in range(SUB):
                nc.gpsimd.indirect_dma_start(
                    out=out[:, :], out_offset=bass.IndirectOffsetOnAxis(ap=who[par][:, s:s + 1], axis=0),
                    in_=ys[par][:, s, :], in_offset=None, bounds_check=TOKENS + ROWS - 1, oob_is_err=True,
                    compute_op=ALU.add).then_inc(added[par], 16)

        PT = TILES // 2

        def over_tiles(eng, tile, between=None):
            with eng.Fori(0, E // 2) as e2:
                for e_par in range(2):
                    e = 2 * e2 + e_par

                    def pair_of(k):
                        pair = e * PT + k
                        for par in range(2):
                            tile(2 * pair + par, e, e_par, par, pair)

                    pair_of(0)
                    if between:
                        between(e + 1, 1 - e_par)
                    with eng.Fori(1, PT) as k:
                        pair_of(k)

        def ahead(n, par, pair):
            return n + 1, 1 - par, pair + par

        block = ctx.enter_context(nc.Block())

        @block.sync
        def _(sp):
            setup_sync(sp)
            pass1_sync(sp)
            sp.wait_ge(x_pooled, B)
            sp.wait_ge(attended[2], B)
            load_expert(sp, 0)
            load_down(sp, 0, 0)
            for par in range(2):
                sp.wait_ge(scattered[par], 64 * (B // 2))
            load_rows(sp, 0, 0, 0)

            def tile(n, e, e_par, par, pair):
                n1, par1, pair1 = ahead(n, par, pair)
                sp.wait_ge(z_made, n)
                sp.wait_ge(y_weighted, n)
                sp.dma_start(xr[par1][:, :, :], rows_n[n1, :, :, :]).then_inc(rows_loaded[par1], 16)

            def between(e, par):
                hold(sp, w_split, e, held)
                hold(sp, down, TILES * (e - 1), held)
                for dst, src in ((w_raw[:, 0, :], w13_t[e, 0:128, :]), (w_raw[0:64, 1, :], w13_t[e, 128:D, :]),
                                 (w_raw[64:128, 1, :], w13_t[e, 128:D, :]),
                                 (nw[:, 0:1], norm_w_t[e, 0:128, :]), (nw[0:64, 1:2], norm_w_t[e, 128:D, :]),
                                 (nw[64:128, 1:2], norm_w_t[e, 128:D, :]),
                                 (w_dn[par][:, :, :], w2_t[e, :, :].rearrange("(j p) n -> p j n", p=128))):
                    sp.dma_start(dst, src).then_inc(w_loaded, 16)

            over_tiles(sp, tile, between)

        @block.gpsimd
        def _(pool):
            pool.wait_ge(prepared, 1)
            pass1_gpsimd(pool)
            for par in range(2):
                pool.wait_ge(h2_stored[par], 16 * (B // 2))
            pool.wait_ge(spare_set, 32)
            inverse_rms(pool, 0)

            def tile(n, e, e_par, par, pair):
                inverse_rms(pool, n + 1)
                add_rows(pool, n, par, pair)

            over_tiles(pool, tile)
            for par in range(2):
                pool.wait_ge(added[par], 16 * SUB * E * PT)

        @block.vector
        def _(dve):
            setup_vector(dve)
            steps(dve, step_vector)
            split_expert(dve, 0, 0)
            make_z(dve, 0, 0)
            split_z(dve, 0)

            def tile(n, e, e_par, par, pair):
                n1, par1, pair1 = ahead(n, par, pair)
                make_hid(dve, n, 0)
                make_hid(dve, n, 1)
                make_z(dve, n1, par1)
                make_hid(dve, n, 2)
                make_hid(dve, n, 3)
                split_z(dve, n1)
                weigh_rows(dve, n, par, pair, e)

            over_tiles(dve, tile, lambda e, par: split_expert(dve, e, par))

        @block.scalar
        def _(act):
            act.wait_ge(prepared, 1)
            steps(act, step_scalar)
            round_expert(act, 0, 0)
            square_rows(act, 0, 0, 0)
            round_z(act, 0)

            def tile(n, e, e_par, par, pair):
                n1, par1, pair1 = ahead(n, par, pair)
                silu(act, n, 0)
                silu(act, n, 1)
                square_rows(act, n1, par1, pair1)
                silu(act, n, 2)
                silu(act, n, 3)
                round_z(act, n1)

            over_tiles(act, tile, lambda e, par: round_expert(act, e, par))

        @block.tensor
        def _(pe):
            setup_tensor(pe)
            steps(pe, step_tensor)
            pe.wait_ge(w_split, 1)
            turn_z(pe, 0)

            def tile(n, e, e_par, par, pair):
                if par == 0:
                    pe.wait_ge(w_split, e + 1)
                for j in range(4):
                    expert_up(pe, n, e_par, j)
                turn_z(pe, n + 1)
                expert_down(pe, n, e_par)

            over_tiles(pe, tile)


def kernel(**inputs):
    import concourse.bacc as bacc
    from concourse.bass_utils import run_bass_kernel_spmd

    def host(name):
        return np.asarray(inputs[name])

    batches = host("x").shape[0]
    tokens = batches * T
    head = np.concatenate([np.arange(0, HD, 2), np.arange(1, HD, 2)])
    cols = np.concatenate([np.arange(2 * HEADS)[:, None] * HD + head, 2 * D + np.arange(D).reshape(HEADS, HD)]).reshape(-1)
    wrap = list(range(E)) + [0]
    arrays = {
        "x": host("x"), "txt": host("txt"), "chan_w": host("L0_tok_channel_weights"),
        "norm_scale": host("L0_attn_norm_scale"), "norm_bias": host("L0_attn_norm_bias"),
        "w_attn": host("L0_attn_W_attn")[:, cols], "b_attn": host("L0_attn_b_attn")[cols],
        "w_proj": host("L0_attn_W_proj"), "b_proj": host("L0_attn_b_proj"),
        "sinks": host("L0_attn_sinks"), "rezero": host("L0_attn_rezero"),
        "gate_t": host("L0_ffn_gate_w").T,
        "w13_t": host("L0_ffn_w13").transpose(0, 2, 1)[wrap],
        "w2_t": host("L0_ffn_w2").transpose(0, 2, 1)[wrap],
        "norm_w_t": host("L0_ffn_norm_w")[wrap][:, :, None],
    }
    fixed = constants(tokens)
    nc = bacc.Bacc("TRN2", target_bir_lowering=False, num_devices=1)
    feeds, aps = {}, {}
    for name, a in list(arrays.items()) + [("const_" + k, v) for k, v in fixed.items()]:
        a = np.ascontiguousarray(a)
        feeds[f"in_{name}"] = a
        aps[name] = nc.dram_tensor(f"in_{name}", a.shape, mybir.dt.from_np(a.dtype), kind="ExternalInput").ap()
    out = nc.dram_tensor("out", [tokens + ROWS, D], mybir.dt.float32, kind="ExternalOutput").ap()
    build(nc, *[aps[name] for name in arrays], {k: aps["const_" + k] for k in fixed}, out)
    r = run_bass_kernel_spmd(nc, [feeds], core_ids=[0])
    return r.results[0]["out"][:tokens].reshape(batches, T, D)
```

```python
import math
from contextlib import ExitStack

import numpy as np
import concourse.bass as bass
from concourse import mybir

IMG, PATCH, CH = 224, 16, 12
SIDE = IMG // PATCH
HALF = PATCH // 2
GRP = 4
NG = CH // GRP
XP = GRP * SIDE * 2
XF = HALF * IMG
D = 192
HEADS, HD = 12, 16
PAIRS = HEADS // 2
TXT = 32
T = SIDE * SIDE + TXT
TT = T // 2
IMG1 = SIDE * SIDE - TT
C = D // 2
C1 = C + 1
E, TOPK, HID = 8, 2, 512
NEG = -1e30
FAR = 1 << 20
RW = 204
COL_W, COL_ID = D, D + E
LN_EPS, RMS_EPS = 1e-5, 1e-6
SUB = 4
ROWS = TT * SUB


def capacity(tokens):
    return int(math.ceil(1.25 * TOPK * tokens / E))


def constants(tokens):
    cap = capacity(tokens)
    f = np.float32
    freqs = f(1.0) / f(10000.0) ** (np.arange(0, HD, 2, dtype=f) / f(HD))
    ang = np.outer(np.arange(T, dtype=f), freqs.astype(f)).astype(f)
    cos = np.cos(ang).astype(f).reshape(2, TT, HD // 2).transpose(1, 0, 2)
    sin = np.sin(ang).astype(f).reshape(2, TT, HD // 2).transpose(1, 0, 2)
    p = np.arange(128)
    q = np.arange(TT)
    later = np.where(q[None, :] > q[:, None], f(NEG), f(0))
    mask_q1 = np.zeros((TT, 2, 2, TT), f)
    mask_q1[:, :, 1, :] = later[:, None, :]
    sel = np.zeros((128, HEADS, TT + 1), f)
    for h in range(HEADS):
        sel[h, h] = 1
        sel[HEADS + h, h] = 1
    term = (p // HD) % 4
    split = np.zeros((128, 4), f)
    split[:, 0] = np.where(term % 2 == 1, -1, 0)
    split[:, 1] = np.where(term >= 2, -1, 0)
    split[HEADS:2 * HEADS, 2] = -1
    split[2 * HEADS + 1, 3] = -1
    small = np.zeros((128, 2 * E + 2), f)
    small[:, 0:E] = np.arange(E) * cap
    small[:, E:2 * E] = np.arange(E)
    small[:, 2 * E] = p
    small[:, 2 * E + 1] = p + TT
    filler = np.zeros((TT, 2, 2, RW), np.uint32)
    for par in range(2):
        for s in range(2):
            filler[:, par, s, COL_ID] = tokens + (par * T + 2 * q + s) % ROWS
    rows = np.arange(XP)
    return {
        "cos": np.ascontiguousarray(cos),
        "sin": np.ascontiguousarray(np.concatenate([sin, -sin], -1)),
        "ident": np.eye(128, dtype=f),
        "mask_q0": np.ascontiguousarray(np.repeat(later[:, None], 4, 1)),
        "mask_q1": mask_q1.reshape(TT, 2, T),
        "mask_k": np.ascontiguousarray(np.repeat(later.T[:, None], 4, 1)),
        "sel": sel,
        "split": split,
        "small": small,
        "before": (q[:, None] < q[None, :]).astype(f),
        "patch": ((rows[:, None] // 2) % SIDE == np.arange(SIDE)[None]).astype(f),
        "filler": filler,
    }


CONST_NAMES = ["cos", "sin", "ident", "mask_q0", "mask_q1", "mask_k", "sel", "split", "small",
               "before", "patch", "filler"]


class Batch:

    def __init__(self, half, par, lag=0):
        self.par = (par - lag) % 2
        self.half = half + (par - lag) // 2
        self.b = 2 * half + (par - lag)

    def ago(self, n):
        return Batch(self.half, self.par, n)


def wait(eng, sem, value):
    if not (isinstance(value, int) and value <= 0):
        eng.wait_ge(sem, value)


def hold(eng, sem, value, held):
    if not (isinstance(value, int) and value <= 0):
        eng.wait_ge(sem, value)
        eng.sem_inc(held, 1)


def build(nc, x, txt, chan_w, norm_scale, norm_bias, w_attn, b_attn, w_proj, b_proj, sinks,
          rezero, gate_t, w13_t, w2_t, norm_w_t, const, out):
    fp32, fp32r, bf16 = mybir.dt.float32, mybir.dt.float32r, mybir.dt.bfloat16
    u32 = mybir.dt.uint32
    ALU, ACT, AX = mybir.AluOpType, mybir.ActivationFunctionType, mybir.AxisListType

    B = x.shape[0]
    TOKENS = B * T
    CAP = capacity(TOKENS)
    SLOTS = E * CAP
    FILLS = CAP // T
    TILES = CAP // ROWS
    assert FILLS * T == CAP and TILES * ROWS == CAP and TILES % 2 == 0 and B % 2 == 0
    assert CAP % (2 * T) == 0

    moe_rows = nc.dram_tensor("moe_rows", [SLOTS + 2 * ROWS, RW], fp32).ap()

    ctx = ExitStack()
    with ctx:
        def sb(name, shape, dt=fp32):
            return ctx.enter_context(nc.sbuf_tensor(name, shape, dt))

        def sem(name):
            return ctx.enter_context(nc.semaphore(name))

        bank = [ctx.enter_context(nc.psum_tensor(f"bank{i}", [128, 512], fp32)) for i in range(8)]

        cos = sb("cos", [TT, 2, 8])
        sin = sb("sin", [TT, 2, 16])
        ident = sb("ident", [128, 128])
        ident_r = sb("ident_r", [128, 128], fp32r)
        mask_q0 = sb("mask_q0", [TT, 4, TT], fp32r)
        mask_q1 = sb("mask_q1", [TT, 2, T], fp32r)
        mask_k = sb("mask_k", [TT, 4, TT], fp32r)
        sel = sb("sel", [128, HEADS, TT + 1], fp32r)
        split = sb("split", [128, 4])
        small = sb("small", [128, 2 * E + 2])
        minus_half = sb("minus_half", [TT, 4])
        before = sb("before", [TT, TT], bf16)
        ones = sb("ones", [TT, TT], bf16)
        patch = sb("patch", [XP, SIDE])
        filler = sb("filler", [TT, 2, 2, RW], u32)
        chan = sb("chan", [XP, NG, D])
        scale_col = sb("scale_col", [C, 2])
        bias_col = sb("bias_col", [C, 2])
        w_qkv = sb("w_qkv", [C1, 2, 3 * D])
        b_row = sb("b_row", [1, 3 * D])
        b_fold = sb("b_fold", [1, 3 * D])
        w_out = sb("w_out", [C1, 2, D])
        rez = sb("rez", [C1, 1])
        sink_tok = sb("sink_tok", [TT, HEADS])
        sink_key = sb("sink_key", [128, HEADS])
        sink_hi = sb("sink_hi", [128, HEADS], fp32r)
        sink_ones = sb("sink_ones", [128, HEADS])
        gate = sb("gate", [C, 2, E])

        arena = sb("arena", [128, 2 * NG * XF])
        xin = [arena[0:XP, NG * XF * i:NG * XF * (i + 1)].rearrange("p (g f) -> p g f", g=NG) for i in range(2)]
        pooled = [sb(f"pooled{i}", [XP, NG, SIDE]) for i in range(2)]
        spread = sb("spread", [XP, NG, SIDE * SIDE])
        h = [sb(f"h{i}", [TT, 2, D]) for i in range(2)]
        h_keep = sb("h_keep", [TT, 2, D])
        st1 = sb("st1", [TT, 2, 6])
        mv1 = sb("mv1", [TT, 2, 2])
        rstd1 = sb("rstd1", [TT, 2])
        var1 = sb("var1", [TT, 2])
        xn = sb("xn", [TT, 2, 2, C1])
        xn_t = sb("xn_t", [C1, 2, T])
        rot_c = sb("rot_c", [TT, 2, 2 * D])
        rot_s = sb("rot_s", [TT, 2, 2 * D])
        qk = sb("qk", [TT, 2, 2 * HEADS, 4, HD])
        val = [sb(f"val{i}", [TT + 1, 2, HEADS, 32]) for i in range(2)]
        rounded = [sb(f"rounded{i}", [128, 4 * TT], fp32r) for i in range(2)]
        q_t = sb("q_t", [128, HEADS, T], fp32r)
        k_t = sb("k_t", [128, PAIRS, 2, TT + 1], fp32r)
        top = sb("top", [TT, 2, HEADS])
        shift = sb("shift", [TT, 2, 128])
        shift_hi = sb("shift_hi", [128, T], fp32r)
        shift_t = sb("shift_t", [128, T], fp32r)
        prob = sb("prob", [128, HEADS * T])
        staging = prob[:, 0:HEADS * (TT + 1)]
        prob0 = prob[0:TT + 1, :].rearrange("p (a n) -> p a n", a=HEADS)
        prob1 = sb("prob1", [TT, HEADS, TT])
        y_t = sb("y_t", [128, 3, T])
        rden = sb("rden", [TT, 2, HEADS])
        yn = sb("yn", [TT, 2, 2, C1])
        yn_t = sb("yn_t", [C1, 2, T])
        h2 = [sb(f"h2_{i}", [TT, 2, D]) for i in range(2)]
        st2 = sb("st2", [TT, 2, 6])
        mv2 = sb("mv2", [TT, 2, 2])
        rstd2 = sb("rstd2", [TT, 2])
        var2 = sb("var2", [TT, 2])
        row = [sb(f"row{i}", [TT, 2, RW]) for i in range(2)]
        xf_t = sb("xf_t", [C, 2, T])
        best = sb("best", [TT, 2, 8])
        best_i = sb("best_i", [TT, 2, 8], u32)
        best_f = sb("best_f", [TT, 2, 2])
        gap = sb("gap", [TT, 2])
        gexp = sb("gexp", [TT, 2])
        gden = sb("gden", [TT, 2])
        gw = sb("gw", [TT, 2, 2])
        hot = sb("hot", [TT, 2, 2, E])
        hot_sum = sb("hot_sum", [TT, 2, E], bf16)
        seen = sb("seen", [TT, E], bf16)
        over = sb("over", [TT, 2, E])
        place = sb("place", [TT, 2, E])
        pick = sb("pick", [TT, 2, 2, E])
        wpick = sb("wpick", [TT, 2, 2, E])
        slot_f = sb("slot_f", [TT, 4])
        slot = [sb(f"slot{i}", [TT, 4], u32) for i in range(2)]
        token = sb("token", [TT, 2])

        taken = 0

        def view(parts, a, b):
            nonlocal taken
            taken += a * b
            assert taken <= 2 * NG * XF
            return arena[0:parts, taken - a * b:taken].rearrange("p (a b) -> p a b", a=a)

        w_raw = view(128, 2, 2 * HID)
        xr = [view(TT, SUB, RW) for _ in range(2)]
        z = view(TT, SUB, 256)
        act_g = view(128, 2, ROWS)
        hid = view(128, 4, ROWS)
        xw = view(TT, SUB, D)
        ys = [view(TT, SUB, D) for _ in range(2)]
        nw = sb("nw", [128, 2])
        w_hi = [sb(f"w_hi{i}", [128, 2, 2 * HID], fp32r) for i in range(2)]
        w_lo = [sb(f"w_lo{i}", [128, 2, 2 * HID], fp32r) for i in range(2)]
        w_dn = [prob[:, 4 * D * i:4 * D * (i + 1)].rearrange("p (j n) -> p j n", j=4) for i in range(2)]
        sq = prob[0:TT, 8 * D:(8 + SUB) * D].rearrange("p (s n) -> p s n", s=SUB)
        ssum = sb("ssum", [TT, SUB])
        rms = sb("rms", [TT, SUB])
        rms2 = sb("rms2", [TT, SUB])
        za_hi = sb("za_hi", [128, ROWS], fp32r)
        za_lo = sb("za_lo", [128, ROWS], fp32r)
        zb_hi = sb("zb_hi", [128, ROWS], fp32r)
        zb = sb("zb", [128, ROWS], fp32r)
        w_slot = [sb(f"w_slot{i}", [TT, SUB]) for i in range(2)]
        who = [sb(f"who{i}", [TT, SUB], u32) for i in range(2)]

        loaded = sem("loaded")
        staged = sem("staged")
        unstaged = sem("unstaged")
        cleared = sem("cleared")
        prepared = sem("prepared")
        fold_done = sem("fold_done")
        folded = sem("folded")
        bias_placed = sem("bias_placed")
        held = sem("held")
        step0 = sem("step0")

        x_loaded = [sem(f"x_loaded{i}") for i in range(2)]
        txt_loaded = [sem(f"txt_loaded{i}") for i in range(2)]
        filled = [sem(f"filled{i}") for i in range(2)]
        h2_stored = [sem(f"h2_stored{i}") for i in range(2)]
        scattered = [sem(f"scattered{i}") for i in range(2)]
        spare_set = sem("spare_set")
        x_pooled = sem("x_pooled")
        x_spread = sem("x_spread")
        h_summed = sem("h_summed")
        h_copied = sem("h_copied")
        h_kept = sem("h_kept")
        ln1_step, ln1_done = sem("ln1_step"), sem("ln1_done")
        xn_turned, xn_ready = sem("xn_turned"), sem("xn_ready")
        qk_made = [sem(f"qk_made{t}") for t in range(2)]
        v_made, v_ready = sem("v_made"), sem("v_ready")
        qk_read = [sem(f"qk_read{t}") for t in range(2)]
        qk_rotated = [sem(f"qk_rotated{t}") for t in range(2)]
        qk_turned = [sem(f"qk_turned{k}") for k in range(6)]
        qk_rounded = sem("qk_rounded")
        qk_split = [sem(f"qk_split{k}") for k in range(6)]
        scored = [sem(f"scored{k}") for k in range(9)]
        maxed = [sem(f"maxed{k}") for k in range(9)]
        top_sink, shift_made = sem("top_sink"), sem("shift_made")
        shift_turned, shift_rounded, shift_ready = (sem(n) for n in ("shift_turned", "shift_rounded", "shift_ready"))
        scored_t = [sem(f"scored_t{k}") for k in range(9)]
        probed = [sem(f"probed{k}") for k in range(9)]
        attended = [sem(f"attended{g}") for g in range(3)]
        y_copied = sem("y_copied")
        y_turned = [sem(f"y_turned{t}") for t in range(2)]
        den_ready = sem("den_ready")
        y_normed = sem("y_normed")
        yn_turned, yn_ready = sem("yn_turned"), sem("yn_ready")
        projected, h2_made = sem("projected"), sem("h2_made")
        ln2_step, ln2_done = sem("ln2_step"), sem("ln2_done")
        xf_turned, xf_ready = sem("xf_turned"), sem("xf_ready")
        gated, ranked, gaps_made, gate_exp = (sem(n) for n in ("gated", "ranked", "gaps_made", "gate_exp"))
        indexed = sem("indexed")
        hots_summed, ranks_made = sem("hots_summed"), sem("ranks_made")
        route_step = sem("route_step")
        weights_made, row_whole, ranks_read = sem("weights_made"), sem("row_whole"), sem("ranks_read")
        seen_counted = sem("seen_counted")
        routed = sem("routed")

        w_loaded = sem("w_loaded")
        w_rounded = sem("w_rounded")
        w_split = sem("w_split")
        rows_loaded = [sem(f"rows_loaded{i}") for i in range(2)]
        squared, rms_sum, rms_made, z_scaled, z_made = (sem(n) for n in ("squared", "rms_sum", "rms_made", "z_scaled", "z_made"))
        za_turned, zb_turned = sem("za_turned"), sem("zb_turned")
        za_rounded, zb_rounded = sem("za_rounded"), sem("zb_rounded")
        za_split, zb_split = sem("za_split"), sem("zb_split")
        gate_up = [sem(f"gate_up{j}") for j in range(4)]
        silued = sem("silued")
        hid_made = [sem(f"hid_made{j}") for j in range(4)]
        down = sem("down")
        numbered, x_weighted, y_weighted = sem("numbered"), sem("x_weighted"), sem("y_weighted")
        added = [sem(f"added{i}") for i in range(2)]

        N_SMALL = 21
        MASKS = 5

        def setup_sync(sp):
            for dst, src in (
                (cos[:, :, :], const["cos"]), (sin[:, :, :], const["sin"]), (ident[:, :], const["ident"]),
                (split[:, :], const["split"]), (small[:, :], const["small"]),
                (patch[:, :], const["patch"]), (filler[:, :, :, :], const["filler"]),
                (scale_col[:, :], norm_scale.rearrange("(c p) -> p c", p=C)),
                (bias_col[:, :], norm_bias.rearrange("(c p) -> p c", p=C)),
                (w_qkv[0:C, :, :], w_attn.rearrange("(c p) n -> p c n", p=C)),
                (b_row[:, :], b_attn.rearrange("(a n) -> a n", a=1)),
                (rez[:, :], rezero.rearrange("(a n) -> a n", a=1).to_broadcast([C1, 1])),
                (sink_tok[:, :], sinks.rearrange("(a n) -> a n", a=1).to_broadcast([TT, HEADS])),
                (gate[:, :, :], gate_t.rearrange("(c p) n -> p c n", p=C)),
            ):
                with nc.allow_non_contiguous_dma(reason="columns of a few vectors"):
                    sp.dma_start(dst, src).then_inc(loaded, 16)
            for g in range(NG):
                sp.dma_start(chan[:, g, :], chan_w[GRP * g:GRP * (g + 1), :].unsqueeze(1)
                             .to_broadcast([GRP, SIDE * 2, D])).then_inc(loaded, 16)
            sp.wait_ge(cleared, 1)
            sp.dma_start(w_out[0:C, :, :], w_proj.rearrange("(c p) n -> p c n", p=C)).then_inc(loaded, 16)
            sp.dma_start(w_out[C:C1, 1, :], b_proj.rearrange("(a n) -> a n", a=1)).then_inc(loaded, 16)
            for r in range(2):
                sp.dma_start(sink_key[2 * HEADS + r:2 * HEADS + r + 1, :],
                             sinks.rearrange("(a n) -> a n", a=1)).then_inc(loaded, 16)
            for n, (name, parts, width) in enumerate((("mask_q0", TT, 4 * TT), ("mask_q1", TT, 2 * T),
                                                      ("mask_k", TT, 4 * TT), ("sel", 128, HEADS * (TT + 1)),
                                                      ("before", TT, TT))):
                wait(sp, unstaged, n)
                src = const[name]
                if len(src.shape) == 3:
                    src = src.rearrange("p a b -> p (a b)")
                sp.dma_start(staging[0:parts, 0:width], src).then_inc(staged, 16)
            sp.wait_ge(loaded, 16 * N_SMALL)
            sp.dma_start(out[TOKENS:TOKENS + ROWS, :].rearrange("(p s) n -> p s n", s=SUB),
                         filler[:, 0, 0, 0:D].bitcast(fp32).unsqueeze(1).to_broadcast([TT, SUB, D])
                         ).then_inc(spare_set, 16)
            sp.dma_start(moe_rows[SLOTS:SLOTS + 2 * ROWS, :].rearrange("(a p s) n -> p a (s n)", p=TT, s=2),
                         filler[:, 0, :, :].bitcast(fp32).rearrange("p s n -> p (s n)").unsqueeze(1)
                         .to_broadcast([TT, 2 * ROWS // T, 2 * RW])).then_inc(spare_set, 16)
            sp.wait_ge(folded, 1)
            sp.dma_start(w_qkv[C:C1, 1, :], b_fold[:, :]).then_inc(bias_placed, 16)

        x_img = x.rearrange("b (g c) (q r) w -> b (c q) g (r w)", g=NG, r=HALF)
        out_b = out[0:TOKENS, :].rearrange("(b t p) n -> b p t n", t=2, p=TT)
        rows_e = moe_rows[0:SLOTS, :].rearrange("(e f p s) n -> f p e (s n)", e=E, p=TT, s=2)

        def load_image(sp, at):
            wait(sp, x_pooled, NG * (at.b - 1))
            sp.dma_start(xin[at.par][:, :, :], x_img[at.b, :, :, :]).then_inc(x_loaded[at.par], 16)

        def load_text(sp, at):
            wait(sp, ln1_done, at.b - 1)
            wait(sp, h_kept, at.b - 1)
            sp.dma_start(h[at.par][IMG1:TT, 1, :], txt[at.b, :, :]).then_inc(txt_loaded[at.par], 16)

        def fill_slots(sp, at):
            wait(sp, filled[at.par], 16 * at.half)
            sp.dma_start(rows_e[at.b, :, :, :],
                         filler[:, at.par, :, :].bitcast(fp32).rearrange("p s n -> p (s n)")
                         .unsqueeze(1).to_broadcast([TT, E, 2 * RW])).then_inc(filled[at.par], 16)

        def store_h2(sp, at):
            sp.wait_ge(h2_made, at.b + 1)
            sp.dma_start(out_b[at.b, :, :, :], h2[at.par][:, :, :]).then_inc(h2_stored[at.par], 16)

        def setup_vector(dve):
            n = 0

            def done(ins):
                nonlocal n
                n += 1
                ins.then_inc(step0, 1)

            nc.vector.memset(sink_key[:, :], 0.0)
            nc.vector.memset(minus_half[:, :], -0.5)
            nc.vector.memset(w_out[:, :, :], 0.0).then_inc(cleared, 1)
            for tile in (w_qkv[C:C1, :, :], k_t[:, :, :, :].bitcast(fp32), q_t[:, :, :].bitcast(fp32),
                         shift[:, :, :], seen[:, :], val[0][:, :, :, :], val[1][:, :, :, :], row[0][:, :, :],
                         row[1][:, :, :]):
                nc.vector.memset(tile, 0.0)
            done(nc.vector.memset(ones[:, :], 1.0))
            dve.wait_ge(step0, n)
            for tile in (xn[:, :, :, C:C1], yn[:, :, :, C:C1], shift[:, :, 2 * HEADS:2 * HEADS + 2],
                         val[0][:, :, :, HD:HD + 1], val[1][:, :, :, HD:HD + 1]):
                nc.vector.memset(tile, 1.0)
            dve.wait_ge(loaded, 16 * N_SMALL)
            for k, (dst, parts, width) in enumerate((
                    (mask_q0[:, :, :], TT, 4 * TT), (mask_q1[:, :, :], TT, 2 * T), (mask_k[:, :, :], TT, 4 * TT),
                    (sel[:, :, :], 128, HEADS * (TT + 1)), (before[:, :], TT, TT))):
                dve.wait_ge(staged, 16 * (k + 1))
                src = staging[0:parts, 0:width]
                if len(dst.shape) == 3:
                    src = src.rearrange("p (a b) -> p a b", a=dst.shape[1])
                nc.vector.tensor_copy(dst, src).then_inc(unstaged, 1)
            nc.vector.tensor_copy(ident_r[:, :], ident[:, :])
            nc.vector.tensor_scalar(sink_tok[:, :], sink_tok[:, :], 4.0, None, ALU.mult)
            done(nc.vector.tensor_scalar(sink_ones[:, :], sink_key[:, :], 4.0, None, ALU.mult))
            nc.vector.tensor_copy(token[:, :], small[0:TT, 2 * E:2 * E + 2])
            dve.wait_ge(step0, n)
            done(nc.vector.tensor_copy(sink_hi[:, :], sink_ones[:, :]))
            dve.wait_ge(step0, n)
            done(nc.vector.scalar_tensor_tensor(out=sink_ones[:, :], in0=sink_hi[:, :].bitcast(fp32), scalar=split[:, 3:4],
                                                in1=sink_ones[:, :], op0=ALU.mult, op1=ALU.add))
            dve.wait_ge(step0, n)
            dve.wait_ge(unstaged, 4)
            sink_col = staging[:, 0:HEADS]
            dve.wait_ge(unstaged, 5)
            done(nc.vector.tensor_copy(sink_col, sel[:, :, TT:TT + 1].bitcast(fp32).rearrange("p a b -> p (a b)")))
            dve.wait_ge(step0, n)
            sink_at = sel[:, :, TT:TT + 1].rearrange("p a b -> p (a b)")
            done(nc.vector.tensor_tensor(sink_at, sink_ones[:, :], sink_col, ALU.add))
            dve.wait_ge(fold_done, 1)
            nc.vector.tensor_tensor(b_fold[:, 0:288], bank[0][0:1, 0:288], b_row[:, 0:288], ALU.add)
            nc.vector.tensor_tensor(b_fold[:, 288:576], bank[1][0:1, 0:288], b_row[:, 288:576],
                                    ALU.add).then_inc(folded, 1)
            for c in range(2):
                nc.vector.tensor_scalar(w_qkv[0:C, c, :], w_qkv[0:C, c, :], scale_col[:, c:c + 1], None, ALU.mult)
            nc.vector.tensor_scalar(w_out[:, :, :], w_out[:, :, :], rez[:, 0:1], None,
                                    ALU.mult).then_inc(prepared, 1)
            dve.wait_ge(prepared, 1)
            dve.wait_ge(step0, n)

        def setup_tensor(pe):
            pe.wait_ge(loaded, 16 * N_SMALL)
            for half in range(2):
                for c in range(2):
                    last = nc.tensor.matmul(bank[half][0:1, 0:288], bias_col[:, c:c + 1],
                                            w_qkv[0:C, c, 288 * half:288 * (half + 1)],
                                            start=(c == 0), stop=(c == 1))
            last.then_inc(fold_done, 1)
            pe.wait_ge(prepared, 1)
            pe.wait_ge(bias_placed, 16)

        TURNS = (0, 3, 1, 4, 2, 5)
        def pool_image(dve, at, g):
            if g == 0:
                dve.wait_ge(x_loaded[at.par], 16 * (at.half + 1))
                wait(dve, x_spread, at.b - 1)
            ins = nc.vector.tensor_reduce(
                pooled[at.par][:, g, :], xin[at.par][:, g, :].rearrange("p (r j c) -> p j r c", r=HALF, c=PATCH),
                AX.XY, ALU.add)
            ins.then_inc(x_pooled, 1)

        def norm1_stats(dve, at):
            n = at.b + 1
            dve.wait_ge(h_copied, n)
            dve.wait_ge(txt_loaded[at.par], 16 * (at.half + 1))
            for t in range(2):
                ins = nc.vector.bn_stats(st1[:, t, :], h[at.par][:, t, :])
            ins.then_inc(ln1_step, 1)
            hold(dve, ln1_step, 4 * at.b + 1, held)
            for t in range(2):
                ins = nc.vector.bn_aggr(mv1[:, t, :], st1[:, t, :])
            ins.then_inc(ln1_step, 1)
            dve.wait_ge(ln1_step, 4 * at.b + 2)
            nc.vector.tensor_scalar(var1[:, :], mv1[:, :, 1:2].rearrange("p a b -> p (a b)"), LN_EPS, None,
                                    ALU.add).then_inc(ln1_step, 1)

        def norm1_apply(dve, at):
            n = at.b + 1
            dve.wait_ge(ln1_step, 4 * n)
            wait(dve, xn_turned, n - 1)
            for t in range(2):
                ins = nc.vector.tensor_scalar(xn[:, t, :, 0:C], h[at.par][:, t, :].rearrange("p (c k) -> p c k", c=2),
                                              mv1[:, t, 0:1], rstd1[:, t:t + 1], ALU.subtract, ALU.mult)
            ins.then_inc(ln1_done, 1)

        def rotate(dve, at, t):
            n = at.b + 1
            dve.wait_ge(qk_made[t], n)
            wait(dve, qk_rotated[t], 2 * at.b)
            src = bank[6 + t][0:TT, 0:2 * D]
            nc.vector.tensor_tensor(rot_c[:, t, :].rearrange("p (a k) -> p a k", k=8), src.rearrange("p (a k) -> p a k", k=8),
                                    cos[:, t, :].unsqueeze(1).to_broadcast([TT, 48, 8]), ALU.mult)
            nc.vector.tensor_tensor(rot_s[:, t, :].rearrange("p (a k) -> p a k", k=16), src.rearrange("p (a k) -> p a k", k=16),
                                    sin[:, t, :].unsqueeze(1).to_broadcast([TT, 24, 16]), ALU.mult).then_inc(qk_read[t], 1)

        def split_qk(dve, at, r):
            dve.wait_ge(qk_rounded, 6 * at.b + r + 1)
            src, hi = bank[r % 4], rounded[r % 2]
            k = TURNS[r]
            if r == 0:
                wait(dve, scored_t[8], at.b)
            if k < 3:
                for side in range(2):
                    lo = slice(64 * side, 64 * side + 64)
                    dst = q_t[lo, :, :].rearrange("p (a s) n -> p a s n", s=2)[:, 2 * k:2 * k + 2, side, :]
                    ins = nc.vector.scalar_tensor_tensor(
                        out=dst, in0=hi[lo, :].bitcast(fp32).rearrange("p (a n) -> p a n", a=2), scalar=split[lo, 0:1],
                        in1=src[lo, 0:4 * TT].rearrange("p (a n) -> p a n", a=2), op0=ALU.mult, op1=ALU.add)
            else:
                kk = k - 3
                dst = k_t[:, 2 * kk:2 * kk + 2, :, 0:TT].rearrange("p a t n -> p (a t) n")
                ins = nc.vector.scalar_tensor_tensor(
                    out=dst, in0=hi[:, :].bitcast(fp32).rearrange("p (a n) -> p a n", a=4), scalar=split[:, 1:2],
                    in1=src[:, 0:4 * TT].rearrange("p (a n) -> p a n", a=4), op0=ALU.mult, op1=ALU.add)
            ins.then_inc(qk_split[r], 1)

        def max_scores(dve, at, k):
            n = at.b + 1
            dve.wait_ge(scored[k], n)
            if k == 0:
                wait(dve, shift_made, at.b)
            if k < 3:
                dst, src = top[:, 0, 4 * k:4 * k + 4], bank[(k + 2) % 4][0:TT, 0:4 * TT].rearrange("p (a n) -> p a n", a=4)
            else:
                kk = k - 3
                dst, src = top[:, 1, 2 * kk:2 * kk + 2], bank[(k + 2) % 4][0:TT, 0:2 * T].rearrange("p (a n) -> p a n", a=2)
            nc.vector.tensor_reduce(dst, src, AX.X, ALU.max).then_inc(maxed[k], 1)

        def make_shift(dve, at):
            n = at.b + 1
            dve.wait_ge(maxed[8], n)
            nc.vector.tensor_tensor(top[:, :, :], top[:, :, :], sink_tok[:, :].unsqueeze(1).to_broadcast([TT, 2, HEADS]),
                                    ALU.max).then_inc(top_sink, 1)
            dve.wait_ge(top_sink, n)
            wait(dve, shift_turned, at.b)
            for part in range(2):
                ins = nc.vector.tensor_scalar(shift[:, :, HEADS * part:HEADS * (part + 1)], top[:, :, :], -1.0, None, ALU.mult)
            ins.then_inc(shift_made, 1)

        def split_shift(dve, at):
            dve.wait_ge(shift_rounded, at.b + 1)
            nc.vector.scalar_tensor_tensor(out=shift_t[:, :], in0=shift_hi[:, :].bitcast(fp32), scalar=split[:, 2:3],
                                           in1=bank[5][:, 0:T], op0=ALU.mult, op1=ALU.add).then_inc(shift_ready, 1)

        def normalize(dve, at, t):
            n = at.b + 1
            dve.wait_ge(y_turned[t], n)
            src = bank[4 + t][0:TT, 0:3 * 128].rearrange("p (a k) -> p a k", k=32)
            nc.vector.reciprocal(rden[:, t, :], src[:, :, HD:HD + 1].rearrange("p a b -> p (a b)")).then_inc(den_ready, 1)
            dve.wait_ge(den_ready, 2 * at.b + t + 1)
            if t == 0:
                wait(dve, yn_turned, at.b)
            for c in range(2):
                ins = nc.vector.tensor_tensor(yn[:, t, c, 0:C].rearrange("p (a k) -> p a k", k=HD), src[:, 6 * c:6 * c + 6, 0:HD],
                                              rden[:, t, 6 * c:6 * c + 6].unsqueeze(2).to_broadcast([TT, 6, HD]), ALU.mult)
            ins.then_inc(y_normed, 1)

        def residual(dve, at):
            n = at.b + 1
            dve.wait_ge(projected, n)
            dve.wait_ge(h_kept, n)
            wait(dve, h2_stored[at.par], 16 * at.half)
            nc.vector.tensor_tensor(h2[at.par][:, :, :], bank[5][0:TT, 0:2 * D].rearrange("p (t n) -> p t n", t=2),
                                    h_keep[:, :, :], ALU.add).then_inc(h2_made, 1)

        def norm2_stats(dve, at):
            n = at.b + 1
            dve.wait_ge(h2_made, n)
            for t in range(2):
                ins = nc.vector.bn_stats(st2[:, t, :], h2[at.par][:, t, :])
            ins.then_inc(ln2_step, 1)
            hold(dve, ln2_step, 4 * at.b + 1, held)
            for t in range(2):
                ins = nc.vector.bn_aggr(mv2[:, t, :], st2[:, t, :])
            ins.then_inc(ln2_step, 1)
            dve.wait_ge(ln2_step, 4 * at.b + 2)
            nc.vector.tensor_scalar(var2[:, :], mv2[:, :, 1:2].rearrange("p a b -> p (a b)"), LN_EPS, None,
                                    ALU.add).then_inc(ln2_step, 1)

        def norm2_apply(dve, at):
            n = at.b + 1
            dve.wait_ge(ln2_step, 4 * n)
            wait(dve, scattered[at.par], 64 * at.half)
            for t in range(2):
                ins = nc.vector.tensor_scalar(row[at.par][:, t, 0:D], h2[at.par][:, t, :], mv2[:, t, 0:1], rstd2[:, t:t + 1],
                                              ALU.subtract, ALU.mult)
            ins.then_inc(ln2_done, 1)

        def choose(dve, at):
            n = at.b + 1
            hold(dve, gated, n, held)
            for t in range(2):
                ins = nc.vector.max(best[:, t, :], bank[5][0:TT, E * t:E * (t + 1)])
            ins.then_inc(ranked, 1)
            hold(dve, ranked, n, held)
            for t in range(2):
                ins = nc.vector.max_index(best_i[:, t, :], best[:, t, :], bank[5][0:TT, E * t:E * (t + 1)])
            ins.then_inc(indexed, 1)
            nc.vector.tensor_tensor(gap[:, :], best[:, :, 1:2].rearrange("p a b -> p (a b)"),
                                    best[:, :, 0:1].rearrange("p a b -> p (a b)"), ALU.subtract).then_inc(gaps_made, 1)
            dve.wait_ge(indexed, n)
            nc.vector.tensor_copy(best_f[:, :, :], best_i[:, :, 0:2]).then_inc(route_step, 1)
            dve.wait_ge(route_step, 8 * at.b + 1)
            nc.vector.tensor_tensor(hot[:, :, :, :].rearrange("p t k e -> p (t k) e"),
                                    small[0:TT, E:2 * E].unsqueeze(1).to_broadcast([TT, 4, E]),
                                    best_f[:, :, :].rearrange("p t k -> p (t k)").unsqueeze(2).to_broadcast([TT, 4, E]),
                                    ALU.is_equal).then_inc(route_step, 1)
            dve.wait_ge(route_step, 8 * at.b + 2)
            wait(dve, seen_counted, at.b)
            nc.vector.tensor_tensor(hot_sum[:, :, :], hot[:, :, 0, :], hot[:, :, 1, :], ALU.add).then_inc(hots_summed, 1)

        def weigh(dve, at):
            n = at.b + 1
            dve.wait_ge(gate_exp, n)
            nc.vector.tensor_scalar(gden[:, :], gexp[:, :], 1.0, None, ALU.add).then_inc(route_step, 1)
            dve.wait_ge(route_step, 8 * at.b + 3)
            nc.vector.reciprocal(gw[:, :, 0:1].rearrange("p a b -> p (a b)"), gden[:, :]).then_inc(route_step, 1)
            dve.wait_ge(route_step, 8 * at.b + 4)
            nc.vector.tensor_tensor(gw[:, :, 1:2].rearrange("p a b -> p (a b)"), gexp[:, :],
                                    gw[:, :, 0:1].rearrange("p a b -> p (a b)"), ALU.mult).then_inc(weights_made, 1)
            dve.wait_ge(weights_made, n)
            nc.vector.tensor_tensor(wpick[:, :, :, :].rearrange("p t k e -> p (t k) e"), hot[:, :, :, :].rearrange("p t k e -> p (t k) e"),
                                    gw[:, :, :].rearrange("p t k -> p (t k)").unsqueeze(2).to_broadcast([TT, 4, E]),
                                    ALU.mult).then_inc(route_step, 1)
            dve.wait_ge(route_step, 8 * at.b + 5)
            nc.vector.tensor_tensor(row[at.par][:, :, COL_W:COL_W + E], wpick[:, :, 0, :], wpick[:, :, 1, :], ALU.add)
            nc.vector.tensor_copy(row[at.par][:, :, COL_ID:COL_ID + 1].bitcast(u32).rearrange("p a b -> p (a b)"),
                                  token[:, :]).then_inc(row_whole, 1)
            dve.wait_ge(row_whole, n)
            nc.vector.tensor_scalar(token[:, :], token[:, :], float(T), None, ALU.add)

        def assign(dve, at):
            n = at.b + 1
            dve.wait_ge(ranks_made, n)
            ranks = bank[6][0:TT, 0:2 * E].rearrange("p (t e) -> p t e", t=2)
            nc.vector.tensor_scalar(over[:, :, :], ranks, float(CAP), float(FAR), ALU.is_ge, ALU.mult)
            nc.vector.tensor_tensor(place[:, :, :], ranks, small[0:TT, 0:E].unsqueeze(1).to_broadcast([TT, 2, E]),
                                    ALU.add).then_inc(route_step, 1)
            dve.wait_ge(route_step, 8 * at.b + 6)
            nc.vector.tensor_tensor(place[:, :, :], place[:, :, :], over[:, :, :], ALU.add).then_inc(ranks_read, 1)
            dve.wait_ge(ranks_read, n)
            for k in range(2):
                ins = nc.vector.tensor_tensor(pick[:, :, k, :], hot[:, :, k, :], place[:, :, :], ALU.mult)
            ins.then_inc(route_step, 1)
            dve.wait_ge(route_step, 8 * at.b + 7)
            nc.vector.tensor_reduce(slot_f[:, :], pick[:, :, :, :].rearrange("p t k e -> p (t k) e"), AX.X,
                                    ALU.add).then_inc(route_step, 1)
            dve.wait_ge(route_step, 8 * at.b + 8)
            nc.vector.tensor_copy(slot[at.par][:, :], slot_f[:, :]).then_inc(routed, 1)
            nc.vector.tensor_tensor(seen[:, :], seen[:, :], hot_sum[:, 0, :], ALU.add).then_inc(seen_counted, 1)
            dve.wait_ge(seen_counted, 2 * at.b + 1)
            nc.vector.tensor_tensor(seen[:, :], seen[:, :], hot_sum[:, 1, :], ALU.add).then_inc(seen_counted, 1)

        def spread_patches(pool, at):
            wait(pool, h_summed, at.b)
            for g in range(NG):
                pool.wait_ge(x_pooled, NG * at.b + g + 1)
                ins = nc.gpsimd.tensor_tensor(spread[:, g, :].rearrange("p (i j) -> p i j", j=SIDE),
                                              pooled[at.par][:, g, :].unsqueeze(1).to_broadcast([XP, SIDE, SIDE]),
                                              patch[:, :].unsqueeze(2).to_broadcast([XP, SIDE, SIDE]), ALU.mult)
            ins.then_inc(x_spread, 1)

        def inverse_std(pool, at, var, rstd, ln_step):
            pool.wait_ge(ln_step, 4 * at.b + 3)
            nc.gpsimd.tensor_tensor(rstd[:, :], var[:, :], minus_half[:, 0:2], ALU.pow).then_inc(ln_step, 1)

        def add_rotation(pool, at, t):
            n = at.b + 1
            pool.wait_ge(qk_read[t], n)
            if t == 0:
                wait(pool, qk_turned[5], at.b)
            for half in range(2):
                dst = qk[:, t, :, :, 8 * half:8 * half + 8]
                a = rot_c[:, t, :].rearrange("p (a s k) -> p a s k", s=2, k=8)[:, :, half, :].unsqueeze(2)
                b = rot_s[:, t, :].rearrange("p (a s k) -> p a s k", s=2, k=8)[:, :, 1 - half, :].unsqueeze(2)
                a, b = (v.to_broadcast([TT, 2 * HEADS, 4, 8]) for v in (a, b))
                nc.gpsimd.tensor_tensor(dst, a, b, ALU.add).then_inc(qk_rotated[t], 1)

        def copy_h(act, at):
            n = at.b + 1
            act.wait_ge(h_summed, n)
            wait(act, ln1_done, at.b - 1)
            wait(act, h_kept, at.b - 1)
            nc.scalar.activation(h[at.par][:, 0, :], bank[6][0:TT, 0:D], ACT.Copy)
            nc.scalar.activation(h[at.par][0:IMG1, 1, :], bank[6][0:IMG1, D:2 * D], ACT.Copy).then_inc(h_copied, 1)

        def keep_h(act, at):
            act.wait_ge(h_copied, at.b + 1)
            act.wait_ge(txt_loaded[at.par], 16 * (at.half + 1))
            wait(act, h2_made, at.b)
            nc.scalar.activation(h_keep[:, :, :], h[at.par][:, :, :], ACT.Copy).then_inc(h_kept, 1)

        def copy_xn(act, at):
            act.wait_ge(xn_turned, at.b + 1)
            wait(act, v_made, at.b)
            nc.scalar.activation(xn_t[:, :, :], bank[7][0:C1, 0:2 * T].rearrange("p (c n) -> p c n", c=2),
                                 ACT.Copy).then_inc(xn_ready, 1)

        def copy_v(act, at):
            act.wait_ge(v_made, at.b + 1)
            wait(act, attended[2], at.b - 1)
            nc.scalar.activation(val[at.par][0:TT, :, :, 0:HD].rearrange("p t a k -> p (t a) k"),
                                 bank[6][0:TT, 0:2 * D].rearrange("p (a k) -> p a k", k=HD), ACT.Copy).then_inc(v_ready, 1)

        def round_qk(act, at, r):
            n = at.b + 1
            act.wait_ge(qk_turned[r], n)
            if r >= 2:
                act.wait_ge(qk_split[r - 2], n)
            else:
                wait(act, qk_split[r + 4], at.b)
            nc.scalar.activation(rounded[r % 2][:, :], bank[r % 4][:, 0:4 * TT], ACT.Copy).then_inc(qk_rounded, 1)

        def round_shift(act, at):
            act.wait_ge(shift_turned, at.b + 1)
            wait(act, shift_ready, at.b)
            nc.scalar.activation(shift_hi[:, :], bank[5][:, 0:T], ACT.Copy).then_inc(shift_rounded, 1)

        def exp_scores(act, at, k):
            g, m = divmod(k, 3)
            act.wait_ge(scored_t[k], at.b + 1)
            if m == 0:
                wait(act, attended[g], at.b)
            src = bank[(k + 3) % 4]
            if m < 2:
                p = 2 * g + m
                nc.scalar.activation(prob0[:, 2 * p:2 * p + 2, :], src[0:TT + 1, 0:2 * T].rearrange("p (a n) -> p a n", a=2),
                                     ACT.Exp, scale=0.25).then_inc(probed[k], 1)
            else:
                nc.scalar.activation(prob1[:, 4 * g:4 * g + 4, :], src[0:TT, 0:4 * TT].rearrange("p (a n) -> p a n", a=4),
                                     ACT.Exp, scale=0.25).then_inc(probed[k], 1)

        def copy_y(act, at):
            act.wait_ge(attended[2], at.b + 1)
            wait(act, y_turned[1], at.b)
            nc.scalar.activation(y_t[:, 0:2, :], bank[4][:, 0:2 * T].rearrange("p (a n) -> p a n", a=2), ACT.Copy)
            nc.scalar.activation(y_t[:, 2, :], bank[5][:, 0:T], ACT.Copy).then_inc(y_copied, 1)

        def copy_yn(act, at):
            act.wait_ge(yn_turned, at.b + 1)
            wait(act, projected, at.b)
            nc.scalar.activation(yn_t[:, :, :], bank[4][0:C1, 0:2 * T].rearrange("p (c n) -> p c n", c=2),
                                 ACT.Copy).then_inc(yn_ready, 1)

        def copy_xf(act, at):
            act.wait_ge(xf_turned, at.b + 1)
            wait(act, gated, at.b)
            nc.scalar.activation(xf_t[:, :, :], bank[4][0:C, 0:2 * T].rearrange("p (c n) -> p c n", c=2),
                                 ACT.Copy).then_inc(xf_ready, 1)

        def exp_gap(act, at):
            act.wait_ge(gaps_made, at.b + 1)
            wait(act, weights_made, at.b)
            nc.scalar.activation(gexp[:, :], gap[:, :], ACT.Exp).then_inc(gate_exp, 1)

        def sum_channels(pe, at):
            n = at.b + 1
            pe.wait_ge(x_spread, n)
            wait(pe, v_ready, at.b)
            wait(pe, ranks_read, at.b - 2)
            for t, (lo, hi) in enumerate(((0, TT), (TT, SIDE * SIDE))):
                for g in range(NG):
                    ins = nc.tensor.matmul(bank[6][0:hi - lo, D * t:D * (t + 1)], spread[:, g, lo:hi], chan[:, g, :],
                                           start=(g == 0), stop=(g == NG - 1))
            ins.then_inc(h_summed, 1)

        def turn_xn(pe, at):
            n = at.b + 1
            pe.wait_ge(ln1_done, n)
            wait(pe, qk_read[1], at.b)
            for c in range(2):
                for t in range(2):
                    ins = nc.tensor.transpose(bank[7][0:C1, T * c + TT * t:T * c + TT * (t + 1)], xn[:, t, c, :], ident[0:TT, 0:TT])
            ins.then_inc(xn_turned, 1)

        def make_qk(pe, at, t):
            n = at.b + 1
            pe.wait_ge(xn_ready, n)
            for c in range(2):
                ins = nc.tensor.matmul(bank[6 + t][0:TT, 0:2 * D], xn_t[:, c, TT * t:TT * (t + 1)], w_qkv[:, c, 0:2 * D],
                                       start=(c == 0), stop=(c == 1))
            ins.then_inc(qk_made[t], 1)

        def make_v(pe, at):
            n = at.b + 1
            pe.wait_ge(qk_read[0], n)
            for t in range(2):
                for c in range(2):
                    ins = nc.tensor.matmul(bank[6][0:TT, D * t:D * (t + 1)], xn_t[:, c, TT * t:TT * (t + 1)],
                                           w_qkv[:, c, 2 * D:3 * D], start=(c == 0), stop=(c == 1))
            ins.then_inc(v_made, 1)

        def turn_qk(pe, at, r):
            n = at.b + 1
            if r == 0:
                pe.wait_ge(qk_rotated[1], 2 * n)
                pe.wait_ge(qk_rotated[0], 2 * n)
            if r < 4:
                wait(pe, probed[5 + r], at.b)
            else:
                pe.wait_ge(qk_split[r - 4], n)
            k = TURNS[r]
            for a in range(2):
                for t in range(2):
                    src = qk[:, t, 4 * k + 2 * a:4 * k + 2 * a + 2, :, :].rearrange("p a s k -> p (a s k)")
                    ins = nc.tensor.transpose(bank[r % 4][:, TT * (2 * a + t):TT * (2 * a + t + 1)], src, ident[0:TT, 0:TT])
            ins.then_inc(qk_turned[r], 1)

        def score(pe, at, k):
            n = at.b + 1
            if k < 3:
                pe.wait_ge(qk_split[2 * k], n)
                pe.wait_ge(qk_split[2 * k + 1], n)
            if k < 4:
                pe.wait_ge(qk_split[k + 2], n)
            else:
                pe.wait_ge(maxed[k - 4], n)
            dst = bank[(k + 2) % 4]
            if k < 3:
                nc.tensor.matmul(dst[0:TT, 0:4 * TT], ident_r[0:TT, 0:TT], mask_q0[:, :, :], start=True, stop=False)
                for a in range(4):
                    hh = 4 * k + a
                    ins = nc.tensor.matmul(dst[0:TT, TT * a:TT * (a + 1)], q_t[:, hh, 0:TT], k_t[:, hh // 2, 0, 0:TT],
                                           start=False, stop=(a == 3))
            else:
                kk = k - 3
                nc.tensor.matmul(dst[0:TT, 0:2 * T], ident_r[0:TT, 0:TT], mask_q1[:, :, :], start=True, stop=False)
                for a in range(2):
                    hh = 2 * kk + a
                    ins = nc.tensor.matmul(dst[0:TT, T * a:T * (a + 1)], q_t[:, hh, TT:T], k_t[:, kk, :, 0:TT],
                                           start=False, stop=(a == 1))
            ins.then_inc(scored[k], 1)

        def turn_shift(pe, at):
            n = at.b + 1
            pe.wait_ge(shift_made, n)
            wait(pe, h2_made, at.b)
            for t in range(2):
                ins = nc.tensor.transpose(bank[5][:, TT * t:TT * (t + 1)], shift[:, t, :], ident[0:TT, 0:TT])
            ins.then_inc(shift_turned, 1)

        def score_t(pe, at, k):
            n = at.b + 1
            g, m = divmod(k, 3)
            if k == 0:
                pe.wait_ge(shift_ready, n)
            if k < 4:
                pe.wait_ge(maxed[5 + k], n)
            else:
                pe.wait_ge(probed[k - 4], n)
            dst = bank[(k + 3) % 4]
            if m < 2:
                p = 2 * g + m
                nc.tensor.matmul(dst[0:TT + 1, 0:2 * T], k_t[:, p, 0, :], q_t[:, 2 * p:2 * p + 2, :], start=True, stop=False)
                for a in range(2):
                    nc.tensor.matmul(dst[0:TT + 1, T * a:T * (a + 1)], sel[:, 2 * p + a, :], shift_t[:, :], start=False, stop=False)
                ins = nc.tensor.matmul(dst[0:TT, 0:2 * T].rearrange("p (a n) -> p a n", a=2)[:, :, 0:TT], ident_r[0:TT, 0:TT],
                                       mask_k[:, 0:2, :], start=False, stop=True)
            else:
                nc.tensor.matmul(dst[0:TT, 0:4 * TT], ident_r[0:TT, 0:TT], mask_k[:, :, :], start=True, stop=False)
                for p in range(2):
                    nc.tensor.matmul(dst[0:TT, 2 * TT * p:2 * TT * (p + 1)], k_t[:, 2 * g + p, 1, 0:TT],
                                     q_t[:, 4 * g + 2 * p:4 * g + 2 * p + 2, TT:T], start=False, stop=False)
                for a in range(4):
                    ins = nc.tensor.matmul(dst[0:TT, TT * a:TT * (a + 1)], sel[:, 4 * g + a, 0:TT], shift_t[:, TT:T],
                                           start=False, stop=(a == 3))
            ins.then_inc(scored_t[k], 1)

        def attend(pe, at, g):
            n = at.b + 1
            if g == 0:
                wait(pe, indexed, at.b)
                pe.wait_ge(v_ready, n)
            for m in range(3):
                pe.wait_ge(probed[3 * g + m], n)
            dst = bank[4][:, T * g:T * (g + 1)] if g < 2 else bank[5][:, 0:T]
            for a in range(4):
                hh = 4 * g + a
                nc.tensor.matmul(dst[32 * a:32 * a + 32, :], val[at.par][:, 0, hh, :], prob0[:, hh, :], start=True, stop=False,
                                 skip_group_check=True)
                ins = nc.tensor.matmul(dst[32 * a:32 * a + 32, TT:T], val[at.par][0:TT, 1, hh, :], prob1[:, hh, :], start=False,
                                       stop=True, skip_group_check=True)
            ins.then_inc(attended[g], 1)

        def after(at, n=1):
            return min(at.b + 1 + n, B) if isinstance(at.b, int) else at.b + 1 + n

        def turn_y(pe, at, t):
            n = at.b + 1
            if t == 0:
                pe.wait_ge(y_copied, n)
            for g in range(3):
                ins = nc.tensor.transpose(bank[4 + t][0:TT, 128 * g:128 * (g + 1)], y_t[:, g, TT * t:TT * (t + 1)], ident[:, :])
            ins.then_inc(y_turned[t], 1)

        def turn_yn(pe, at):
            n = at.b + 1
            pe.wait_ge(y_normed, 2 * n)
            for c in range(2):
                for t in range(2):
                    ins = nc.tensor.transpose(bank[4][0:C1, T * c + TT * t:T * c + TT * (t + 1)], yn[:, t, c, :], ident[0:TT, 0:TT])
            ins.then_inc(yn_turned, 1)

        def project(pe, at):
            n = at.b + 1
            pe.wait_ge(yn_ready, n)
            for t in range(2):
                for c in range(2):
                    ins = nc.tensor.matmul(bank[5][0:TT, D * t:D * (t + 1)], yn_t[:, c, TT * t:TT * (t + 1)], w_out[:, c, :],
                                           start=(c == 0), stop=(c == 1))
            ins.then_inc(projected, 1)

        def turn_xf(pe, at):
            n = at.b + 1
            pe.wait_ge(ln2_done, n)
            for c in range(2):
                for t in range(2):
                    ins = nc.tensor.transpose(bank[4][0:C, T * c + TT * t:T * c + TT * (t + 1)], row[at.par][:, t, C * c:C * (c + 1)],
                                              ident[0:TT, 0:TT])
            ins.then_inc(xf_turned, 1)

        def gate_logits(pe, at):
            n = at.b + 1
            pe.wait_ge(xf_ready, n)
            pe.wait_ge(shift_ready, after(at))
            for t in range(2):
                for c in range(2):
                    ins = nc.tensor.matmul(bank[5][0:TT, E * t:E * (t + 1)], xf_t[:, c, TT * t:TT * (t + 1)], gate[:, c, :],
                                           start=(c == 0), stop=(c == 1))
            ins.then_inc(gated, 1)

        def rank(pe, at):
            n = at.b + 1
            pe.wait_ge(hots_summed, n)
            pe.wait_ge(v_ready, after(at, 2))
            wait(pe, seen_counted, 2 * at.b)
            first, second = bank[6][0:TT, 0:E], bank[6][0:TT, E:2 * E]
            nc.tensor.matmul(first, before[:, :], hot_sum[:, 0, :], start=True, stop=False)
            nc.tensor.matmul(first, ones[:, :], seen[:, :], start=False, stop=True)
            nc.tensor.matmul(second, before[:, :], hot_sum[:, 1, :], start=True, stop=False)
            nc.tensor.matmul(second, ones[:, :], hot_sum[:, 0, :], start=False, stop=False)
            nc.tensor.matmul(second, ones[:, :], seen[:, :], start=False, stop=True).then_inc(ranks_made, 1)

        def step_tensor(pe, p, a, m, z):
            if m:
                turn_qk(pe, m, 0)
                turn_qk(pe, m, 1)
            if z:
                attend(pe, z, 2)
            if m:
                turn_qk(pe, m, 2)
                turn_qk(pe, m, 3)
            if z:
                turn_y(pe, z, 0)
                turn_y(pe, z, 1)
            if a:
                sum_channels(pe, a)
            if m:
                turn_qk(pe, m, 4)
                turn_qk(pe, m, 5)
            if z:
                turn_yn(pe, z)
            if m:
                for k in range(3):
                    score(pe, m, k)
            if z:
                project(pe, z)
            if m:
                for k in range(3, 6):
                    score(pe, m, k)
            if a:
                turn_xn(pe, a)
            if m:
                score(pe, m, 6)
                score(pe, m, 7)
            if a:
                make_qk(pe, a, 0)
            if m:
                score(pe, m, 8)
            if a:
                make_qk(pe, a, 1)
            if m:
                turn_shift(pe, m)
            if a:
                make_v(pe, a)
            if z:
                turn_xf(pe, z)
            if m:
                score_t(pe, m, 0)
                score_t(pe, m, 1)
            if z:
                gate_logits(pe, z)
            if m:
                score_t(pe, m, 2)
                score_t(pe, m, 3)
            if z:
                rank(pe, z)
            if m:
                score_t(pe, m, 4)
                attend(pe, m, 0)
                for k in range(5, 7):
                    score_t(pe, m, k)
                attend(pe, m, 1)
                for k in range(7, 9):
                    score_t(pe, m, k)

        def step_scalar(act, p, a, m, z):
            if m:
                round_qk(act, m, 0)
                round_qk(act, m, 1)
            if z:
                copy_y(act, z)
            if m:
                round_qk(act, m, 2)
                round_qk(act, m, 3)
            if a:
                copy_h(act, a)
            if m:
                for r in range(4, 6):
                    round_qk(act, m, r)
            if z:
                copy_yn(act, z)
            if a:
                copy_xn(act, a)
            if m:
                keep_h(act, m)
                round_shift(act, m)
            if a:
                copy_v(act, a)
            if z:
                copy_xf(act, z)
            if m:
                exp_scores(act, m, 0)
                exp_scores(act, m, 1)
            if z:
                exp_gap(act, z)
            if m:
                for k in range(2, 9):
                    exp_scores(act, m, k)

        def step_vector(dve, p, a, m, z):
            if m:
                for r in range(4):
                    split_qk(dve, m, r)
            if z:
                normalize(dve, z, 0)
                normalize(dve, z, 1)
            if m:
                for r in range(4, 6):
                    split_qk(dve, m, r)
            if a:
                norm1_stats(dve, a)
            if m:
                for k in range(3):
                    max_scores(dve, m, k)
            if a:
                norm1_apply(dve, a)
            if p:
                pool_image(dve, p, 0)
            if z:
                residual(dve, z)
            if m:
                for k in range(3, 6):
                    max_scores(dve, m, k)
            if z:
                norm2_stats(dve, z)
            if a:
                rotate(dve, a, 0)
            if m:
                for k in range(6, 9):
                    max_scores(dve, m, k)
                make_shift(dve, m)
            if z:
                norm2_apply(dve, z)
            if m:
                split_shift(dve, m)
            if a:
                rotate(dve, a, 1)
            if p:
                pool_image(dve, p, 1)
            if z:
                choose(dve, z)
                weigh(dve, z)
            if p:
                pool_image(dve, p, 2)
            if z:
                assign(dve, z)

        PEEL = 6

        def steps(eng, step):
            def one(half, par, known):
                i = 2 * half + par if known else None
                step(eng, *(Batch(half, par, lag) if not known or 0 <= i - lag < B else None for lag in range(4)))

            for i in range(PEEL):
                one(i // 2, i % 2, True)
            with eng.Fori(PEEL // 2, B // 2) as half:
                one(half, 0, False)
                one(half, 1, False)
            for i in range(B, B + 3):
                one(i // 2, i % 2, True)

        def pass1_sync(sp):
            def one(half, par, fill, known=None):
                p, a, z = (Batch(half, par, lag) if known is None or 0 <= known - lag < B else None for lag in (0, 1, 3))
                if p:
                    load_image(sp, p)
                if a:
                    load_text(sp, a)
                if fill:
                    fill_slots(sp, p)
                if z:
                    store_h2(sp, z)

            for i in range(PEEL):
                one(i // 2, i % 2, i < FILLS, i)
            with sp.Fori(PEEL // 2, FILLS // 2) as half:
                one(half, 0, True)
                one(half, 1, True)
            with sp.Fori(FILLS // 2, B // 2) as half:
                one(half, 0, False)
                one(half, 1, False)
            for i in range(B, B + 3):
                one(i // 2, i % 2, False, i)

        def pass1_gpsimd(pool):
            def one(half, par, known=None, fill=None):
                p, a, z = (Batch(half, par, lag) if known is None or 0 <= known - lag < B else None for lag in (0, 1, 3))
                if a:
                    inverse_std(pool, a, var1, rstd1, ln1_step)
                if z:
                    inverse_std(pool, z, var2, rstd2, ln2_step)
                if a:
                    add_rotation(pool, a, 0)
                    add_rotation(pool, a, 1)
                if p:
                    spread_patches(pool, p)
                if z:
                    scatter_waits(pool, z, fill)

            for i in range(PEEL):
                one(i // 2, i % 2, i)
            with pool.Fori(PEEL // 2, FILLS // 2) as half:
                one(half, 0, fill=True)
                one(half, 1, fill=True)
            with pool.Fori(FILLS // 2, B // 2) as half:
                one(half, 0, fill=False)
                one(half, 1, fill=False)
            for i in range(B, B + 3):
                one(i // 2, i % 2, i)

        def scatter_waits(pool, z, fill):
            if fill or (fill is None and z.b < FILLS):
                pool.wait_ge(filled[z.par], 16 * (z.half + 1))
            else:
                pool.wait_ge(filled[z.par], 16 * (FILLS // 2))
            scatter_rows(pool, z)

        def scatter_rows(pool, at):
            pool.wait_ge(row_whole, at.b + 1)
            hold(pool, routed, at.b + 1, held)
            for t in range(2):
                for k in range(TOPK):
                    nc.gpsimd.indirect_dma_start(
                        out=moe_rows[0:SLOTS, :],
                        out_offset=bass.IndirectOffsetOnAxis(ap=slot[at.par][:, 2 * t + k:2 * t + k + 1], axis=0),
                        in_=row[at.par][:, t, :], in_offset=None, bounds_check=SLOTS - 1, oob_is_err=False,
                    ).then_inc(scattered[at.par], 16)

        rows_n = moe_rows.rearrange("(n p s) w -> n p s w", p=TT, s=SUB)

        def load_expert(sp, e, par):
            for dst, src in ((w_raw[:, 0, :], w13_t[e, 0:128, :]), (w_raw[0:64, 1, :], w13_t[e, 128:D, :]),
                             (w_raw[64:128, 1, :], w13_t[e, 128:D, :]),
                             (nw[:, 0:1], norm_w_t[e, 0:128, :]), (nw[0:64, 1:2], norm_w_t[e, 128:D, :]),
                             (nw[64:128, 1:2], norm_w_t[e, 128:D, :]),
                             (w_dn[par][:, :, :], w2_t[e, :, :].rearrange("(j p) n -> p j n", p=128))):
                sp.dma_start(dst, src).then_inc(w_loaded, 16)

        def load_rows(sp, n, par):
            sp.dma_start(xr[par][:, :, :], rows_n[n, :, :, :]).then_inc(rows_loaded[par], 16)

        def round_expert(act, e, par):
            act.wait_ge(w_loaded, 112 * (e + 1))
            wait(act, down, TILES * (e - 1))
            for c in range(2):
                ins = nc.scalar.activation(w_hi[par][:, c, :], w_raw[:, c, :], ACT.Copy, scale=nw[:, c:c + 1])
            ins.then_inc(w_rounded, 1)

        def split_expert(dve, e, par):
            dve.wait_ge(w_rounded, e + 1)
            for c in range(2):
                ins = nc.vector.scalar_tensor_tensor(out=w_lo[par][:, c, :], in0=w_raw[:, c, :], scalar=nw[:, c:c + 1],
                                                     in1=w_hi[par][:, c, :].bitcast(fp32), op0=ALU.mult, op1=ALU.subtract)
            ins.then_inc(w_split, 1)

        def square_rows(act, n, par, pair):
            act.wait_ge(rows_loaded[par], 16 * (pair + 1))
            wait(act, rms_sum, n)
            for s in range(SUB):
                ins = nc.scalar.activation(sq[:, s, :], xr[par][:, s, 0:D], ACT.Square, accum_out=ssum[:, s:s + 1])
            ins.then_inc(squared, 1)

        def make_z(dve, n, par):
            dve.wait_ge(rms_made, n + 1)
            wait(dve, zb_turned, n)
            for s in range(SUB):
                ins = nc.vector.tensor_scalar(z[:, s, 0:D], xr[par][:, s, 0:D], rms2[:, s:s + 1], None, ALU.mult)
            ins.then_inc(z_scaled, 1)
            dve.wait_ge(z_scaled, n + 1)
            nc.vector.tensor_copy(z[:, :, D:256], z[:, :, 128:D]).then_inc(z_made, 1)

        def mean_square(dve, n):
            dve.wait_ge(squared, n + 1)
            nc.vector.tensor_scalar(rms[:, :], ssum[:, :], 1.0 / D, RMS_EPS / 4.0, ALU.mult, ALU.add).then_inc(rms_sum, 1)

        def take_numbers(dve, n, par, pair, e):
            wait(dve, added[par], 16 * SUB * pair)
            dve.wait_ge(rows_loaded[par], 16 * (pair + 1))
            hold(dve, y_weighted, n - 1, held)
            nc.vector.tensor_copy(w_slot[par][:, :].unsqueeze(2), xr[par][:, :, bass.ds(COL_W + e, 1)])
            nc.vector.tensor_copy(who[par][:, :].unsqueeze(2),
                                  xr[par][:, :, COL_ID:COL_ID + 1].bitcast(u32)).then_inc(numbered, 1)

        def weigh_x(act, n, par):
            act.wait_ge(numbered, n + 1)
            wait(act, y_weighted, n)
            for s in range(SUB):
                ins = nc.scalar.activation(xw[:, s, :], xr[par][:, s, 0:D], ACT.Copy, scale=w_slot[par][:, s:s + 1])
            ins.then_inc(x_weighted, 1)

        def turn_z(pe, n):
            pe.wait_ge(z_made, n + 1)
            wait(pe, za_split, n)
            wait(pe, zb_split, n)
            for s in range(SUB):
                ins = nc.tensor.transpose(bank[4][:, TT * s:TT * (s + 1)], z[:, s, 0:128], ident[0:TT, 0:TT])
            ins.then_inc(za_turned, 1)
            for s in range(SUB):
                ins = nc.tensor.transpose(bank[5][:, TT * s:TT * (s + 1)], z[:, s, 128:256], ident[0:TT, 0:TT])
            ins.then_inc(zb_turned, 1)

        def round_z(act, n):
            act.wait_ge(za_turned, n + 1)
            nc.scalar.activation(za_hi[:, :], bank[4][:, 0:ROWS], ACT.Copy).then_inc(za_rounded, 1)
            act.wait_ge(zb_turned, n + 1)
            nc.scalar.activation(zb_hi[:, :], bank[5][:, 0:ROWS], ACT.Copy).then_inc(zb_rounded, 1)

        def split_z(dve, n):
            dve.wait_ge(za_rounded, n + 1)
            nc.vector.tensor_tensor(za_lo[:, :], bank[4][:, 0:ROWS], za_hi[:, :].bitcast(fp32), ALU.subtract).then_inc(za_split, 1)
            dve.wait_ge(zb_rounded, n + 1)
            nc.vector.tensor_copy(zb[0:64, :], zb_hi[0:64, :].bitcast(fp32))
            nc.vector.tensor_tensor(zb[64:128, :], bank[5][64:128, 0:ROWS], zb_hi[64:128, :].bitcast(fp32),
                                    ALU.subtract).then_inc(zb_split, 1)

        def expert_up(pe, n, e_par, j):
            if j == 0:
                pe.wait_ge(za_split, n + 1)
                pe.wait_ge(zb_split, n + 1)
            if j >= 2:
                pe.wait_ge(hid_made[j - 2], n + 1)
            else:
                wait(pe, hid_made[j + 2], n)
            hi, lo = w_hi[e_par], w_lo[e_par]
            for side in range(2):
                dst = bank[2 * (j % 2) + side][:, 0:ROWS]
                col = slice(HID * side + 128 * j, HID * side + 128 * (j + 1))
                nc.tensor.matmul(dst, hi[:, 0, col], za_hi[:, :], start=True, stop=False)
                nc.tensor.matmul(dst, hi[:, 0, col], za_lo[:, :], start=False, stop=False)
                nc.tensor.matmul(dst, lo[:, 0, col], za_hi[:, :], start=False, stop=False)
                nc.tensor.matmul(dst, hi[:, 1, col], zb[:, :], start=False, stop=False)
                ins = nc.tensor.matmul(dst, lo[:, 1, col], zb[:, :], start=False, stop=True)
            ins.then_inc(gate_up[j], 1)

        def silu(act, n, j):
            act.wait_ge(gate_up[j], n + 1)
            if j >= 2:
                act.wait_ge(hid_made[j - 2], n + 1)
            else:
                wait(act, hid_made[j + 2], n)
            nc.scalar.activation(act_g[:, j % 2, :], bank[2 * (j % 2)][:, 0:ROWS], ACT.Silu).then_inc(silued, 1)

        def make_hid(dve, n, j):
            dve.wait_ge(silued, 4 * n + j + 1)
            if j == 0:
                wait(dve, down, n)
            nc.vector.tensor_tensor(hid[:, j, :], bank[2 * (j % 2) + 1][:, 0:ROWS], act_g[:, j % 2, :], ALU.mult).then_inc(hid_made[j], 1)

        def expert_down(pe, n, e_par):
            wait(pe, y_weighted, n)
            for j in range(4):
                pe.wait_ge(hid_made[j], n + 1)
                for s in range(SUB):
                    ins = nc.tensor.matmul(bank[6 + s // 2][0:TT, D * (s % 2):D * (s % 2 + 1)], hid[:, j, TT * s:TT * (s + 1)],
                                           w_dn[e_par][:, j, :], start=(j == 0 and s % 2 == 0), stop=(j == 3),
                                           skip_group_check=True)
            ins.then_inc(down, 1)

        def weigh_rows(dve, n, par):
            dve.wait_ge(down, n + 1)
            dve.wait_ge(x_weighted, n + 1)
            for s in range(SUB):
                ins = nc.vector.scalar_tensor_tensor(
                    out=ys[par][:, s, :], in0=bank[6 + s // 2][0:TT, D * (s % 2):D * (s % 2 + 1)], scalar=w_slot[par][:, s:s + 1],
                    in1=xw[:, s, :], op0=ALU.mult, op1=ALU.add)
            ins.then_inc(y_weighted, 1)

        def inverse_rms(pool, n):
            pool.wait_ge(rms_sum, n + 1)
            nc.gpsimd.tensor_tensor(rms2[:, :], rms[:, :], minus_half[:, 0:SUB], ALU.pow).then_inc(rms_made, 1)

        def add_rows(pool, n, par, pair):
            pool.wait_ge(y_weighted, n + 1)
            pool.wait_ge(numbered, n + 1)
            if par:
                hold(pool, added[0], 16 * SUB * (pair + 1), held)
            else:
                hold(pool, added[1], 16 * SUB * pair, held)
            for s in range(SUB):
                nc.gpsimd.indirect_dma_start(
                    out=out[:, :], out_offset=bass.IndirectOffsetOnAxis(ap=who[par][:, s:s + 1], axis=0),
                    in_=ys[par][:, s, :], in_offset=None, bounds_check=TOKENS + ROWS - 1, oob_is_err=True,
                    compute_op=ALU.add).then_inc(added[par], 16)

        PT = TILES // 2

        def over_tiles(eng, tile, between=None):
            def expert(e, e_par):
                def pair_of(k):
                    pair = e * PT + k
                    for par in range(2):
                        next_e = e + 1 if par and isinstance(k, int) and k == PT - 1 else e
                        tile(2 * pair + par, e, e_par, par, pair, next_e)

                pair_of(0)
                if between:
                    between(e + 1, 1 - e_par)
                with eng.Fori(1, PT - 1) as k:
                    pair_of(k)
                pair_of(PT - 1)

            expert(0, 0)
            expert(1, 1)
            with eng.Fori(1, E // 2) as e2:
                expert(2 * e2, 0)
                expert(2 * e2 + 1, 1)

        def ahead(n, par, pair):
            return n + 1, 1 - par, pair + par

        block = ctx.enter_context(nc.Block())

        @block.sync
        def _(sp):
            setup_sync(sp)
            pass1_sync(sp)
            sp.wait_ge(x_pooled, NG * B)
            sp.wait_ge(attended[2], B)
            load_expert(sp, 0, 0)
            for par in range(2):
                sp.wait_ge(scattered[par], 64 * (B // 2))
            for par in range(2):
                load_rows(sp, par, par)

            def tile(n, e, e_par, par, pair, next_e):
                sp.wait_ge(z_made, n + 1)
                sp.wait_ge(x_weighted, n + 1)
                sp.wait_ge(numbered, n + 1)
                load_rows(sp, n + 2, par)

            def between(e, par):
                hold(sp, w_split, e, held)
                hold(sp, down, TILES * (e - 1), held)
                load_expert(sp, e, par)

            over_tiles(sp, tile, between)

        @block.gpsimd
        def _(pool):
            pool.wait_ge(prepared, 1)
            pass1_gpsimd(pool)
            for par in range(2):
                pool.wait_ge(h2_stored[par], 16 * (B // 2))
            pool.wait_ge(spare_set, 32)
            inverse_rms(pool, 0)
            inverse_rms(pool, 1)

            def tile(n, e, e_par, par, pair, next_e):
                inverse_rms(pool, n + 2)
                add_rows(pool, n, par, pair)

            over_tiles(pool, tile)
            for par in range(2):
                pool.wait_ge(added[par], 16 * SUB * E * PT)

        @block.vector
        def _(dve):
            setup_vector(dve)
            steps(dve, step_vector)
            mean_square(dve, 0)
            make_z(dve, 0, 0)
            split_expert(dve, 0, 0)
            split_z(dve, 0)
            take_numbers(dve, 0, 0, 0, 0)
            mean_square(dve, 1)

            def tile(n, e, e_par, par, pair, next_e):
                n1, par1, pair1 = ahead(n, par, pair)
                make_hid(dve, n, 0)
                make_z(dve, n1, par1)
                for j in range(1, 4):
                    make_hid(dve, n, j)
                split_z(dve, n1)
                take_numbers(dve, n1, par1, pair1, next_e)
                mean_square(dve, n + 2)
                weigh_rows(dve, n, par)

            over_tiles(dve, tile, lambda e, par: split_expert(dve, e, par))

        @block.scalar
        def _(act):
            act.wait_ge(prepared, 1)
            steps(act, step_scalar)
            round_expert(act, 0, 0)
            square_rows(act, 0, 0, 0)
            round_z(act, 0)
            square_rows(act, 1, 1, 0)

            def tile(n, e, e_par, par, pair, next_e):
                n1, par1, pair1 = ahead(n, par, pair)
                silu(act, n, 0)
                weigh_x(act, n, par)
                for j in range(1, 4):
                    silu(act, n, j)
                round_z(act, n + 1)
                square_rows(act, n + 2, par, pair + 1)

            over_tiles(act, tile, lambda e, par: round_expert(act, e, par))

        @block.tensor
        def _(pe):
            setup_tensor(pe)
            steps(pe, step_tensor)
            pe.wait_ge(w_split, 1)
            turn_z(pe, 0)

            def tile(n, e, e_par, par, pair, next_e):
                if par == 0:
                    pe.wait_ge(w_split, e + 1)
                for j in range(4):
                    expert_up(pe, n, e_par, j)
                turn_z(pe, n + 1)
                expert_down(pe, n, e_par)

            over_tiles(pe, tile)


def kernel(**inputs):
    import concourse.bacc as bacc
    from concourse.bass_utils import run_bass_kernel_spmd

    def host(name):
        return np.asarray(inputs[name])

    batches = host("x").shape[0]
    tokens = batches * T
    head = np.concatenate([np.arange(0, HD, 2), np.arange(1, HD, 2)])
    cols = np.concatenate([np.arange(2 * HEADS)[:, None] * HD + head, 2 * D + np.arange(D).reshape(HEADS, HD)]).reshape(-1)
    wrap = list(range(E)) + [0]
    arrays = {
        "x": host("x"), "txt": host("txt"), "chan_w": host("L0_tok_channel_weights"),
        "norm_scale": host("L0_attn_norm_scale"), "norm_bias": host("L0_attn_norm_bias"),
        "w_attn": host("L0_attn_W_attn")[:, cols], "b_attn": host("L0_attn_b_attn")[cols],
        "w_proj": host("L0_attn_W_proj"), "b_proj": host("L0_attn_b_proj"),
        "sinks": host("L0_attn_sinks"), "rezero": host("L0_attn_rezero"),
        "gate_t": host("L0_ffn_gate_w").T,
        "w13_t": host("L0_ffn_w13").transpose(0, 2, 1)[wrap],
        "w2_t": host("L0_ffn_w2").transpose(0, 2, 1)[wrap],
        "norm_w_t": host("L0_ffn_norm_w")[wrap][:, :, None],
    }
    fixed = constants(tokens)
    nc = bacc.Bacc("TRN2", target_bir_lowering=False, num_devices=1)
    feeds, aps = {}, {}
    for name, a in list(arrays.items()) + [("const_" + k, v) for k, v in fixed.items()]:
        a = np.ascontiguousarray(a)
        feeds[f"in_{name}"] = a
        aps[name] = nc.dram_tensor(f"in_{name}", a.shape, mybir.dt.from_np(a.dtype), kind="ExternalInput").ap()
    out = nc.dram_tensor("out", [tokens + ROWS, D], mybir.dt.float32, kind="ExternalOutput").ap()
    build(nc, *[aps[name] for name in arrays], {k: aps["const_" + k] for k in fixed}, out)
    r = run_bass_kernel_spmd(nc, [feeds], core_ids=[0])
    return r.results[0]["out"][:tokens].reshape(batches, T, D)
```

```python
import math
from contextlib import ExitStack

import numpy as np
import concourse.bass as bass
from concourse import mybir

IMG, PATCH, CH = 224, 16, 12
SIDE = IMG // PATCH
HALF = PATCH // 2
GRP = 4
NG = CH // GRP
XP = GRP * SIDE * 2
XF = HALF * IMG
D = 192
HEADS, HD = 12, 16
PAIRS = HEADS // 2
TXT = 32
T = SIDE * SIDE + TXT
TT = T // 2
IMG1 = SIDE * SIDE - TT
C = D // 2
C1 = C + 1
E, TOPK, HID = 8, 2, 512
NEG = -1e30
FAR = 1 << 20
RW = 204
COL_W, COL_ID = D, D + E
LN_EPS, RMS_EPS = 1e-5, 1e-6
SUB = 4
ROWS = TT * SUB


def capacity(tokens):
    return int(math.ceil(1.25 * TOPK * tokens / E))


def constants(tokens):
    cap = capacity(tokens)
    f = np.float32
    freqs = f(1.0) / f(10000.0) ** (np.arange(0, HD, 2, dtype=f) / f(HD))
    ang = np.outer(np.arange(T, dtype=f), freqs.astype(f)).astype(f)
    cos = np.cos(ang).astype(f).reshape(2, TT, HD // 2).transpose(1, 0, 2)
    sin = np.sin(ang).astype(f).reshape(2, TT, HD // 2).transpose(1, 0, 2)
    p = np.arange(128)
    q = np.arange(TT)
    later = np.where(q[None, :] > q[:, None], f(NEG), f(0))
    sel = np.zeros((128, HEADS, TT + 1), f)
    for h in range(HEADS):
        sel[h, h] = -1
        sel[HEADS + h, h] = -1
    term = (p // HD) % 4
    split = np.zeros((128, 4), f)
    split[:, 0] = np.where(term % 2 == 1, -1, 0)
    split[:, 1] = np.where(term >= 2, -1, 0)
    split[HEADS:2 * HEADS, 2] = -1
    split[2 * HEADS + 1, 3] = -1
    small = np.zeros((128, 2 * E + 2), f)
    small[:, 0:E] = np.arange(E) * cap
    small[:, E:2 * E] = np.arange(E)
    small[:, 2 * E] = p
    small[:, 2 * E + 1] = p + TT
    filler = np.zeros((TT, 2, 2, RW), np.uint32)
    for par in range(2):
        for s in range(2):
            filler[:, par, s, COL_ID] = tokens + (par * T + 2 * q + s) % ROWS
    rows = np.arange(XP)
    return {
        "cos": np.ascontiguousarray(cos),
        "sin": np.ascontiguousarray(np.concatenate([sin, -sin], -1)),
        "ident": np.eye(128, dtype=f),
        "mask_q0": np.ascontiguousarray(np.repeat(later[:, None], 4, 1)),
        "mask_k": np.ascontiguousarray(np.repeat(later.T[:, None], 4, 1)),
        "sel": sel,
        "split": split,
        "small": small,
        "before": (q[:, None] < q[None, :]).astype(f),
        "patch": ((rows[:, None] // 2) % SIDE == np.arange(SIDE)[None]).astype(f),
        "filler": filler,
    }


CONST_NAMES = ["cos", "sin", "ident", "mask_q0", "mask_k", "sel", "split", "small",
               "before", "patch", "filler"]


class Batch:

    def __init__(self, half, par, lag=0):
        self.par = (par - lag) % 2
        self.half = half + (par - lag) // 2
        self.b = 2 * half + (par - lag)

    def ago(self, n):
        return Batch(self.half, self.par, n)


def wait(eng, sem, value):
    if not (isinstance(value, int) and value <= 0):
        eng.wait_ge(sem, value)


def hold(eng, sem, value, held):
    if not (isinstance(value, int) and value <= 0):
        eng.wait_ge(sem, value)
        eng.sem_inc(held, 1)


def build(nc, x, txt, chan_w, norm_scale, norm_bias, w_attn, b_attn, w_proj, b_proj, sinks,
          rezero, gate_t, w13_t, w2_t, norm_w_t, const, out):
    fp32, fp32r, bf16 = mybir.dt.float32, mybir.dt.float32r, mybir.dt.bfloat16
    u32 = mybir.dt.uint32
    ALU, ACT, AX = mybir.AluOpType, mybir.ActivationFunctionType, mybir.AxisListType

    B = x.shape[0]
    TOKENS = B * T
    CAP = capacity(TOKENS)
    SLOTS = E * CAP
    FILLS = CAP // T
    TILES = CAP // ROWS
    assert FILLS * T == CAP and TILES * ROWS == CAP and TILES % 2 == 0 and B % 2 == 0
    assert CAP % (2 * T) == 0

    moe_rows = nc.dram_tensor("moe_rows", [SLOTS + 2 * ROWS, RW], fp32).ap()

    ctx = ExitStack()
    with ctx:
        def sb(name, shape, dt=fp32):
            return ctx.enter_context(nc.sbuf_tensor(name, shape, dt))

        def sem(name):
            return ctx.enter_context(nc.semaphore(name))

        bank = [ctx.enter_context(nc.psum_tensor(f"bank{i}", [128, 512], fp32)) for i in range(8)]

        cos = sb("cos", [TT, 2, 8])
        sin = sb("sin", [TT, 2, 16])
        ident = sb("ident", [128, 128])
        ident_r = sb("ident_r", [128, 128], fp32r)
        mask_q0 = sb("mask_q0", [TT, 4, TT], fp32r)
        mask_k = sb("mask_k", [TT, 4, TT], fp32r)
        sel = sb("sel", [128, HEADS, TT + 1], fp32r)
        split = sb("split", [128, 4])
        small = sb("small", [128, 2 * E + 2])
        minus_half = sb("minus_half", [TT, 4])
        before = sb("before", [TT, TT], bf16)
        ones = sb("ones", [TT, TT], bf16)
        patch = sb("patch", [XP, SIDE])
        filler = sb("filler", [TT, 2, 2, RW], u32)
        chan = sb("chan", [XP, NG, D])
        scale_col = sb("scale_col", [C, 2])
        bias_col = sb("bias_col", [C, 2])
        w_qkv = sb("w_qkv", [C1, 2, 3 * D])
        b_row = sb("b_row", [1, 3 * D])
        b_fold = sb("b_fold", [1, 3 * D])
        w_out = sb("w_out", [C1, 2, D])
        rez = sb("rez", [C1, 1])
        sink_tok = sb("sink_tok", [TT, HEADS])
        sink_key = sb("sink_key", [128, HEADS])
        sink_hi = sb("sink_hi", [128, HEADS], fp32r)
        sink_ones = sb("sink_ones", [128, HEADS])
        gate = sb("gate", [C, 2, E])

        arena = sb("arena", [128, 2 * NG * XF])
        xin = [arena[0:XP, NG * XF * i:NG * XF * (i + 1)].rearrange("p (g f) -> p g f", g=NG) for i in range(2)]
        pooled = [sb(f"pooled{i}", [XP, NG, SIDE]) for i in range(2)]
        spread = sb("spread", [XP, NG, SIDE * SIDE])
        h = [sb(f"h{i}", [TT, 2, D]) for i in range(2)]
        h_keep = [sb(f"h_keep{i}", [TT, 2, D]) for i in range(2)]
        st1 = sb("st1", [TT, 2, 6])
        mv1 = sb("mv1", [TT, 2, 2])
        rstd1 = sb("rstd1", [TT, 2])
        minus_mean1 = sb("minus_mean1", [TT, 2])
        shifted1 = sb("shifted1", [TT, 2])
        var1 = sb("var1", [TT, 2])
        xn = sb("xn", [TT, 2, 2, C1])
        xn_t = sb("xn_t", [C1, 2, T])
        rot_c = sb("rot_c", [TT, 2, 2 * D])
        rot_s = sb("rot_s", [TT, 2, 2 * D])
        qk = sb("qk", [TT, 2, 2 * HEADS, 4, HD])
        val = [sb(f"val{i}", [TT + 1, 2, HEADS, 32]) for i in range(2)]
        rounded = [sb(f"rounded{i}", [128, 4 * TT], fp32r) for i in range(2)]
        pieces = sb("pieces", [128, 16 * HID + 4 * ROWS], fp32r)
        QF, KF = HEADS * T, PAIRS * 2 * (TT + 1)
        assert 2 * (QF + KF) <= 16 * HID + 4 * ROWS
        q_t = [pieces[:, QF * i:QF * (i + 1)].rearrange("p (a n) -> p a n", a=HEADS) for i in range(2)]
        k_t = [pieces[:, 2 * QF + KF * i:2 * QF + KF * (i + 1)].rearrange("p (a t n) -> p a t n", a=PAIRS, t=2)
               for i in range(2)]
        top = sb("top", [TT, 2, HEADS])
        shift = sb("shift", [TT, 2, 128])
        shift_hi = sb("shift_hi", [128, T], fp32r)
        shift_t = sb("shift_t", [128, T], fp32r)
        prob = sb("prob", [128, HEADS * T])
        staging, start = {}, 0
        for name, rows, width in (("mask_q0", TT, 4 * TT), ("mask_k", TT, 4 * TT), ("sel", 128, HEADS * (TT + 1)),
                                  ("before", TT, TT), ("sink_col", 128, HEADS)):
            staging[name] = prob[0:rows, start:start + width]
            start += width
        prob0 = prob[0:TT + 1, :].rearrange("p (a n) -> p a n", a=HEADS)
        prob1 = sb("prob1", [TT, HEADS, TT])
        y_t = sb("y_t", [128, 3, T])
        rden = sb("rden", [TT, 2, HEADS])
        yn = sb("yn", [TT, 2, 2, C1])
        yn_t = sb("yn_t", [C1, 2, T])
        h2 = [sb(f"h2_{i}", [TT, 2, D]) for i in range(2)]
        st2 = sb("st2", [TT, 2, 6])
        mv2 = sb("mv2", [TT, 2, 2])
        rstd2 = sb("rstd2", [TT, 2])
        minus_mean2 = sb("minus_mean2", [TT, 2])
        shifted2 = sb("shifted2", [TT, 2])
        var2 = sb("var2", [TT, 2])
        row = [sb(f"row{i}", [TT, 2, RW]) for i in range(2)]
        xf_t = sb("xf_t", [C, 2, T])
        best = sb("best", [TT, 2, 8])
        best_i = sb("best_i", [TT, 2, 8], u32)
        best_f = sb("best_f", [TT, 2, 2])
        gap = sb("gap", [TT, 2])
        gexp = sb("gexp", [TT, 2])
        gden = sb("gden", [TT, 2])
        gw = sb("gw", [TT, 2, 2])
        hot = sb("hot", [TT, 2, 2, E])
        hot_sum = sb("hot_sum", [TT, 2, E], bf16)
        seen = sb("seen", [TT, E], bf16)
        over = sb("over", [TT, 2, E])
        place = sb("place", [TT, 2, E])
        pick = sb("pick", [TT, 2, 2, E])
        wpick = sb("wpick", [TT, 2, 2, E])
        slot_f = sb("slot_f", [TT, 4])
        slot = [sb(f"slot{i}", [TT, 4], u32) for i in range(2)]
        token = sb("token", [TT, 2])

        taken = 0

        def view(parts, a, b):
            nonlocal taken
            taken += a * b
            assert taken <= 2 * NG * XF
            return arena[0:parts, taken - a * b:taken].rearrange("p (a b) -> p a b", a=a)

        w_raw = view(128, 2, 2 * HID)
        xr = [view(TT, SUB, RW) for _ in range(2)]
        z = view(TT, SUB, 256)
        act_g = view(128, 2, ROWS)
        hid = view(128, 4, ROWS)
        xw = view(TT, SUB, D)
        ys = [view(TT, SUB, D) for _ in range(2)]
        nw = sb("nw", [128, 2])
        w_hi, w_lo = ([pieces[:, 4 * HID * i:4 * HID * (i + 1)].rearrange("p (a n) -> p a n", a=2) for i in pair]
                      for pair in ((0, 1), (2, 3)))
        w_dn = [prob[:, 4 * D * i:4 * D * (i + 1)].rearrange("p (j n) -> p j n", j=4) for i in range(2)]
        sq = prob[0:TT, 8 * D:(8 + SUB) * D].rearrange("p (s n) -> p s n", s=SUB)
        ssum = sb("ssum", [TT, SUB])
        rms = sb("rms", [TT, SUB])
        rms2 = sb("rms2", [TT, SUB])
        za_hi, za_lo, zb_hi, zb = (pieces[:, 16 * HID + ROWS * i:16 * HID + ROWS * (i + 1)] for i in range(4))
        w_slot = [sb(f"w_slot{i}", [TT, SUB]) for i in range(2)]
        who = [sb(f"who{i}", [TT, SUB], u32) for i in range(2)]

        loaded = sem("loaded")
        cleared = sem("cleared")
        prepared = sem("prepared")
        fold_done = sem("fold_done")
        folded = sem("folded")
        bias_placed = sem("bias_placed")
        held = sem("held")
        step0 = sem("step0")

        x_loaded = [sem(f"x_loaded{i}") for i in range(2)]
        txt_loaded = [sem(f"txt_loaded{i}") for i in range(2)]
        filled = [sem(f"filled{i}") for i in range(2)]
        h2_stored = [sem(f"h2_stored{i}") for i in range(2)]
        scattered = [sem(f"scattered{i}") for i in range(2)]
        spare_set = sem("spare_set")
        x_folded = sem("x_folded")
        x_pooled = sem("x_pooled")
        x_spread = sem("x_spread")
        h_summed = sem("h_summed")
        h_copied = sem("h_copied")
        h_kept = sem("h_kept")
        ln1_step, ln1_done = sem("ln1_step"), sem("ln1_done")
        xn_turned, xn_ready = sem("xn_turned"), sem("xn_ready")
        qk_made = [sem(f"qk_made{t}") for t in range(2)]
        v_made, v_ready = sem("v_made"), sem("v_ready")
        qk_read = [sem(f"qk_read{t}") for t in range(2)]
        qk_rotated = [sem(f"qk_rotated{t}") for t in range(2)]
        qk_turned = [sem(f"qk_turned{k}") for k in range(6)]
        qk_rounded = sem("qk_rounded")
        qk_split = [sem(f"qk_split{k}") for k in range(6)]
        scored = [sem(f"scored{k}") for k in range(9)]
        maxed = [sem(f"maxed{k}") for k in range(9)]
        shift_made = sem("shift_made")
        shift_turned, shift_rounded, shift_ready = (sem(n) for n in ("shift_turned", "shift_rounded", "shift_ready"))
        scored_t = [sem(f"scored_t{k}") for k in range(9)]
        probed = [sem(f"probed{k}") for k in range(9)]
        attended = [sem(f"attended{g}") for g in range(3)]
        y_copied = sem("y_copied")
        y_turned = [sem(f"y_turned{t}") for t in range(2)]
        den_ready = sem("den_ready")
        y_normed = sem("y_normed")
        yn_turned, yn_ready = sem("yn_turned"), sem("yn_ready")
        projected, h2_made = sem("projected"), sem("h2_made")
        ln2_step, ln2_done = sem("ln2_step"), sem("ln2_done")
        xf_turned, xf_ready = sem("xf_turned"), sem("xf_ready")
        gated, ranked, gaps_made, gate_exp = (sem(n) for n in ("gated", "ranked", "gaps_made", "gate_exp"))
        indexed = sem("indexed")
        hots_summed, ranks_made = sem("hots_summed"), sem("ranks_made")
        route_step = sem("route_step")
        weights_made, row_whole, ranks_read = sem("weights_made"), sem("row_whole"), sem("ranks_read")
        seen_counted = sem("seen_counted")
        routed = sem("routed")

        w_loaded = sem("w_loaded")
        w_rounded = sem("w_rounded")
        w_split = sem("w_split")
        rows_loaded = [sem(f"rows_loaded{i}") for i in range(2)]
        squared, rms_sum, rms_made, z_scaled, z_made = (sem(n) for n in ("squared", "rms_sum", "rms_made", "z_scaled", "z_made"))
        za_turned, zb_turned = sem("za_turned"), sem("zb_turned")
        za_rounded, zb_rounded = sem("za_rounded"), sem("zb_rounded")
        za_split, zb_split = sem("za_split"), sem("zb_split")
        gate_up = [sem(f"gate_up{j}") for j in range(4)]
        silued = sem("silued")
        hid_made = [sem(f"hid_made{j}") for j in range(4)]
        down = sem("down")
        numbered, x_weighted, y_weighted = sem("numbered"), sem("x_weighted"), sem("y_weighted")
        added = [sem(f"added{i}") for i in range(2)]

        N_SMALL = 25

        def setup_sync(sp):
            for dst, src in (
                (cos[:, :, :], const["cos"]), (sin[:, :, :], const["sin"]), (ident[:, :], const["ident"]),
                (split[:, :], const["split"]), (small[:, :], const["small"]),
                (patch[:, :], const["patch"]), (filler[:, :, :, :], const["filler"]),
                (scale_col[:, :], norm_scale.rearrange("(c p) -> p c", p=C)),
                (bias_col[:, :], norm_bias.rearrange("(c p) -> p c", p=C)),
                (w_qkv[0:C, :, :], w_attn.rearrange("(c p) n -> p c n", p=C)),
                (b_row[:, :], b_attn.rearrange("(a n) -> a n", a=1)),
                (rez[:, :], rezero.rearrange("(a n) -> a n", a=1).to_broadcast([C1, 1])),
                (sink_tok[:, :], sinks.rearrange("(a n) -> a n", a=1).to_broadcast([TT, HEADS])),
                (gate[:, :, :], gate_t.rearrange("(c p) n -> p c n", p=C)),
            ):
                with nc.allow_non_contiguous_dma(reason="columns of a few vectors"):
                    sp.dma_start(dst, src).then_inc(loaded, 16)
            for g in range(NG):
                sp.dma_start(chan[:, g, :], chan_w[GRP * g:GRP * (g + 1), :].unsqueeze(1)
                             .to_broadcast([GRP, SIDE * 2, D])).then_inc(loaded, 16)
            for name in ("mask_q0", "mask_k", "sel", "before"):
                src = const[name]
                if len(src.shape) == 3:
                    src = src.rearrange("p a b -> p (a b)")
                sp.dma_start(staging[name], src).then_inc(loaded, 16)
            sp.wait_ge(cleared, 1)
            sp.dma_start(w_out[0:C, :, :], w_proj.rearrange("(c p) n -> p c n", p=C)).then_inc(loaded, 16)
            sp.dma_start(w_out[C:C1, 1, :], b_proj.rearrange("(a n) -> a n", a=1)).then_inc(loaded, 16)
            for r in range(2):
                sp.dma_start(sink_key[2 * HEADS + r:2 * HEADS + r + 1, :],
                             sinks.rearrange("(a n) -> a n", a=1)).then_inc(loaded, 16)
            sp.wait_ge(loaded, 16 * N_SMALL)
            sp.dma_start(out[TOKENS:TOKENS + ROWS, :].rearrange("(p s) n -> p s n", s=SUB),
                         filler[:, 0, 0, 0:D].bitcast(fp32).unsqueeze(1).to_broadcast([TT, SUB, D])
                         ).then_inc(spare_set, 16)
            sp.dma_start(moe_rows[SLOTS:SLOTS + 2 * ROWS, :].rearrange("(a p s) n -> p a (s n)", p=TT, s=2),
                         filler[:, 0, :, :].bitcast(fp32).rearrange("p s n -> p (s n)").unsqueeze(1)
                         .to_broadcast([TT, 2 * ROWS // T, 2 * RW])).then_inc(spare_set, 16)
            sp.wait_ge(folded, 1)
            sp.dma_start(w_qkv[C:C1, 1, :], b_fold[:, :]).then_inc(bias_placed, 16)

        x_img = x.rearrange("b (g c) (q r) w -> b (c q) g (r w)", g=NG, r=HALF)
        out_b = out[0:TOKENS, :].rearrange("(b t p) n -> b p t n", t=2, p=TT)
        rows_e = moe_rows[0:SLOTS, :].rearrange("(e f p s) n -> f p e (s n)", e=E, p=TT, s=2)

        def load_image(sp, at):
            wait(sp, x_pooled, NG * (at.b - 1))
            sp.dma_start(xin[at.par][:, :, :], x_img[at.b, :, :, :]).then_inc(x_loaded[at.par], 16)

        def load_text(sp, at):
            wait(sp, ln1_done, at.b - 1)
            wait(sp, h_kept, at.b - 1)
            sp.dma_start(h[at.par][IMG1:TT, 1, :], txt[at.b, :, :]).then_inc(txt_loaded[at.par], 16)

        def fill_slots(sp, at):
            wait(sp, filled[at.par], 16 * at.half)
            sp.dma_start(rows_e[at.b, :, :, :],
                         filler[:, at.par, :, :].bitcast(fp32).rearrange("p s n -> p (s n)")
                         .unsqueeze(1).to_broadcast([TT, E, 2 * RW])).then_inc(filled[at.par], 16)

        def store_h2(sp, at):
            sp.wait_ge(h2_made, at.b + 1)
            sp.dma_start(out_b[at.b, :, :, :], h2[at.par][:, :, :]).then_inc(h2_stored[at.par], 16)

        def setup_vector(dve):
            n = 0

            def done(ins):
                nonlocal n
                n += 1
                ins.then_inc(step0, 1)

            nc.vector.memset(sink_key[:, :], 0.0)
            nc.vector.memset(minus_half[:, :], -0.5)
            nc.vector.memset(w_out[:, :, :], 0.0).then_inc(cleared, 1)
            for tile in (w_qkv[C:C1, :, :], pieces[:, 0:2 * QF].bitcast(fp32),
                         k_t[0][:, :, :, TT:TT + 1].bitcast(fp32), k_t[1][:, :, :, TT:TT + 1].bitcast(fp32),
                         shift[:, :, :], seen[:, :], val[0][:, :, :, :], val[1][:, :, :, :], row[0][:, :, :],
                         row[1][:, :, :]):
                nc.vector.memset(tile, 0.0)
            done(nc.vector.memset(ones[:, :], 1.0))
            dve.wait_ge(step0, n)
            for tile in (xn[:, :, :, C:C1], yn[:, :, :, C:C1], shift[:, :, 2 * HEADS:2 * HEADS + 2],
                         val[0][:, :, :, HD:HD + 1], val[1][:, :, :, HD:HD + 1]):
                nc.vector.memset(tile, 1.0)
            dve.wait_ge(loaded, 16 * N_SMALL)
            for dst, src in ((mask_q0[:, :, :], staging["mask_q0"]), (mask_k[:, :, :], staging["mask_k"]),
                             (sel[:, :, :], staging["sel"]), (before[:, :], staging["before"])):
                if len(dst.shape) == 3:
                    src = src.rearrange("p (a b) -> p a b", a=dst.shape[1])
                nc.vector.tensor_copy(dst, src)
            nc.vector.tensor_copy(ident_r[:, :], ident[:, :])
            nc.vector.tensor_scalar(sink_tok[:, :], sink_tok[:, :], 4.0, None, ALU.mult)
            done(nc.vector.tensor_scalar(sink_ones[:, :], sink_key[:, :], 4.0, None, ALU.mult))
            nc.vector.tensor_copy(token[:, :], small[0:TT, 2 * E:2 * E + 2])
            dve.wait_ge(step0, n)
            done(nc.vector.tensor_copy(sink_hi[:, :], sink_ones[:, :]))
            dve.wait_ge(step0, n)
            done(nc.vector.scalar_tensor_tensor(out=sink_ones[:, :], in0=sink_hi[:, :].bitcast(fp32), scalar=split[:, 3:4],
                                                in1=sink_ones[:, :], op0=ALU.mult, op1=ALU.add))
            dve.wait_ge(step0, n)
            sink_col = staging["sink_col"]
            done(nc.vector.tensor_copy(sink_col, sel[:, :, TT:TT + 1].bitcast(fp32).rearrange("p a b -> p (a b)")))
            dve.wait_ge(step0, n)
            sink_at = sel[:, :, TT:TT + 1].rearrange("p a b -> p (a b)")
            done(nc.vector.tensor_tensor(sink_at, sink_ones[:, :], sink_col, ALU.add))
            dve.wait_ge(fold_done, 1)
            nc.vector.tensor_tensor(b_fold[:, 0:288], bank[0][0:1, 0:288], b_row[:, 0:288], ALU.add)
            nc.vector.tensor_tensor(b_fold[:, 288:576], bank[1][0:1, 0:288], b_row[:, 288:576],
                                    ALU.add).then_inc(folded, 1)
            for c in range(2):
                nc.vector.tensor_scalar(w_qkv[0:C, c, :], w_qkv[0:C, c, :], scale_col[:, c:c + 1], None, ALU.mult)
            nc.vector.tensor_scalar(w_out[:, :, :], w_out[:, :, :], rez[:, 0:1], None,
                                    ALU.mult).then_inc(prepared, 1)
            dve.wait_ge(prepared, 1)
            dve.wait_ge(step0, n)

        def setup_tensor(pe):
            pe.wait_ge(loaded, 16 * N_SMALL)
            for half in range(2):
                for c in range(2):
                    last = nc.tensor.matmul(bank[half][0:1, 0:288], bias_col[:, c:c + 1],
                                            w_qkv[0:C, c, 288 * half:288 * (half + 1)],
                                            start=(c == 0), stop=(c == 1))
            last.then_inc(fold_done, 1)
            pe.wait_ge(prepared, 1)
            pe.wait_ge(bias_placed, 16)

        RING = [("score_t" if c == "S" else "turn", int(k)) for c, k in
                (item for item in "T0 T1 S0 T2 S1 S2 T3 S3 S4 T4 S5 S6 T5 S7 S8".split())]
        RING += [("score", k) for k in range(9)]
        TURNS = (0, 3, 1, 4, 2, 5)
        def pool_image(dve, at, g):
            if g == 0:
                wait(dve, x_spread, at.b - 1)
            dve.wait_ge(x_folded, NG * at.b + g + 1)
            ins = nc.vector.tensor_reduce(
                pooled[at.par][:, g, :],
                xin[at.par][:, g, 0:XF // 2].rearrange("p (r j c) -> p j r c", r=HALF // 2, c=PATCH), AX.XY, ALU.add)
            ins.then_inc(x_pooled, 1)

        norm1 = (st1, mv1, var1, minus_mean1, rstd1, shifted1, ln1_step, ln1_done)
        norm2 = (st2, mv2, var2, minus_mean2, rstd2, shifted2, ln2_step, ln2_done)

        def row_stats(dve, at, src, norm):
            stats, mv, var, minus_mean, _, _, step, _ = norm
            wait(dve, step, 5 * at.b)
            for t in range(2):
                ins = nc.vector.bn_stats(stats[:, t, :], src[:, t, :])
            ins.then_inc(step, 1)
            hold(dve, step, 5 * at.b + 1, held)
            for t in range(2):
                ins = nc.vector.bn_aggr(mv[:, t, :], stats[:, t, :])
            ins.then_inc(step, 1)
            dve.wait_ge(step, 5 * at.b + 2)
            nc.vector.tensor_scalar(minus_mean[:, :], mv[:, :, 0:1].rearrange("p a b -> p (a b)"), -1.0, None, ALU.mult)
            nc.vector.tensor_scalar(var[:, :], mv[:, :, 1:2].rearrange("p a b -> p (a b)"), LN_EPS, None,
                                    ALU.add).then_inc(step, 1)

        def norm1_stats(dve, at):
            dve.wait_ge(h_copied, at.b + 1)
            dve.wait_ge(txt_loaded[at.par], 16 * (at.half + 1))
            row_stats(dve, at, h[at.par], norm1)

        def rotate(dve, at, t):
            n = at.b + 1
            dve.wait_ge(qk_made[t], n)
            wait(dve, qk_rotated[t], 2 * at.b)
            src = bank[6 + t][0:TT, 0:2 * D]
            nc.vector.tensor_tensor(rot_c[:, t, :].rearrange("p (a k) -> p a k", k=8), src.rearrange("p (a k) -> p a k", k=8),
                                    cos[:, t, :].unsqueeze(1).to_broadcast([TT, 48, 8]), ALU.mult)
            nc.vector.tensor_tensor(rot_s[:, t, :].rearrange("p (a k) -> p a k", k=16), src.rearrange("p (a k) -> p a k", k=16),
                                    sin[:, t, :].unsqueeze(1).to_broadcast([TT, 24, 16]), ALU.mult).then_inc(qk_read[t], 1)

        def split_qk(dve, at, r):
            dve.wait_ge(qk_rounded, 6 * at.b + r + 1)
            src, hi = bank[bank_of("turn", r)], rounded[r % 2]
            k = TURNS[r]
            if r == 0:
                wait(dve, scored_t[8], at.b - 1)
            if k < 3:
                for side in range(2):
                    lo = slice(64 * side, 64 * side + 64)
                    dst = q_t[at.par][lo, :, :].rearrange("p (a s) n -> p a s n", s=2)[:, 2 * k:2 * k + 2, side, :]
                    ins = nc.vector.scalar_tensor_tensor(
                        out=dst, in0=hi[lo, :].bitcast(fp32).rearrange("p (a n) -> p a n", a=2), scalar=split[lo, 0:1],
                        in1=src[lo, 0:4 * TT].rearrange("p (a n) -> p a n", a=2), op0=ALU.mult, op1=ALU.add)
            else:
                kk = k - 3
                dst = k_t[at.par][:, 2 * kk:2 * kk + 2, :, 0:TT].rearrange("p a t n -> p (a t) n")
                ins = nc.vector.scalar_tensor_tensor(
                    out=dst, in0=hi[:, :].bitcast(fp32).rearrange("p (a n) -> p a n", a=4), scalar=split[:, 1:2],
                    in1=src[:, 0:4 * TT].rearrange("p (a n) -> p a n", a=4), op0=ALU.mult, op1=ALU.add)
            ins.then_inc(qk_split[r], 1)

        def max_scores(dve, at, k):
            n = at.b + 1
            dve.wait_ge(scored[k], n)
            if k == 0:
                wait(dve, shift_made, at.b)
            if k < 3:
                dst, src = top[:, 0, 4 * k:4 * k + 4], bank[bank_of("score", k)][0:TT, 0:4 * TT].rearrange("p (a n) -> p a n", a=4)
            else:
                kk = k - 3
                dst, src = top[:, 1, 2 * kk:2 * kk + 2], bank[bank_of("score", k)][0:TT, 0:2 * T].rearrange("p (a n) -> p a n", a=2)
            nc.vector.tensor_reduce(dst, src, AX.X, ALU.max).then_inc(maxed[k], 1)

        def make_shift(dve, at):
            n = at.b + 1
            dve.wait_ge(maxed[8], n)
            wait(dve, shift_turned, at.b)
            for part in range(2):
                ins = nc.vector.tensor_tensor(shift[:, :, HEADS * part:HEADS * (part + 1)], top[:, :, :],
                                              sink_tok[:, :].unsqueeze(1).to_broadcast([TT, 2, HEADS]), ALU.max)
            ins.then_inc(shift_made, 1)

        def split_shift(dve, at):
            dve.wait_ge(shift_rounded, at.b + 1)
            wait(dve, scored_t[8], at.b)
            nc.vector.scalar_tensor_tensor(out=shift_t[:, :], in0=shift_hi[:, :].bitcast(fp32), scalar=split[:, 2:3],
                                           in1=bank[7][:, 0:T], op0=ALU.mult, op1=ALU.add).then_inc(shift_ready, 1)

        def normalize(dve, at, t):
            n = at.b + 1
            dve.wait_ge(y_turned[t], n)
            src = bank[4 + t][0:TT, 0:3 * 128].rearrange("p (a k) -> p a k", k=32)
            nc.vector.reciprocal(rden[:, t, :], src[:, :, HD:HD + 1].rearrange("p a b -> p (a b)")).then_inc(den_ready, 1)
            dve.wait_ge(den_ready, 2 * at.b + t + 1)
            if t == 0:
                wait(dve, yn_turned, at.b)
            for c in range(2):
                ins = nc.vector.tensor_tensor(yn[:, t, c, 0:C].rearrange("p (a k) -> p a k", k=HD), src[:, 6 * c:6 * c + 6, 0:HD],
                                              rden[:, t, 6 * c:6 * c + 6].unsqueeze(2).to_broadcast([TT, 6, HD]), ALU.mult)
            ins.then_inc(y_normed, 1)

        def residual(dve, at):
            n = at.b + 1
            dve.wait_ge(projected, n)
            dve.wait_ge(h_kept, n)
            wait(dve, ln2_done, at.b - 1)
            wait(dve, h2_stored[at.par], 16 * at.half)
            nc.vector.tensor_tensor(h2[at.par][:, :, :], bank[5][0:TT, 0:2 * D].rearrange("p (t n) -> p t n", t=2),
                                    h_keep[at.par][:, :, :], ALU.add).then_inc(h2_made, 1)

        def norm2_stats(dve, at):
            dve.wait_ge(h2_made, at.b + 1)
            row_stats(dve, at, h2[at.par], norm2)

        def choose(dve, at):
            n = at.b + 1
            hold(dve, gated, n, held)
            for t in range(2):
                ins = nc.vector.max(best[:, t, :], bank[7][0:TT, E * t:E * (t + 1)])
            ins.then_inc(ranked, 1)
            hold(dve, ranked, n, held)
            for t in range(2):
                ins = nc.vector.max_index(best_i[:, t, :], best[:, t, :], bank[7][0:TT, E * t:E * (t + 1)])
            ins.then_inc(indexed, 1)
            nc.vector.tensor_tensor(gap[:, :], best[:, :, 1:2].rearrange("p a b -> p (a b)"),
                                    best[:, :, 0:1].rearrange("p a b -> p (a b)"), ALU.subtract).then_inc(gaps_made, 1)
            dve.wait_ge(indexed, n)
            nc.vector.tensor_copy(best_f[:, :, :], best_i[:, :, 0:2]).then_inc(route_step, 1)
            dve.wait_ge(route_step, 8 * at.b + 1)
            nc.vector.tensor_tensor(hot[:, :, :, :].rearrange("p t k e -> p (t k) e"),
                                    small[0:TT, E:2 * E].unsqueeze(1).to_broadcast([TT, 4, E]),
                                    best_f[:, :, :].rearrange("p t k -> p (t k)").unsqueeze(2).to_broadcast([TT, 4, E]),
                                    ALU.is_equal).then_inc(route_step, 1)
            dve.wait_ge(route_step, 8 * at.b + 2)
            wait(dve, seen_counted, at.b)
            nc.vector.tensor_tensor(hot_sum[:, :, :], hot[:, :, 0, :], hot[:, :, 1, :], ALU.add).then_inc(hots_summed, 1)

        def weigh(dve, at):
            n = at.b + 1
            dve.wait_ge(gate_exp, n)
            nc.vector.tensor_scalar(gden[:, :], gexp[:, :], 1.0, None, ALU.add).then_inc(route_step, 1)
            dve.wait_ge(route_step, 8 * at.b + 3)
            nc.vector.reciprocal(gw[:, :, 0:1].rearrange("p a b -> p (a b)"), gden[:, :]).then_inc(route_step, 1)
            dve.wait_ge(route_step, 8 * at.b + 4)
            nc.vector.tensor_tensor(gw[:, :, 1:2].rearrange("p a b -> p (a b)"), gexp[:, :],
                                    gw[:, :, 0:1].rearrange("p a b -> p (a b)"), ALU.mult).then_inc(weights_made, 1)
            dve.wait_ge(weights_made, n)
            nc.vector.tensor_tensor(wpick[:, :, :, :].rearrange("p t k e -> p (t k) e"), hot[:, :, :, :].rearrange("p t k e -> p (t k) e"),
                                    gw[:, :, :].rearrange("p t k -> p (t k)").unsqueeze(2).to_broadcast([TT, 4, E]),
                                    ALU.mult).then_inc(route_step, 1)
            dve.wait_ge(route_step, 8 * at.b + 5)
            nc.vector.tensor_tensor(row[at.par][:, :, COL_W:COL_W + E], wpick[:, :, 0, :], wpick[:, :, 1, :], ALU.add)
            nc.vector.tensor_copy(row[at.par][:, :, COL_ID:COL_ID + 1].bitcast(u32).rearrange("p a b -> p (a b)"),
                                  token[:, :]).then_inc(row_whole, 1)
            dve.wait_ge(row_whole, n)
            nc.vector.tensor_scalar(token[:, :], token[:, :], float(T), None, ALU.add)

        def assign(dve, at):
            n = at.b + 1
            dve.wait_ge(ranks_made, n)
            ranks = bank[7][0:TT, 0:2 * E].rearrange("p (t e) -> p t e", t=2)
            nc.vector.tensor_scalar(over[:, :, :], ranks, float(CAP), float(FAR), ALU.is_ge, ALU.mult)
            nc.vector.tensor_tensor(place[:, :, :], ranks, small[0:TT, 0:E].unsqueeze(1).to_broadcast([TT, 2, E]),
                                    ALU.add).then_inc(route_step, 1)
            dve.wait_ge(route_step, 8 * at.b + 6)
            nc.vector.tensor_tensor(place[:, :, :], place[:, :, :], over[:, :, :], ALU.add).then_inc(ranks_read, 1)
            dve.wait_ge(ranks_read, n)
            for k in range(2):
                ins = nc.vector.tensor_tensor(pick[:, :, k, :], hot[:, :, k, :], place[:, :, :], ALU.mult)
            ins.then_inc(route_step, 1)
            dve.wait_ge(route_step, 8 * at.b + 7)
            nc.vector.tensor_reduce(slot_f[:, :], pick[:, :, :, :].rearrange("p t k e -> p (t k) e"), AX.X,
                                    ALU.add).then_inc(route_step, 1)
            dve.wait_ge(route_step, 8 * at.b + 8)
            nc.vector.tensor_copy(slot[at.par][:, :], slot_f[:, :]).then_inc(routed, 1)
            nc.vector.tensor_tensor(seen[:, :], seen[:, :], hot_sum[:, 0, :], ALU.add).then_inc(seen_counted, 1)
            dve.wait_ge(seen_counted, 2 * at.b + 1)
            nc.vector.tensor_tensor(seen[:, :], seen[:, :], hot_sum[:, 1, :], ALU.add).then_inc(seen_counted, 1)

        def fold_image(pool, at, g):
            pool.wait_ge(x_loaded[at.par], 16 * (at.half + 1))
            mid = XF // 2
            nc.gpsimd.tensor_tensor(xin[at.par][:, g, 0:mid], xin[at.par][:, g, 0:mid], xin[at.par][:, g, mid:XF],
                                    ALU.add).then_inc(x_folded, 1)

        def spread_patches(pool, at):
            wait(pool, h_summed, at.b)
            for g in range(NG):
                pool.wait_ge(x_pooled, NG * at.b + g + 1)
                ins = nc.gpsimd.tensor_tensor(spread[:, g, :].rearrange("p (i j) -> p i j", j=SIDE),
                                              pooled[at.par][:, g, :].unsqueeze(1).to_broadcast([XP, SIDE, SIDE]),
                                              patch[:, :].unsqueeze(2).to_broadcast([XP, SIDE, SIDE]), ALU.mult)
            ins.then_inc(x_spread, 1)

        def inverse_std(pool, at, norm):
            _, _, var, minus_mean, rstd, shifted, step, done = norm
            pool.wait_ge(step, 5 * at.b + 3)
            wait(pool, done, at.b)
            nc.gpsimd.tensor_tensor(rstd[:, :], var[:, :], minus_half[:, 0:2], ALU.pow).then_inc(step, 1)
            pool.wait_ge(step, 5 * at.b + 4)
            nc.gpsimd.tensor_tensor(shifted[:, :], minus_mean[:, :], rstd[:, :], ALU.mult).then_inc(step, 1)

        def add_rotation(pool, at, t):
            n = at.b + 1
            pool.wait_ge(qk_read[t], n)
            if t == 0:
                wait(pool, qk_turned[5], at.b)
            for half in range(2):
                dst = qk[:, t, :, :, 8 * half:8 * half + 8]
                a = rot_c[:, t, :].rearrange("p (a s k) -> p a s k", s=2, k=8)[:, :, half, :].unsqueeze(2)
                b = rot_s[:, t, :].rearrange("p (a s k) -> p a s k", s=2, k=8)[:, :, 1 - half, :].unsqueeze(2)
                a, b = (v.to_broadcast([TT, 2 * HEADS, 4, 8]) for v in (a, b))
                nc.gpsimd.tensor_tensor(dst, a, b, ALU.add).then_inc(qk_rotated[t], 1)

        def copy_h(act, at):
            n = at.b + 1
            act.wait_ge(h_summed, n)
            wait(act, ln1_done, at.b - 1)
            wait(act, h_kept, at.b - 1)
            nc.scalar.activation(h[at.par][:, 0, :], bank[6][0:TT, 0:D], ACT.Copy)
            nc.scalar.activation(h[at.par][0:IMG1, 1, :], bank[6][0:IMG1, D:2 * D], ACT.Copy).then_inc(h_copied, 1)

        def norm1_apply(act, at):
            act.wait_ge(ln1_step, 5 * (at.b + 1))
            wait(act, xn_turned, at.b)
            for t in range(2):
                ins = nc.scalar.activation(xn[:, t, :, 0:C], h[at.par][:, t, :].rearrange("p (c k) -> p c k", c=2),
                                           ACT.Identity, scale=rstd1[:, t:t + 1], bias=shifted1[:, t:t + 1])
            ins.then_inc(ln1_done, 1)

        def norm2_apply(act, at):
            act.wait_ge(ln2_step, 5 * (at.b + 1))
            wait(act, scattered[at.par], 64 * at.half)
            for t in range(2):
                ins = nc.scalar.activation(row[at.par][:, t, 0:D], h2[at.par][:, t, :], ACT.Identity,
                                           scale=rstd2[:, t:t + 1], bias=shifted2[:, t:t + 1])
            ins.then_inc(ln2_done, 1)

        def keep_h(act, at):
            act.wait_ge(h_copied, at.b + 1)
            act.wait_ge(txt_loaded[at.par], 16 * (at.half + 1))
            wait(act, h2_made, at.b - 1)
            nc.scalar.activation(h_keep[at.par][:, :, :], h[at.par][:, :, :], ACT.Copy).then_inc(h_kept, 1)

        def copy_xn(act, at):
            act.wait_ge(xn_turned, at.b + 1)
            wait(act, v_made, at.b)
            nc.scalar.activation(xn_t[:, :, :], bank[6][0:C1, 0:2 * T].rearrange("p (c n) -> p c n", c=2),
                                 ACT.Copy).then_inc(xn_ready, 1)

        def copy_v(act, at):
            act.wait_ge(v_made, at.b + 1)
            wait(act, attended[2], at.b - 1)
            nc.scalar.activation(val[at.par][0:TT, :, :, 0:HD].rearrange("p t a k -> p (t a) k"),
                                 bank[6][0:TT, 0:2 * D].rearrange("p (a k) -> p a k", k=HD), ACT.Copy).then_inc(v_ready, 1)

        def round_qk(act, at, r):
            n = at.b + 1
            act.wait_ge(qk_turned[r], n)
            if r >= 2:
                act.wait_ge(qk_split[r - 2], n)
            else:
                wait(act, qk_split[r + 4], at.b)
            nc.scalar.activation(rounded[r % 2][:, :], bank[bank_of("turn", r)][:, 0:4 * TT], ACT.Copy).then_inc(qk_rounded, 1)

        def round_shift(act, at):
            act.wait_ge(shift_turned, at.b + 1)
            wait(act, shift_ready, at.b)
            nc.scalar.activation(shift_hi[:, :], bank[7][:, 0:T], ACT.Copy).then_inc(shift_rounded, 1)

        def exp_scores(act, at, k):
            g, m = divmod(k, 3)
            act.wait_ge(scored_t[k], at.b + 1)
            if m == 0:
                wait(act, attended[g], at.b)
            src = bank[bank_of("score_t", k)]
            if m < 2:
                p = 2 * g + m
                nc.scalar.activation(prob0[:, 2 * p:2 * p + 2, :], src[0:TT + 1, 0:2 * T].rearrange("p (a n) -> p a n", a=2),
                                     ACT.Exp, scale=0.25).then_inc(probed[k], 1)
            else:
                nc.scalar.activation(prob1[:, 4 * g:4 * g + 4, :], src[0:TT, 0:4 * TT].rearrange("p (a n) -> p a n", a=4),
                                     ACT.Exp, scale=0.25).then_inc(probed[k], 1)

        def copy_y(act, at):
            act.wait_ge(attended[2], at.b + 1)
            wait(act, y_turned[1], at.b)
            nc.scalar.activation(y_t[:, 0:2, :], bank[4][:, 0:2 * T].rearrange("p (a n) -> p a n", a=2), ACT.Copy)
            nc.scalar.activation(y_t[:, 2, :], bank[5][:, 0:T], ACT.Copy).then_inc(y_copied, 1)

        def copy_yn(act, at):
            act.wait_ge(yn_turned, at.b + 1)
            wait(act, projected, at.b)
            nc.scalar.activation(yn_t[:, :, :], bank[4][0:C1, 0:2 * T].rearrange("p (c n) -> p c n", c=2),
                                 ACT.Copy).then_inc(yn_ready, 1)

        def copy_xf(act, at):
            act.wait_ge(xf_turned, at.b + 1)
            wait(act, gated, at.b)
            nc.scalar.activation(xf_t[:, :, :], bank[7][0:C, 0:2 * T].rearrange("p (c n) -> p c n", c=2),
                                 ACT.Copy).then_inc(xf_ready, 1)

        def exp_gap(act, at):
            act.wait_ge(gaps_made, at.b + 1)
            wait(act, weights_made, at.b)
            nc.scalar.activation(gexp[:, :], gap[:, :], ACT.Exp).then_inc(gate_exp, 1)

        def sum_channels(pe, at):
            n = at.b + 1
            pe.wait_ge(x_spread, n)
            wait(pe, v_ready, at.b)
            for t, (lo, hi) in enumerate(((0, TT), (TT, SIDE * SIDE))):
                for g in range(NG):
                    ins = nc.tensor.matmul(bank[6][0:hi - lo, D * t:D * (t + 1)], spread[:, g, lo:hi], chan[:, g, :],
                                           start=(g == 0), stop=(g == NG - 1))
            ins.then_inc(h_summed, 1)

        def turn_xn(pe, at):
            n = at.b + 1
            pe.wait_ge(ln1_done, n)
            for c in range(2):
                for t in range(2):
                    ins = nc.tensor.transpose(bank[6][0:C1, T * c + TT * t:T * c + TT * (t + 1)], xn[:, t, c, :], ident[0:TT, 0:TT])
            ins.then_inc(xn_turned, 1)

        def make_qk(pe, at, t):
            n = at.b + 1
            pe.wait_ge(xn_ready, n)
            if t == 1:
                wait(pe, ranks_read, at.b - 2)
            for c in range(2):
                ins = nc.tensor.matmul(bank[6 + t][0:TT, 0:2 * D], xn_t[:, c, TT * t:TT * (t + 1)], w_qkv[:, c, 0:2 * D],
                                       start=(c == 0), stop=(c == 1))
            ins.then_inc(qk_made[t], 1)

        def make_v(pe, at):
            n = at.b + 1
            pe.wait_ge(qk_read[0], n)
            for t in range(2):
                for c in range(2):
                    ins = nc.tensor.matmul(bank[6][0:TT, D * t:D * (t + 1)], xn_t[:, c, TT * t:TT * (t + 1)],
                                           w_qkv[:, c, 2 * D:3 * D], start=(c == 0), stop=(c == 1))
            ins.then_inc(v_made, 1)

        def bank_of(kind, k):
            return RING.index((kind, k)) % 4

        def bank_free(pe, kind, k, m, t):
            at = RING.index((kind, k)) - 4
            while at >= 0:
                kind, k = RING[at]
                if kind == "turn" and m:
                    return pe.wait_ge(qk_split[k], m.b + 1)
                if kind == "score" and m:
                    return pe.wait_ge(maxed[k], m.b + 1)
                if kind == "score_t" and t:
                    return pe.wait_ge(probed[k], t.b + 1)
                at -= 4
            if t:
                pe.wait_ge(maxed[RING[at][1]], t.b + 1)

        def turn_qk(pe, at, before_it, r):
            n = at.b + 1
            if r == 0:
                pe.wait_ge(qk_rotated[1], 2 * n)
                pe.wait_ge(qk_rotated[0], 2 * n)
            bank_free(pe, "turn", r, at, before_it)
            k = TURNS[r]
            dst = bank[bank_of("turn", r)]
            for a in range(2):
                for t in range(2):
                    src = qk[:, t, 4 * k + 2 * a:4 * k + 2 * a + 2, :, :].rearrange("p a s k -> p (a s k)")
                    ins = nc.tensor.transpose(dst[:, TT * (2 * a + t):TT * (2 * a + t + 1)], src, ident[0:TT, 0:TT])
            ins.then_inc(qk_turned[r], 1)

        def score(pe, at, before_it, k):
            n = at.b + 1
            if k < 3:
                pe.wait_ge(qk_split[2 * k], n)
                pe.wait_ge(qk_split[2 * k + 1], n)
            bank_free(pe, "score", k, at, before_it)
            dst = bank[bank_of("score", k)]
            if k < 3:
                nc.tensor.matmul(dst[0:TT, 0:4 * TT], ident_r[0:TT, 0:TT], mask_q0[:, :, :], start=True, stop=False)
                for a in range(4):
                    hh = 4 * k + a
                    ins = nc.tensor.matmul(dst[0:TT, TT * a:TT * (a + 1)], q_t[at.par][:, hh, 0:TT], k_t[at.par][:, hh // 2, 0, 0:TT],
                                           start=False, stop=(a == 3))
            else:
                kk = k - 3
                for a in range(2):
                    hh = 2 * kk + a
                    nc.tensor.matmul(dst[0:TT, T * a:T * (a + 1)], q_t[at.par][:, hh, TT:T], k_t[at.par][:, kk, :, 0:TT],
                                     start=(a == 0), stop=False, skip_group_check=True)
                ins = nc.tensor.matmul(dst[0:TT, 0:2 * T].rearrange("p (a n) -> p a n", a=2)[:, :, TT:T], ident_r[0:TT, 0:TT],
                                       mask_q0[:, 0:2, :], start=False, stop=True, skip_group_check=True)
            ins.then_inc(scored[k], 1)

        def turn_shift(pe, at):
            n = at.b + 1
            pe.wait_ge(shift_made, n)
            pe.wait_ge(qk_read[1], after(at))
            for t in range(2):
                ins = nc.tensor.transpose(bank[7][:, TT * t:TT * (t + 1)], shift[:, t, :], ident[0:TT, 0:TT])
            ins.then_inc(shift_turned, 1)

        def score_t(pe, at, following, k):
            n = at.b + 1
            g, m = divmod(k, 3)
            if k == 0:
                pe.wait_ge(shift_ready, n)
            bank_free(pe, "score_t", k, following, at)
            dst = bank[bank_of("score_t", k)]
            if m < 2:
                p = 2 * g + m
                nc.tensor.matmul(dst[0:TT + 1, 0:2 * T], k_t[at.par][:, p, 0, :], q_t[at.par][:, 2 * p:2 * p + 2, :],
                                 start=True, stop=False)
                for a in range(2):
                    nc.tensor.matmul(dst[0:TT + 1, T * a:T * (a + 1)], sel[:, 2 * p + a, :], shift_t[:, :], start=False, stop=False)
                ins = nc.tensor.matmul(dst[0:TT, 0:2 * T].rearrange("p (a n) -> p a n", a=2)[:, :, 0:TT], ident_r[0:TT, 0:TT],
                                       mask_k[:, 0:2, :], start=False, stop=True)
            else:
                nc.tensor.matmul(dst[0:TT, 0:4 * TT], ident_r[0:TT, 0:TT], mask_k[:, :, :], start=True, stop=False)
                for p in range(2):
                    nc.tensor.matmul(dst[0:TT, 2 * TT * p:2 * TT * (p + 1)], k_t[at.par][:, 2 * g + p, 1, 0:TT],
                                     q_t[at.par][:, 4 * g + 2 * p:4 * g + 2 * p + 2, TT:T], start=False, stop=False)
                for a in range(4):
                    ins = nc.tensor.matmul(dst[0:TT, TT * a:TT * (a + 1)], sel[:, 4 * g + a, 0:TT], shift_t[:, TT:T],
                                           start=False, stop=(a == 3))
            ins.then_inc(scored_t[k], 1)

        def attend(pe, at, g):
            n = at.b + 1
            if g == 0:
                wait(pe, yn_ready, at.b)
                wait(pe, h2_made, at.b)
                pe.wait_ge(v_ready, n)
            for m in range(3):
                pe.wait_ge(probed[3 * g + m], n)
            dst = bank[4][:, T * g:T * (g + 1)] if g < 2 else bank[5][:, 0:T]
            for a in range(4):
                hh = 4 * g + a
                nc.tensor.matmul(dst[32 * a:32 * a + 32, :], val[at.par][:, 0, hh, :], prob0[:, hh, :], start=True, stop=False,
                                 skip_group_check=True)
                ins = nc.tensor.matmul(dst[32 * a:32 * a + 32, TT:T], val[at.par][0:TT, 1, hh, :], prob1[:, hh, :], start=False,
                                       stop=True, skip_group_check=True)
            ins.then_inc(attended[g], 1)

        def after(at, n=1):
            return min(at.b + 1 + n, B) if isinstance(at.b, int) else at.b + 1 + n

        def turn_y(pe, at, t):
            n = at.b + 1
            if t == 0:
                pe.wait_ge(y_copied, n)
            for g in range(3):
                ins = nc.tensor.transpose(bank[4 + t][0:TT, 128 * g:128 * (g + 1)], y_t[:, g, TT * t:TT * (t + 1)], ident[:, :])
            ins.then_inc(y_turned[t], 1)

        def turn_yn(pe, at):
            n = at.b + 1
            pe.wait_ge(y_normed, 2 * n)
            for c in range(2):
                for t in range(2):
                    ins = nc.tensor.transpose(bank[4][0:C1, T * c + TT * t:T * c + TT * (t + 1)], yn[:, t, c, :], ident[0:TT, 0:TT])
            ins.then_inc(yn_turned, 1)

        def project(pe, at):
            n = at.b + 1
            pe.wait_ge(yn_ready, n)
            for t in range(2):
                for c in range(2):
                    ins = nc.tensor.matmul(bank[5][0:TT, D * t:D * (t + 1)], yn_t[:, c, TT * t:TT * (t + 1)], w_out[:, c, :],
                                           start=(c == 0), stop=(c == 1))
            ins.then_inc(projected, 1)

        def turn_xf(pe, at):
            n = at.b + 1
            pe.wait_ge(ln2_done, n)
            pe.wait_ge(shift_ready, after(at))
            for c in range(2):
                for t in range(2):
                    ins = nc.tensor.transpose(bank[7][0:C, T * c + TT * t:T * c + TT * (t + 1)], row[at.par][:, t, C * c:C * (c + 1)],
                                              ident[0:TT, 0:TT])
            ins.then_inc(xf_turned, 1)

        def gate_logits(pe, at):
            n = at.b + 1
            pe.wait_ge(xf_ready, n)
            for t in range(2):
                for c in range(2):
                    ins = nc.tensor.matmul(bank[7][0:TT, E * t:E * (t + 1)], xf_t[:, c, TT * t:TT * (t + 1)], gate[:, c, :],
                                           start=(c == 0), stop=(c == 1))
            ins.then_inc(gated, 1)

        def rank(pe, at):
            n = at.b + 1
            pe.wait_ge(hots_summed, n)
            wait(pe, seen_counted, 2 * at.b)
            first, second = bank[7][0:TT, 0:E], bank[7][0:TT, E:2 * E]
            nc.tensor.matmul(first, before[:, :], hot_sum[:, 0, :], start=True, stop=False)
            nc.tensor.matmul(first, ones[:, :], seen[:, :], start=False, stop=True)
            nc.tensor.matmul(second, before[:, :], hot_sum[:, 1, :], start=True, stop=False)
            nc.tensor.matmul(second, ones[:, :], hot_sum[:, 0, :], start=False, stop=False)
            nc.tensor.matmul(second, ones[:, :], seen[:, :], start=False, stop=True).then_inc(ranks_made, 1)

        def step_tensor(pe, p, a, m, t, z):
            def half1(items):
                for c, k in items.split():
                    if c == "T" and m:
                        turn_qk(pe, m, t, int(k))
                    elif c == "S" and t:
                        score_t(pe, t, m, int(k))

            half1("T0")
            if t:
                turn_shift(pe, t)
            half1("T1")
            if a:
                sum_channels(pe, a)
            half1("S0 T2 S1 S2 T3")
            if z:
                turn_xf(pe, z)
            half1("S3")
            if a:
                turn_xn(pe, a)
            half1("S4")
            if z:
                gate_logits(pe, z)
            if t:
                attend(pe, t, 0)
            half1("T4 S5")
            if a:
                make_qk(pe, a, 0)
            half1("S6")
            if z:
                rank(pe, z)
            if t:
                attend(pe, t, 1)
            half1("T5 S7 S8")
            if m:
                score(pe, m, t, 0)
            if a:
                make_qk(pe, a, 1)
            if t:
                attend(pe, t, 2)
            if m:
                score(pe, m, t, 1)
                score(pe, m, t, 2)
            if t:
                turn_y(pe, t, 0)
                turn_y(pe, t, 1)
            if m:
                score(pe, m, t, 3)
            if m:
                for k in range(4, 6):
                    score(pe, m, t, k)
            if t:
                turn_yn(pe, t)
            if m:
                score(pe, m, t, 6)
                score(pe, m, t, 7)
                score(pe, m, t, 8)
            if t:
                project(pe, t)
            if a:
                make_v(pe, a)

        def step_scalar(act, p, a, m, t, z):
            def half1(items):
                for c, k in items.split():
                    if c == "T" and m:
                        round_qk(act, m, int(k))
                    elif c == "S" and t:
                        exp_scores(act, t, int(k))

            half1("T0")
            if t:
                round_shift(act, t)
            half1("T1")
            if a:
                copy_h(act, a)
            half1("S0 T2 S1")
            if z:
                norm2_apply(act, z)
            half1("S2 T3")
            if a:
                norm1_apply(act, a)
            if z:
                copy_xf(act, z)
            half1("S3")
            if a:
                copy_xn(act, a)
            half1("S4")
            if z:
                exp_gap(act, z)
            half1("T4 S5 S6")
            if m:
                keep_h(act, m)
            half1("T5 S7 S8")
            if t:
                copy_y(act, t)
            if t:
                copy_yn(act, t)
            if a:
                copy_v(act, a)

        def step_vector(dve, p, a, m, t, z):
            if m:
                split_qk(dve, m, 0)
            if t:
                split_shift(dve, t)
            if z:
                norm2_stats(dve, z)
            if m:
                split_qk(dve, m, 1)
            if a:
                norm1_stats(dve, a)
            if m:
                split_qk(dve, m, 2)
            if m:
                split_qk(dve, m, 3)
            if p:
                pool_image(dve, p, 0)
            if z:
                choose(dve, z)
            if m:
                split_qk(dve, m, 4)
            if z:
                weigh(dve, z)
            if a:
                rotate(dve, a, 0)
            if z:
                assign(dve, z)
            if m:
                split_qk(dve, m, 5)
            if p:
                pool_image(dve, p, 1)
            if m:
                max_scores(dve, m, 0)
            if a:
                rotate(dve, a, 1)
            if m:
                max_scores(dve, m, 1)
            if t:
                normalize(dve, t, 0)
                normalize(dve, t, 1)
            if m:
                for k in range(2, 6):
                    max_scores(dve, m, k)
            if p:
                pool_image(dve, p, 2)
            if m:
                for k in range(6, 9):
                    max_scores(dve, m, k)
                make_shift(dve, m)
            if t:
                residual(dve, t)

        PEEL = 6

        def batches(half, par, known=None):
            return [Batch(half, par, lag) if known is None or 0 <= known - lag < B else None for lag in range(5)]

        def steps(eng, step):
            def one(half, par, known):
                step(eng, *batches(half, par, 2 * half + par if known else None))

            for i in range(PEEL):
                one(i // 2, i % 2, True)
            with eng.Fori(PEEL // 2, B // 2) as half:
                one(half, 0, False)
                one(half, 1, False)
            for i in range(B, B + 4):
                one(i // 2, i % 2, True)

        def pass1_sync(sp):
            def one(half, par, fill, known=None):
                p, _, _, _, z = batches(half, par, known)
                if known is None or known + 1 < B:
                    load_image(sp, Batch(half, par, -1))
                if p:
                    load_text(sp, p)
                if fill:
                    fill_slots(sp, p)
                if z:
                    store_h2(sp, z)

            load_image(sp, Batch(0, 0))
            for i in range(PEEL):
                one(i // 2, i % 2, i < FILLS, i)
            with sp.Fori(PEEL // 2, FILLS // 2) as half:
                one(half, 0, True)
                one(half, 1, True)
            with sp.Fori(FILLS // 2, B // 2 - 1) as half:
                one(half, 0, False)
                one(half, 1, False)
            for i in range(B - 2, B + 4):
                one(i // 2, i % 2, False, i)

        def pass1_gpsimd(pool):
            def one(half, par, known=None, fill=None):
                p, a, _, _, z = batches(half, par, known)
                if z:
                    inverse_std(pool, z, norm2)
                if a:
                    inverse_std(pool, a, norm1)
                if p:
                    for g in range(NG):
                        fold_image(pool, p, g)
                if a:
                    add_rotation(pool, a, 0)
                if z:
                    scatter_waits(pool, z, fill)
                if a:
                    add_rotation(pool, a, 1)
                if p:
                    spread_patches(pool, p)

            for i in range(PEEL):
                one(i // 2, i % 2, i)
            with pool.Fori(PEEL // 2, FILLS // 2) as half:
                one(half, 0, fill=True)
                one(half, 1, fill=True)
            with pool.Fori(FILLS // 2, B // 2) as half:
                one(half, 0, fill=False)
                one(half, 1, fill=False)
            for i in range(B, B + 4):
                one(i // 2, i % 2, i)

        def scatter_waits(pool, z, fill):
            if fill or (fill is None and z.b < FILLS):
                pool.wait_ge(filled[z.par], 16 * (z.half + 1))
            else:
                pool.wait_ge(filled[z.par], 16 * (FILLS // 2))
            scatter_rows(pool, z)

        def scatter_rows(pool, at):
            pool.wait_ge(row_whole, at.b + 1)
            hold(pool, routed, at.b + 1, held)
            for t in range(2):
                for k in range(TOPK):
                    nc.gpsimd.indirect_dma_start(
                        out=moe_rows[0:SLOTS, :],
                        out_offset=bass.IndirectOffsetOnAxis(ap=slot[at.par][:, 2 * t + k:2 * t + k + 1], axis=0),
                        in_=row[at.par][:, t, :], in_offset=None, bounds_check=SLOTS - 1, oob_is_err=False,
                    ).then_inc(scattered[at.par], 16)

        rows_n = moe_rows.rearrange("(n p s) w -> n p s w", p=TT, s=SUB)

        def load_expert(sp, e, par):
            for dst, src in ((w_raw[:, 0, :], w13_t[e, 0:128, :]), (w_raw[0:64, 1, :], w13_t[e, 128:D, :]),
                             (w_raw[64:128, 1, :], w13_t[e, 128:D, :]),
                             (nw[:, 0:1], norm_w_t[e, 0:128, :]), (nw[0:64, 1:2], norm_w_t[e, 128:D, :]),
                             (nw[64:128, 1:2], norm_w_t[e, 128:D, :]),
                             (w_dn[par][:, :, :], w2_t[e, :, :].rearrange("(j p) n -> p j n", p=128))):
                sp.dma_start(dst, src).then_inc(w_loaded, 16)

        def load_rows(sp, n, par):
            sp.dma_start(xr[par][:, :, :], rows_n[n, :, :, :]).then_inc(rows_loaded[par], 16)

        def round_expert(act, e, par):
            act.wait_ge(w_loaded, 112 * (e + 1))
            wait(act, down, TILES * (e - 1))
            if isinstance(e, int) and e == 0:
                act.wait_ge(scored_t[8], B)
            for c in range(2):
                ins = nc.scalar.activation(w_hi[par][:, c, :], w_raw[:, c, :], ACT.Copy, scale=nw[:, c:c + 1])
            ins.then_inc(w_rounded, 1)

        def split_expert(dve, e, par):
            dve.wait_ge(w_rounded, e + 1)
            for c in range(2):
                ins = nc.vector.scalar_tensor_tensor(out=w_lo[par][:, c, :], in0=w_raw[:, c, :], scalar=nw[:, c:c + 1],
                                                     in1=w_hi[par][:, c, :].bitcast(fp32), op0=ALU.mult, op1=ALU.subtract)
            ins.then_inc(w_split, 1)

        def square_rows(act, n, par, pair):
            act.wait_ge(rows_loaded[par], 16 * (pair + 1))
            wait(act, rms_sum, n)
            for s in range(SUB):
                ins = nc.scalar.activation(sq[:, s, :], xr[par][:, s, 0:D], ACT.Square, accum_out=ssum[:, s:s + 1])
            ins.then_inc(squared, 1)

        def make_z(dve, n, par):
            dve.wait_ge(rms_made, n + 1)
            wait(dve, zb_turned, n)
            for s in range(SUB):
                ins = nc.vector.tensor_scalar(z[:, s, 0:D], xr[par][:, s, 0:D], rms2[:, s:s + 1], None, ALU.mult)
            ins.then_inc(z_scaled, 1)
            dve.wait_ge(z_scaled, n + 1)
            nc.vector.tensor_copy(z[:, :, D:256], z[:, :, 128:D]).then_inc(z_made, 1)

        def mean_square(dve, n):
            dve.wait_ge(squared, n + 1)
            nc.vector.tensor_scalar(rms[:, :], ssum[:, :], 1.0 / D, RMS_EPS / 4.0, ALU.mult, ALU.add).then_inc(rms_sum, 1)

        def take_numbers(dve, n, par, pair, e):
            wait(dve, added[par], 16 * SUB * pair)
            dve.wait_ge(rows_loaded[par], 16 * (pair + 1))
            hold(dve, y_weighted, n - 1, held)
            nc.vector.tensor_copy(w_slot[par][:, :].unsqueeze(2), xr[par][:, :, bass.ds(COL_W + e, 1)])
            nc.vector.tensor_copy(who[par][:, :].unsqueeze(2),
                                  xr[par][:, :, COL_ID:COL_ID + 1].bitcast(u32)).then_inc(numbered, 1)

        def weigh_x(act, n, par):
            act.wait_ge(numbered, n + 1)
            wait(act, y_weighted, n)
            for s in range(SUB):
                ins = nc.scalar.activation(xw[:, s, :], xr[par][:, s, 0:D], ACT.Copy, scale=w_slot[par][:, s:s + 1])
            ins.then_inc(x_weighted, 1)

        def turn_z(pe, n):
            pe.wait_ge(z_made, n + 1)
            wait(pe, za_split, n)
            wait(pe, zb_split, n)
            for s in range(SUB):
                ins = nc.tensor.transpose(bank[4][:, TT * s:TT * (s + 1)], z[:, s, 0:128], ident[0:TT, 0:TT])
            ins.then_inc(za_turned, 1)
            for s in range(SUB):
                ins = nc.tensor.transpose(bank[5][:, TT * s:TT * (s + 1)], z[:, s, 128:256], ident[0:TT, 0:TT])
            ins.then_inc(zb_turned, 1)

        def round_z(act, n):
            act.wait_ge(za_turned, n + 1)
            nc.scalar.activation(za_hi[:, :], bank[4][:, 0:ROWS], ACT.Copy).then_inc(za_rounded, 1)
            act.wait_ge(zb_turned, n + 1)
            nc.scalar.activation(zb_hi[:, :], bank[5][:, 0:ROWS], ACT.Copy).then_inc(zb_rounded, 1)

        def split_z(dve, n):
            dve.wait_ge(za_rounded, n + 1)
            nc.vector.tensor_tensor(za_lo[:, :], bank[4][:, 0:ROWS], za_hi[:, :].bitcast(fp32), ALU.subtract).then_inc(za_split, 1)
            dve.wait_ge(zb_rounded, n + 1)
            nc.vector.tensor_copy(zb[0:64, :], zb_hi[0:64, :].bitcast(fp32))
            nc.vector.tensor_tensor(zb[64:128, :], bank[5][64:128, 0:ROWS], zb_hi[64:128, :].bitcast(fp32),
                                    ALU.subtract).then_inc(zb_split, 1)

        def expert_up(pe, n, e_par, j):
            if j == 0:
                pe.wait_ge(za_split, n + 1)
                pe.wait_ge(zb_split, n + 1)
            if j >= 2:
                pe.wait_ge(hid_made[j - 2], n + 1)
            else:
                wait(pe, hid_made[j + 2], n)
            hi, lo = w_hi[e_par], w_lo[e_par]
            for side in range(2):
                dst = bank[2 * (j % 2) + side][:, 0:ROWS]
                col = slice(HID * side + 128 * j, HID * side + 128 * (j + 1))
                nc.tensor.matmul(dst, hi[:, 0, col], za_hi[:, :], start=True, stop=False)
                nc.tensor.matmul(dst, hi[:, 0, col], za_lo[:, :], start=False, stop=False)
                nc.tensor.matmul(dst, lo[:, 0, col], za_hi[:, :], start=False, stop=False)
                nc.tensor.matmul(dst, hi[:, 1, col], zb[:, :], start=False, stop=False)
                ins = nc.tensor.matmul(dst, lo[:, 1, col], zb[:, :], start=False, stop=True)
            ins.then_inc(gate_up[j], 1)

        def silu(act, n, j):
            act.wait_ge(gate_up[j], n + 1)
            if j >= 2:
                act.wait_ge(hid_made[j - 2], n + 1)
            else:
                wait(act, hid_made[j + 2], n)
            nc.scalar.activation(act_g[:, j % 2, :], bank[2 * (j % 2)][:, 0:ROWS], ACT.Silu).then_inc(silued, 1)

        def make_hid(dve, n, j):
            dve.wait_ge(silued, 4 * n + j + 1)
            if j == 0:
                wait(dve, down, n)
            nc.vector.tensor_tensor(hid[:, j, :], bank[2 * (j % 2) + 1][:, 0:ROWS], act_g[:, j % 2, :], ALU.mult).then_inc(hid_made[j], 1)

        def expert_down(pe, n, e_par):
            wait(pe, y_weighted, n)
            for j in range(4):
                pe.wait_ge(hid_made[j], n + 1)
                for s in range(SUB):
                    ins = nc.tensor.matmul(bank[6 + s // 2][0:TT, D * (s % 2):D * (s % 2 + 1)], hid[:, j, TT * s:TT * (s + 1)],
                                           w_dn[e_par][:, j, :], start=(j == 0 and s % 2 == 0), stop=(j == 3),
                                           skip_group_check=True)
            ins.then_inc(down, 1)

        def weigh_rows(dve, n, par):
            dve.wait_ge(down, n + 1)
            dve.wait_ge(x_weighted, n + 1)
            for s in range(SUB):
                ins = nc.vector.scalar_tensor_tensor(
                    out=ys[par][:, s, :], in0=bank[6 + s // 2][0:TT, D * (s % 2):D * (s % 2 + 1)], scalar=w_slot[par][:, s:s + 1],
                    in1=xw[:, s, :], op0=ALU.mult, op1=ALU.add)
            ins.then_inc(y_weighted, 1)

        def inverse_rms(pool, n):
            pool.wait_ge(rms_sum, n + 1)
            nc.gpsimd.tensor_tensor(rms2[:, :], rms[:, :], minus_half[:, 0:SUB], ALU.pow).then_inc(rms_made, 1)

        def add_rows(pool, n, par, pair):
            pool.wait_ge(y_weighted, n + 1)
            pool.wait_ge(numbered, n + 1)
            if par:
                hold(pool, added[0], 16 * SUB * (pair + 1), held)
            else:
                hold(pool, added[1], 16 * SUB * pair, held)
            for s in range(SUB):
                nc.gpsimd.indirect_dma_start(
                    out=out[:, :], out_offset=bass.IndirectOffsetOnAxis(ap=who[par][:, s:s + 1], axis=0),
                    in_=ys[par][:, s, :], in_offset=None, bounds_check=TOKENS + ROWS - 1, oob_is_err=True,
                    compute_op=ALU.add).then_inc(added[par], 16)

        PT = TILES // 2

        def over_tiles(eng, tile, between=None):
            def expert(e, e_par):
                def pair_of(k):
                    pair = e * PT + k
                    for par in range(2):
                        next_e = e + 1 if par and isinstance(k, int) and k == PT - 1 else e
                        tile(2 * pair + par, e, e_par, par, pair, next_e)

                pair_of(0)
                if between:
                    between(e + 1, 1 - e_par)
                with eng.Fori(1, PT - 1) as k:
                    pair_of(k)
                pair_of(PT - 1)

            expert(0, 0)
            expert(1, 1)
            with eng.Fori(1, E // 2) as e2:
                expert(2 * e2, 0)
                expert(2 * e2 + 1, 1)

        block = ctx.enter_context(nc.Block())

        @block.sync
        def _(sp):
            setup_sync(sp)
            pass1_sync(sp)
            sp.wait_ge(x_pooled, NG * B)
            sp.wait_ge(attended[2], B)
            load_expert(sp, 0, 0)
            for par in range(2):
                sp.wait_ge(scattered[par], 64 * (B // 2))
            for par in range(2):
                load_rows(sp, par, par)

            def tile(n, e, e_par, par, pair, next_e):
                sp.wait_ge(z_made, n + 1)
                sp.wait_ge(x_weighted, n + 1)
                sp.wait_ge(numbered, n + 1)
                load_rows(sp, n + 2, par)

            def between(e, par):
                hold(sp, w_split, e, held)
                hold(sp, down, TILES * (e - 1), held)
                load_expert(sp, e, par)

            over_tiles(sp, tile, between)

        @block.gpsimd
        def _(pool):
            pool.wait_ge(prepared, 1)
            pass1_gpsimd(pool)
            for par in range(2):
                pool.wait_ge(h2_stored[par], 16 * (B // 2))
            pool.wait_ge(spare_set, 32)
            inverse_rms(pool, 0)
            inverse_rms(pool, 1)

            def tile(n, e, e_par, par, pair, next_e):
                inverse_rms(pool, n + 2)
                add_rows(pool, n, par, pair)

            over_tiles(pool, tile)
            for par in range(2):
                pool.wait_ge(added[par], 16 * SUB * E * PT)

        @block.vector
        def _(dve):
            setup_vector(dve)
            steps(dve, step_vector)
            mean_square(dve, 0)
            make_z(dve, 0, 0)
            split_expert(dve, 0, 0)
            split_z(dve, 0)
            take_numbers(dve, 0, 0, 0, 0)
            mean_square(dve, 1)

            def tile(n, e, e_par, par, pair, next_e):
                n1, par1, pair1 = n + 1, 1 - par, pair + par
                make_hid(dve, n, 0)
                make_z(dve, n1, par1)
                for j in range(1, 4):
                    make_hid(dve, n, j)
                split_z(dve, n1)
                take_numbers(dve, n1, par1, pair1, next_e)
                mean_square(dve, n + 2)
                weigh_rows(dve, n, par)

            over_tiles(dve, tile, lambda e, par: split_expert(dve, e, par))

        @block.scalar
        def _(act):
            act.wait_ge(prepared, 1)
            steps(act, step_scalar)
            round_expert(act, 0, 0)
            square_rows(act, 0, 0, 0)
            round_z(act, 0)
            square_rows(act, 1, 1, 0)

            def tile(n, e, e_par, par, pair, next_e):
                silu(act, n, 0)
                weigh_x(act, n, par)
                for j in range(1, 4):
                    silu(act, n, j)
                round_z(act, n + 1)
                square_rows(act, n + 2, par, pair + 1)

            over_tiles(act, tile, lambda e, par: round_expert(act, e, par))

        @block.tensor
        def _(pe):
            setup_tensor(pe)
            steps(pe, step_tensor)
            pe.wait_ge(w_split, 1)
            turn_z(pe, 0)

            def tile(n, e, e_par, par, pair, next_e):
                if par == 0:
                    pe.wait_ge(w_split, e + 1)
                for j in range(4):
                    expert_up(pe, n, e_par, j)
                turn_z(pe, n + 1)
                expert_down(pe, n, e_par)

            over_tiles(pe, tile)


def kernel(**inputs):
    import concourse.bacc as bacc
    from concourse.bass_utils import run_bass_kernel_spmd

    def host(name):
        return np.asarray(inputs[name])

    batches = host("x").shape[0]
    tokens = batches * T
    head = np.concatenate([np.arange(0, HD, 2), np.arange(1, HD, 2)])
    cols = np.concatenate([np.arange(2 * HEADS)[:, None] * HD + head, 2 * D + np.arange(D).reshape(HEADS, HD)]).reshape(-1)
    wrap = list(range(E)) + [0]
    arrays = {
        "x": host("x"), "txt": host("txt"), "chan_w": host("L0_tok_channel_weights"),
        "norm_scale": host("L0_attn_norm_scale"), "norm_bias": host("L0_attn_norm_bias"),
        "w_attn": host("L0_attn_W_attn")[:, cols], "b_attn": host("L0_attn_b_attn")[cols],
        "w_proj": host("L0_attn_W_proj"), "b_proj": host("L0_attn_b_proj"),
        "sinks": host("L0_attn_sinks"), "rezero": host("L0_attn_rezero"),
        "gate_t": host("L0_ffn_gate_w").T,
        "w13_t": host("L0_ffn_w13").transpose(0, 2, 1)[wrap],
        "w2_t": host("L0_ffn_w2").transpose(0, 2, 1)[wrap],
        "norm_w_t": host("L0_ffn_norm_w")[wrap][:, :, None],
    }
    fixed = constants(tokens)
    nc = bacc.Bacc("TRN2", target_bir_lowering=False, num_devices=1)
    feeds, aps = {}, {}
    for name, a in list(arrays.items()) + [("const_" + k, v) for k, v in fixed.items()]:
        a = np.ascontiguousarray(a)
        feeds[f"in_{name}"] = a
        aps[name] = nc.dram_tensor(f"in_{name}", a.shape, mybir.dt.from_np(a.dtype), kind="ExternalInput").ap()
    out = nc.dram_tensor("out", [tokens + ROWS, D], mybir.dt.float32, kind="ExternalOutput").ap()
    build(nc, *[aps[name] for name in arrays], {k: aps["const_" + k] for k in fixed}, out)
    r = run_bass_kernel_spmd(nc, [feeds], core_ids=[0])
    return r.results[0]["out"][:tokens].reshape(batches, T, D)
```
